# Optimizing a Trainium2 kernel written in Bass

```python
import numpy as np
import jax
import jax.numpy as jnp

def _softmax(x, axis=-1):
    return jax.nn.softmax(x, axis=axis)

def _gelu(x):
    return jax.nn.gelu(x, approximate=True)

def _silu(x):
    return jax.nn.silu(x)

def _sigmoid(x):
    return jax.nn.sigmoid(x)

def _layernorm(x, axis=-1, eps=1e-05):
    m = jnp.mean(x, axis=axis, keepdims=True)
    v = jnp.var(x, axis=axis, keepdims=True)
    return (x - m) / jnp.sqrt(v + eps)

def _scatter_add(tgt, idx, src, axis=0):
    return tgt.at[idx].add(src)

def _segment_sum(src, seg, n):
    return jax.ops.segment_sum(src, seg, n)
kernel_name = 'mk_gnn_resnorm_d4_gnn_r8_45e1c8'

def setup_inputs(seed: int=0):
    np.random.seed(seed)
    _w = jnp.asarray

    def _rec_inputs():
        import jax
        import jax.numpy as jnp
        _gk = jax.random.key(seed)
        x = -0.000202 + 1 * jax.random.normal(jax.random.fold_in(_gk, 1), (6250, 128), jnp.float32)
        _s = jax.random.randint(jax.random.fold_in(_gk, 2), (50000,), 0, 6250, jnp.int32)
        _d = jax.random.randint(jax.random.fold_in(_gk, 3), (50000,), 0, 6250, jnp.int32)
        _loop = jnp.arange(6250, dtype=jnp.int32)
        src = jnp.concatenate([_s, _d, _loop])
        dst = jnp.concatenate([_d, _s, _loop])
        _o = jnp.argsort(dst, stable=True)
        src = src[_o]
        dst = dst[_o]
        return (x, src, dst)
    x, src, dst = _rec_inputs()

    def _L0_gnn_setup():
        import jax, jax.numpy as jnp
        import numpy as np
        N = 6250
        E = 100000
        IN_C = 128
        OUT_C = 32
        HEADS = 4
        NEG_SLOPE = 0.2
        key = jax.random.key(seed)
        k1, k2, k3, k4, k5, k6 = jax.random.split(key, 6)
        x = jax.random.normal(k1, (N, IN_C), dtype=jnp.float32)
        edge_index = jax.random.randint(k2, (2, E), 0, N, dtype=jnp.int64)
        W = jax.random.normal(k3, (IN_C, HEADS * OUT_C), dtype=jnp.float32) * (1.0 / np.sqrt(IN_C))
        att_src = jax.random.normal(k4, (HEADS, OUT_C), dtype=jnp.float32) * (1.0 / np.sqrt(OUT_C))
        att_dst = jax.random.normal(k5, (HEADS, OUT_C), dtype=jnp.float32) * (1.0 / np.sqrt(OUT_C))
        bias = jnp.zeros((HEADS * OUT_C,), dtype=jnp.float32)
        return {'x': x, 'edge_index': edge_index, 'W': W, 'att_src': att_src, 'att_dst': att_dst, 'bias': bias}
    _L0_gnn_all = _L0_gnn_setup()
    _L0_gnn_in = {k: v for k, v in _L0_gnn_all.items() if k in ('W', 'att_src', 'att_dst', 'bias')}
    del _L0_gnn_all

    def _L1_gnn_setup():
        import jax, jax.numpy as jnp
        import numpy as np
        N_NODES = 6250
        N_EDGES = 100000
        IN_FEAT = 128
        OUT_FEAT = 128
        key = jax.random.key(seed)
        ks = jax.random.split(key, 9)
        s = 1.0 / np.sqrt(IN_FEAT)
        return {'x': jax.random.normal(ks[0], (N_NODES, IN_FEAT), dtype=jnp.float32), 'src': jax.random.randint(ks[1], (N_EDGES,), 0, N_NODES), 'dst': jax.random.randint(ks[2], (N_EDGES,), 0, N_NODES), 'W1': jax.random.uniform(ks[3], (IN_FEAT, OUT_FEAT), jnp.float32, -s, s), 'b1': jax.random.uniform(ks[4], (OUT_FEAT,), jnp.float32, -s, s), 'W2': jax.random.uniform(ks[5], (OUT_FEAT, 1), jnp.float32, -s, s), 'b2': jax.random.uniform(ks[6], (1,), jnp.float32, -s, s), 'W4': jax.random.uniform(ks[7], (IN_FEAT, OUT_FEAT), jnp.float32, -s, s), 'b4': jax.random.uniform(ks[8], (OUT_FEAT,), jnp.float32, -s, s)}
    _L1_gnn_all = _L1_gnn_setup()
    _L1_gnn_in = {k: v for k, v in _L1_gnn_all.items() if k in ('W1', 'b1', 'W2', 'b2', 'W4', 'b4')}
    del _L1_gnn_all

    def _L2_gnn_setup():
        import jax, jax.numpy as jnp
        import numpy as np
        N, E, D_IN, D_OUT = (6250, 75000, 128, 128)
        BETA, ALPHA = (0.4, 0.6)

        def gcn_conv(x, edge_index, W, b):
            n = x.shape[0]
            loops = jnp.arange(n, dtype=edge_index.dtype)
            src = jnp.concatenate([edge_index[0], loops])
            dst = jnp.concatenate([edge_index[1], loops])
            deg = jax.ops.segment_sum(jnp.ones_like(dst, jnp.float32), dst, num_segments=n)
            d_inv_sqrt = jax.lax.rsqrt(deg)
            norm = d_inv_sqrt[src] * d_inv_sqrt[dst]
            xw = x @ W.T
            out = jax.ops.segment_sum(xw[src] * norm[:, None], dst, num_segments=n)
            return out + b
        key = jax.random.key(seed)
        ks = jax.random.split(key, 8)

        def xavier(k, shape):
            std = (2.0 / (shape[0] + shape[1])) ** 0.5
            return jax.random.normal(k, shape, jnp.float32) * std
        x = jax.random.normal(ks[0], (N, D_IN), jnp.float32)
        edge_index = jax.random.randint(ks[1], (2, E), 0, N, jnp.int32)
        Wq = xavier(ks[2], (D_IN, D_OUT))
        Wk = xavier(ks[3], (D_IN, D_OUT))
        Wv = xavier(ks[4], (D_IN, D_IN))
        W_gcn = xavier(ks[5], (D_IN, D_IN))
        b_gcn = jnp.zeros((D_IN,), jnp.float32)
        W_lin = xavier(ks[6], (D_OUT, D_IN))
        b_lin = jnp.zeros((D_OUT,), jnp.float32)
        return {'x': x, 'edge_index': edge_index, 'Wq': Wq, 'Wk': Wk, 'Wv': Wv, 'W_gcn': W_gcn, 'b_gcn': b_gcn, 'W_lin': W_lin, 'b_lin': b_lin}
    _L2_gnn_all = _L2_gnn_setup()
    _L2_gnn_in = {k: v for k, v in _L2_gnn_all.items() if k in ('Wq', 'Wk', 'Wv', 'W_gcn', 'b_gcn', 'W_lin', 'b_lin')}
    del _L2_gnn_all

    def _L3_gnn_setup():
        import jax, jax.numpy as jnp
        import numpy as np
        BN_EPS = 1e-05

        def _batchnorm(h, gamma, beta):
            mu = jnp.mean(h, axis=0)
            var = jnp.mean(jnp.square(h - mu), axis=0)
            return (h - mu) * jax.lax.rsqrt(var + BN_EPS) * gamma + beta
        key = jax.random.key(seed)
        ks = jax.random.split(key, 8)
        N, E, D = (6250, 100000, 128)
        x = jax.random.normal(ks[0], (N, D), dtype=jnp.float32)
        edge_index = jax.random.randint(ks[1], (2, E), 0, N, dtype=jnp.int64)
        s = 1.0 / np.sqrt(D)
        W1 = jax.random.uniform(ks[2], (D, D), jnp.float32, -s, s)
        b1 = jax.random.uniform(ks[3], (D,), jnp.float32, -s, s)
        W2 = jax.random.uniform(ks[4], (D, D), jnp.float32, -s, s)
        b2 = jax.random.uniform(ks[5], (D,), jnp.float32, -s, s)
        g1 = jnp.ones((D,), jnp.float32)
        be1 = jnp.zeros((D,), jnp.float32)
        g2 = jnp.ones((D,), jnp.float32)
        be2 = jnp.zeros((D,), jnp.float32)
        eps = jnp.zeros((), jnp.float32)
        return {'x': x, 'edge_index': edge_index, 'eps': eps, 'W1': W1, 'b1': b1, 'g1': g1, 'be1': be1, 'W2': W2, 'b2': b2, 'g2': g2, 'be2': be2}
    _L3_gnn_all = _L3_gnn_setup()
    _L3_gnn_in = {k: v for k, v in _L3_gnn_all.items() if k in ('eps', 'W1', 'b1', 'g1', 'be1', 'W2', 'b2', 'g2', 'be2')}
    del _L3_gnn_all
    return {'x': x, 'src': src, 'dst': dst, 'L0_gnn_W': _L0_gnn_in['W'], 'L0_gnn_att_src': _L0_gnn_in['att_src'], 'L0_gnn_att_dst': _L0_gnn_in['att_dst'], 'L0_gnn_bias': _L0_gnn_in['bias'], 'L1_gnn_W1': _L1_gnn_in['W1'], 'L1_gnn_b1': _L1_gnn_in['b1'], 'L1_gnn_W2': _L1_gnn_in['W2'], 'L1_gnn_b2': _L1_gnn_in['b2'], 'L1_gnn_W4': _L1_gnn_in['W4'], 'L1_gnn_b4': _L1_gnn_in['b4'], 'L2_gnn_Wq': _L2_gnn_in['Wq'], 'L2_gnn_Wk': _L2_gnn_in['Wk'], 'L2_gnn_Wv': _L2_gnn_in['Wv'], 'L2_gnn_W_gcn': _L2_gnn_in['W_gcn'], 'L2_gnn_b_gcn': _L2_gnn_in['b_gcn'], 'L2_gnn_W_lin': _L2_gnn_in['W_lin'], 'L2_gnn_b_lin': _L2_gnn_in['b_lin'], 'L3_gnn_eps': _L3_gnn_in['eps'], 'L3_gnn_W1': _L3_gnn_in['W1'], 'L3_gnn_b1': _L3_gnn_in['b1'], 'L3_gnn_g1': _L3_gnn_in['g1'], 'L3_gnn_be1': _L3_gnn_in['be1'], 'L3_gnn_W2': _L3_gnn_in['W2'], 'L3_gnn_b2': _L3_gnn_in['b2'], 'L3_gnn_g2': _L3_gnn_in['g2'], 'L3_gnn_be2': _L3_gnn_in['be2']}

def reference(x, src, dst, L0_gnn_W, L0_gnn_att_src, L0_gnn_att_dst, L0_gnn_bias, L1_gnn_W1, L1_gnn_b1, L1_gnn_W2, L1_gnn_b2, L1_gnn_W4, L1_gnn_b4, L2_gnn_Wq, L2_gnn_Wk, L2_gnn_Wv, L2_gnn_W_gcn, L2_gnn_b_gcn, L2_gnn_W_lin, L2_gnn_b_lin, L3_gnn_eps, L3_gnn_W1, L3_gnn_b1, L3_gnn_g1, L3_gnn_be1, L3_gnn_W2, L3_gnn_b2, L3_gnn_g2, L3_gnn_be2):
    import jax
    import jax.numpy as jnp

    def _L0_gnn_ref(x, edge_index, W, att_src, att_dst, bias):
        import jax, jax.numpy as jnp
        import numpy as np
        N = 6250
        E = 100000
        IN_C = 128
        OUT_C = 32
        HEADS = 4
        NEG_SLOPE = 0.2
        n = x.shape[0]
        loop = jnp.arange(n, dtype=edge_index.dtype)
        src = jnp.concatenate([edge_index[0], loop])
        dst = jnp.concatenate([edge_index[1], loop])
        xp = (x @ W).reshape(n, HEADS, OUT_C)
        a_src = jnp.einsum('nhc,hc->nh', xp, att_src)
        a_dst = jnp.einsum('nhc,hc->nh', xp, att_dst)
        e = a_src[src] + a_dst[dst]
        e = jnp.where(e >= 0, e, NEG_SLOPE * e)
        m = jax.ops.segment_max(e, dst, num_segments=n)
        ex = jnp.exp(e - m[dst])
        denom = jax.ops.segment_sum(ex, dst, num_segments=n)
        alpha = ex / denom[dst]
        msgs = alpha[:, :, None] * xp[src]
        out = jax.ops.segment_sum(msgs, dst, num_segments=n)
        out = out.reshape(n, HEADS * OUT_C) + bias
        return jax.nn.relu(out)

    def _L1_gnn_ref(x, src, dst, W1, b1, W2, b2, W4, b4):
        import jax, jax.numpy as jnp
        import numpy as np
        N_NODES = 6250
        N_EDGES = 100000
        IN_FEAT = 128
        OUT_FEAT = 128
        n_nodes = x.shape[0]
        theta = x[dst] - x[src]
        w = jax.nn.sigmoid(jax.nn.relu(theta @ W1 + b1) @ W2 + b2)
        w_theta = w * theta
        agg = jax.ops.segment_sum(w_theta, dst, num_segments=n_nodes)
        indeg = jax.ops.segment_sum(jnp.ones((dst.shape[0], 1), x.dtype), dst, num_segments=n_nodes)
        return agg + indeg * (x @ W4 + b4)

    def _L2_gnn_ref(x, edge_index, Wq, Wk, Wv, W_gcn, b_gcn, W_lin, b_lin):
        import jax, jax.numpy as jnp
        import numpy as np
        N, E, D_IN, D_OUT = (6250, 75000, 128, 128)
        BETA, ALPHA = (0.4, 0.6)

        def gcn_conv(x, edge_index, W, b):
            n = x.shape[0]
            loops = jnp.arange(n, dtype=edge_index.dtype)
            src = jnp.concatenate([edge_index[0], loops])
            dst = jnp.concatenate([edge_index[1], loops])
            deg = jax.ops.segment_sum(jnp.ones_like(dst, jnp.float32), dst, num_segments=n)
            d_inv_sqrt = jax.lax.rsqrt(deg)
            norm = d_inv_sqrt[src] * d_inv_sqrt[dst]
            xw = x @ W.T
            out = jax.ops.segment_sum(xw[src] * norm[:, None], dst, num_segments=n)
            return out + b
        n, d_in = x.shape
        q = x @ Wq
        q_hat = q / jnp.linalg.norm(q)
        k = x @ Wk
        k_hat = k / jnp.linalg.norm(k)
        v = x @ Wv
        qk = q_hat @ k_hat.sum(axis=0) / d_in
        scale = 1.0 / (1.0 + qk)
        attn = v + q_hat @ (k_hat.T @ v) / d_in
        Z = BETA * scale[:, None] * attn + (1.0 - BETA) * x
        gcn = gcn_conv(x, edge_index, W_gcn, b_gcn)
        Z_out = (1.0 - ALPHA) * Z + ALPHA * gcn
        return Z_out @ W_lin.T + b_lin

    def _L3_gnn_ref(x, edge_index, eps, W1, b1, g1, be1, W2, b2, g2, be2):
        import jax, jax.numpy as jnp
        import numpy as np
        BN_EPS = 1e-05

        def _batchnorm(h, gamma, beta):
            mu = jnp.mean(h, axis=0)
            var = jnp.mean(jnp.square(h - mu), axis=0)
            return (h - mu) * jax.lax.rsqrt(var + BN_EPS) * gamma + beta
        N = x.shape[0]
        src, dst = (edge_index[0], edge_index[1])
        agg = jax.ops.segment_sum(x[src], dst, num_segments=N)
        h = (1.0 + eps) * x + agg
        h = h @ W1.T + b1
        h = jax.nn.relu(_batchnorm(h, g1, be1))
        h = h @ W2.T + b2
        return jax.nn.relu(_batchnorm(h, g2, be2))
    edge_index = jnp.stack([src, dst])
    x = _layernorm(x + _L0_gnn_ref(x, edge_index, L0_gnn_W, L0_gnn_att_src, L0_gnn_att_dst, L0_gnn_bias), axis=-1)
    x = _layernorm(x + _L1_gnn_ref(x, src, dst, L1_gnn_W1, L1_gnn_b1, L1_gnn_W2, L1_gnn_b2, L1_gnn_W4, L1_gnn_b4), axis=-1)
    x = _layernorm(x + _L2_gnn_ref(x, edge_index, L2_gnn_Wq, L2_gnn_Wk, L2_gnn_Wv, L2_gnn_W_gcn, L2_gnn_b_gcn, L2_gnn_W_lin, L2_gnn_b_lin), axis=-1)
    x = _layernorm(x + _L3_gnn_ref(x, edge_index, L3_gnn_eps, L3_gnn_W1, L3_gnn_b1, L3_gnn_g1, L3_gnn_be1, L3_gnn_W2, L3_gnn_b2, L3_gnn_g2, L3_gnn_be2), axis=-1)
    return x

_drawn_inputs = setup_inputs


def setup_inputs(seed=0):
    import zlib

    import numpy as np

    out = dict(_drawn_inputs(seed))
    spreads = {'L0_gnn_bias': (0.0, 0.1),
     'L2_gnn_b_gcn': (0.0, 0.1),
     'L2_gnn_b_lin': (0.0, 0.1),
     'L3_gnn_g1': (1.0, 0.2),
     'L3_gnn_be1': (0.0, 0.1),
     'L3_gnn_g2': (1.0, 0.2),
     'L3_gnn_be2': (0.0, 0.1)}
    factors = {'L1_gnn_b1': 21.976,
     'L2_gnn_Wq': 64.0,
     'L2_gnn_Wk': 64.0,
     'L3_gnn_b1': 64.0,
     'L3_gnn_b2': 64.0}
    for name, (base, spread) in spreads.items():
        noise = np.random.default_rng([zlib.crc32(name.encode()), seed]).standard_normal(out[name].shape)
        drawn = base * np.exp(spread * noise) if base else spread * noise
        out[name] = jnp.asarray(drawn.astype(out[name].dtype))
    for name, factor in factors.items():
        out[name] = (out[name] * factor).astype(out[name].dtype)
    return out
```

```python
import numpy as np
from contextlib import ExitStack

import concourse.bass as bass
from concourse import mybir

P = 128
N = 6250
E = 106250
D = 128
H = 4
HC = D // H
NB = -(-N // P)
LAST = N - (NB - 1) * P
CB = 7
NCH = NB // CB
TILES = -(-E // P)
BT = 4
RB = 4
RT = RB * BT
ITERS = -(-TILES // RT)
IC = -(-(ITERS + 1) * RT // P)
TPAD = IC * P
FULL = E // P
REST = E - FULL * P
SLOPE = 0.2
ALPHA, BETA = 0.6, 0.4
LN_EPS = 1e-5
BN_EPS = 1e-5
RANGE = 60.0
FAR = 30000
WS = D + H
WAB = 2 * D
FM = 512
NFM = N // FM
FREST = N - NFM * FM
F32 = mybir.dt.float32
I32 = mybir.dt.int32
ALU = mybir.AluOpType
ACT = mybir.ActivationFunctionType
AX = mybir.AxisListType


class Chain:

    def __init__(self, eng, sem):
        self.eng, self.sem, self.n, self.i, self.per = eng, sem, 0, None, 0

    def enter(self, i, per):
        self.i, self.per, self.start = i, per, self.n

    def leave(self, count):
        assert self.n - self.start == self.per, (self.n - self.start, self.per)
        self.n, self.i = self.start + self.per * count, None

    def mark(self, ins):
        ins.then_inc(self.sem, 1)
        self.n += 1

    def wait(self):
        self.eng.wait_ge(self.sem, self.n if self.i is None else self.i * self.per + self.n)

    def link(self, ins):
        self.mark(ins)
        self.wait()


def gnn(nc, a, out, table):
    ctx = ExitStack()
    with ctx:
        def sb(name, shape, dt=F32):
            return ctx.enter_context(nc.sbuf_tensor(name, shape, dt))

        def sem(name):
            return ctx.enter_context(nc.semaphore(name))

        X = sb("X", [P, NB, D])
        AB = sb("AB", [P, NB + 1, WAB])
        sums = sb("sums", [P, NB + 1, WS])
        selfw = sb("selfw", [P, NB, H])
        valid = sb("valid", [P, NB])
        dinv = sb("dinv", [P, NB])
        ABf = AB[:, :, :].rearrange("p b c -> p (b c)")
        HT = [ABf[:, 0:NB * P], ABf[:, NB * P:2 * NB * P]]
        srcI = sb("srcI", [P, TPAD], I32)
        relF = sb("relF", [P, TPAD])
        blk = sb("blk", [1, TPAD], I32)
        idx = sb("idx", [P, RT], I32)
        onehot = sb("onehot", [P, 2 * BT, 2 * P])
        onehotT = sb("onehotT", [P, BT, 2, P])
        rows = sb("rows", [P, RT, 2 * D])
        msg = sb("msg", [P, 2 * BT, WS])
        diff = sb("diff", [P, 2, BT, D])
        prod = sb("prod", [P, D])
        score = sb("score", [P, 2, BT, H])
        logit = sb("logit", [P, 2, BT])
        ident = sb("ident", [P, P])
        ones = sb("ones", [P, P])
        iota = sb("iota", [P, 2 * P])
        hmask = sb("hmask", [P, H])
        eps_ln = sb("eps_ln", [P, 1])
        wA = sb("wA", [P, D + 2 * H])
        wB = sb("wB", [P, 2 * D])
        wX = sb("wX", [P, 2 * D + 2])
        wG = sb("wG", [P, P])
        W = {k: sb(f"w_{k}", [P, P]) for k in
             ("q", "k", "v", "gcn", "lin", "w1", "w2", "qT", "kT", "linT", "KQ", "w1T", "w2T", "gram", "gv", "t")}
        row = {k: sb(f"row_{k}", [P, D]) for k in ("bias", "b1", "w2", "b4", "blin")}
        col = {k: sb(f"col_{k}", [P, 1]) for k in
               ("as", "ad", "b2", "bg", "eps", "lb1", "g1", "be1", "lb2", "g2", "be2")}
        att = sb("att", [P, 2 * H])
        tmp = sb("tmp", [P, CB, D])
        res = sb("res", [P, CB, D])
        relv = sb("relv", [P, IC, P])
        xT = sb("xT", [P, 2, P])
        stats = sb("stats", [P, CB, 6])
        mv = sb("mv", [P, CB, 2])
        rstd = sb("rstd", [P, CB])
        firsti = sb("firsti", [P, IC], I32)
        firstf = sb("firstf", [P, IC])
        den = sb("den", [P, CB, H])[:, :, :]
        top = sb("top", [P, 3 * H])
        bound = sb("bound", [P, NB, H])
        own = sb("own", [P, NB, H])
        scal = sb("scal", [P, 12])
        sx = sb("sx", [P, 1])
        bnst = sb("bnst", [P, NFM + 1, 6])
        bnmv = sb("bnmv", [P, 8])

        bank = [ctx.enter_context(nc.psum_tensor(f"bank{i}", [P, 512], F32)) for i in range(8)]

        semaphores = {}

        def sem(phase, name):
            key = f"{phase}_{name}"
            if key not in semaphores:
                semaphores[key] = nc.alloc_semaphore(key)
            return semaphores[key]

        def clear_semaphores():
            nc.clear_and_free_semaphores(list(semaphores.values()))
            semaphores.clear()
            nc.all_engine_barrier()

        def chunk(t, c, of=slice(None)):
            return t[:, bass.ds(c * CB, CB), of]

        def table_rows(l, c):
            return table[l].rearrange("(b p) c -> p b c", p=P)[:, bass.ds(c * CB, CB), :]

        def first_blocks(eng, tile, count):
            return nc.values_load_multi_w_load_instructions(
                blk[0:1, bass.ds(tile, count)], engines=[eng.engine], min_val=0, max_val=NB - 1,
                skip_runtime_bounds_check_because="every dst is below N")[1]

        def zeros(k, width):
            return iota[:, 0:1].unsqueeze(2).broadcast_to([P, k, width])

        def pass_gate(eng, S):
            eng.sem_inc(S("gate" + str(eng.engine)[-4:]), 1)

        def normalise(dve, seq, nb, S, k, mask, to=lambda j: res[:, j, :]):
            for j in range(nb):
                seq.mark(dve.bn_stats(stats[:, j, :], tmp[:, j, :]))
            seq.wait()
            pass_gate(dve, S)
            for j in range(nb - 1):
                seq.mark(dve.bn_aggr(mv[:, j, :], stats[:, j, :]))
            seq.wait()
            pass_gate(dve, S)
            dve.bn_aggr(mv[:, nb - 1, :], stats[:, nb - 1, :]).then_inc(S("var"), 1)
            dve.wait_ge(S("root"), k)
            seq.link(dve.reciprocal(rstd[:, 0:nb], rstd[:, 0:nb]))
            seq.link(dve.tensor_tensor(rstd[:, 0:nb], rstd[:, 0:nb], mask, ALU.mult))
            for j in range(nb):
                seq.mark(dve.tensor_scalar(to(j), tmp[:, j, :], mv[:, j, 0:1], rstd[:, j:j + 1],
                                           op0=ALU.subtract, op1=ALU.mult))
            seq.wait()

        def roots(act, nb, S, k):
            act.wait_ge(S("var"), k)
            act.activation(rstd[:, 0:nb], mv[:, 0:nb, 1], ACT.Sqrt, bias=eps_ln[:, :]).then_inc(S("root"), 1)

        NORM = 3 * CB + 1

        def prepare():
            def S(name):
                return sem("prep", name)

            dst_t = tmp[:, :, :].bitcast(I32)
            src_t = res[:, :, :].bitcast(I32)
            src_f = AB[:, 0:IC, 0:P]
            to_turn = [relv[:, c, :] for c in range(IC)] + [src_f[:, c, :] for c in range(IC)]
            loads = [(wA[:, 0:D], a["L0_gnn_W"]),
                     (col["as"][:, :], a["L0_gnn_att_src"].rearrange("h (c o) -> (h c) o", o=1)),
                     (col["ad"][:, :], a["L0_gnn_att_dst"].rearrange("h (c o) -> (h c) o", o=1)),
                     (wB[:, 0:D], a["L1_gnn_W1"]), (wB[:, D:2 * D], a["L1_gnn_W4"]),
                     (col["b2"][:, :], a["L1_gnn_b2"].partition_broadcast(P)),
                     (row["w2"][:, :], a["L1_gnn_W2"].rearrange("k o -> (k o)").partition_broadcast(P)),
                     (W["q"][:, :], a["L2_gnn_Wq"]), (W["k"][:, :], a["L2_gnn_Wk"]), (W["v"][:, :], a["L2_gnn_Wv"]),
                     (W["gcn"][:, :], a["L2_gnn_W_gcn"]), (W["lin"][:, :], a["L2_gnn_W_lin"]),
                     (W["w1"][:, :], a["L3_gnn_W1"]), (W["w2"][:, :], a["L3_gnn_W2"]),
                     (col["eps"][:, :], a["L3_gnn_eps"].partition_broadcast(P))]
            loads += [(row[r][:, :], a[name].partition_broadcast(P)) for r, name in
                      (("bias", "L0_gnn_bias"), ("b1", "L1_gnn_b1"), ("b4", "L1_gnn_b4"), ("blin", "L2_gnn_b_lin"))]
            loads += [(col[c][:, :], a[name].rearrange("(p o) -> p o", o=1)) for c, name in
                      (("bg", "L2_gnn_b_gcn"), ("lb1", "L3_gnn_b1"), ("g1", "L3_gnn_g1"), ("be1", "L3_gnn_be1"),
                       ("lb2", "L3_gnn_b2"), ("g2", "L3_gnn_g2"), ("be2", "L3_gnn_be2"))]

            with nc.Block() as block:
                @block.sync
                def _(sp):
                    sp.wait_ge(S("filled"), 1)
                    t0 = (IC - 1) * P
                    for v, name in ((dst_t, "dst"), (src_t, "src")):
                        e = a[name]
                        sp.dma_start(v[:, 0:IC - 1, :], e[0:t0 * P].rearrange("(c p e) -> p c e", p=P, e=P)).then_inc(S("idx"), 16)
                        sp.dma_start(v[0:FULL - t0, IC - 1, :], e[t0 * P:FULL * P].rearrange("(p e) -> p e", e=P)).then_inc(S("idx"), 16)
                        sp.dma_start(v[FULL - t0:FULL - t0 + 1, IC - 1, 0:REST],
                                     e[FULL * P:E].rearrange("(p e) -> p e", p=1)).then_inc(S("idx"), 16)
                    sp.dma_start(blk[0:1, 0:FULL], a["dst"][0:FULL * P].rearrange("(t e) -> e t", e=P)[0:1, :],
                                 allow_slow_non_contiguous=True).then_inc(S("first"), 16)
                    sp.dma_start(blk[0:1, FULL:FULL + 1],
                                 a["dst"][FULL * P:FULL * P + 1].rearrange("(p e) -> p e", p=1)).then_inc(S("first"), 16)
                    sp.dma_start(X[:, 0:NB - 1, :], a["x"][0:(NB - 1) * P].rearrange("(b p) c -> p b c", p=P)).then_inc(S("x"), 16)
                    sp.dma_start(X[0:LAST, NB - 1, :], a["x"][(NB - 1) * P:N]).then_inc(S("x"), 16)
                    sp.wait_ge(S("x"), 32)

                @block.gpsimd
                def _(pool):
                    seq = Chain(pool, S("pool"))
                    seq.mark(pool.memset(dst_t[:, IC - 1, :], FAR))
                    seq.mark(pool.memset(src_t[:, IC - 1, :], 0))
                    seq.mark(pool.memset(blk[:, :], 0))
                    seq.link(pool.memset(X[:, NB - 1, :], 0.0))
                    pool.sem_inc(S("filled"), 1)
                    seq.mark(pool.memset(ident[:, :], 0.0))
                    seq.mark(pool.memset(hmask[:, :], 1.0))
                    seq.mark(pool.memset(valid[:, :], 1.0))
                    seq.mark(pool.memset(ones[:, :], 1.0))
                    seq.mark(pool.memset(eps_ln[:, :], LN_EPS))
                    seq.link(pool.iota(iota[:, :], pattern=[[1, 2 * P]], base=0, channel_multiplier=0,
                                       allow_small_or_imprecise_dtypes=True))
                    seq.mark(pool.affine_select(out=ident[:, :], in_=ident[:, :], compare_op=ALU.not_equal, fill=1.0,
                                                base=0, pattern=[[-1, P]], channel_multiplier=1))
                    seq.mark(pool.affine_select(out=valid[:, NB - 1:NB], in_=valid[:, NB - 1:NB], compare_op=ALU.is_ge,
                                                fill=0.0, base=LAST - 1, pattern=[[0, 1]], channel_multiplier=-1))
                    seq.link(pool.affine_select(out=hmask[:, :], in_=hmask[:, :], compare_op=ALU.is_ge, fill=0.0,
                                                base=0, pattern=[[-HC, H]], channel_multiplier=1))
                    seq.link(pool.affine_select(out=hmask[:, :], in_=hmask[:, :], compare_op=ALU.is_ge, fill=0.0,
                                                base=HC - 1, pattern=[[HC, H]], channel_multiplier=-1))
                    pool.sem_inc(S("consts"), 1)
                    seq.mark(pool.memset(sums[:, :, :], 0.0))
                    seq.mark(pool.memset(AB[:, NB, :], 0.0))
                    seq.link(pool.memset(msg[:, :, D:D + H], 1.0))

                @block.scalar
                def _(act):
                    for to, of in loads:
                        act.dma_start(to, of).then_inc(S("w"), 16)
                    act.wait_ge(S("w"), 16 * len(loads))
                    act.sem_inc(S("weights"), 1)
                    act.wait_ge(S("wt"), 1)
                    act.activation(W["t"][:, :], bank[4][:, 0:P], ACT.Copy).then_inc(S("wt_sb"), 1)
                    act.activation(W["qT"][:, :], bank[4][:, P:2 * P], ACT.Copy).then_inc(S("wt_sb"), 1)
                    act.activation(W["kT"][:, :], bank[4][:, 2 * P:3 * P], ACT.Copy).then_inc(S("wt_sb"), 1)
                    act.activation(W["linT"][:, :], bank[4][:, 3 * P:4 * P], ACT.Copy).then_inc(S("wt_sb"), 1)
                    act.activation(W["w1T"][:, :], bank[5][:, 0:P], ACT.Copy).then_inc(S("wt_sb"), 1)
                    act.activation(W["w2T"][:, :], bank[5][:, P:2 * P], ACT.Copy).then_inc(S("wt_sb"), 1)
                    act.wait_ge(S("wp"), 1)
                    act.activation(wA[:, D:D + 2 * H], bank[6][:, 0:2 * H], ACT.Copy).then_inc(S("act"), 1)
                    act.activation(W["KQ"][:, :], bank[6][:, P:2 * P], ACT.Copy).then_inc(S("act"), 1)
                    act.activation(wG[:, :], bank[6][:, 2 * P:3 * P], ACT.Copy, scale=ALPHA).then_inc(S("act"), 1)
                    act.wait_ge(S("act"), 3)

                @block.tensor
                def _(pe):
                    pe.wait_ge(S("consts"), 1)
                    pe.wait_ge(S("weights"), 1)
                    for b, w in enumerate((wA[:, 0:D], W["q"][:, :], W["k"][:, :], W["lin"][:, :])):
                        pe.transpose(bank[4][:, b * P:(b + 1) * P], w, ident[:, :])
                    pe.transpose(bank[5][:, 0:P], W["w1"][:, :], ident[:, :])
                    pe.transpose(bank[5][:, P:2 * P], W["w2"][:, :], ident[:, :]).then_inc(S("wt"), 1)
                    pe.wait_ge(S("tof"), 1)
                    for j, v in enumerate(to_turn):
                        pe.transpose(bank[j // 4][:, (j % 4) * P:(j % 4 + 1) * P], v, ident[:, :]).then_inc(S("turned"), 1)
                    pe.wait_ge(S("wt_sb"), 6)
                    pe.wait_ge(S("att"), 1)
                    pe.matmul(bank[6][:, 0:2 * H], W["t"][:, :], att[:, :], start=True, stop=True)
                    pe.matmul(bank[6][:, P:2 * P], W["kT"][:, :], W["qT"][:, :], start=True, stop=True)
                    pe.matmul(bank[6][:, 2 * P:3 * P], W["gcn"][:, :], W["linT"][:, :], start=True, stop=True).then_inc(S("wp"), 1)
                    pe.matmul(bank[7][:, 0:P], W["gram"][:, :], W["linT"][:, :], start=True, stop=True).then_inc(S("bl"), 1)

                @block.vector
                def _(dve):
                    seq = Chain(dve, S("dve"))
                    dve.wait_ge(S("idx"), 16 * 6)
                    seq.link(dve.tensor_scalar(firsti[:, :], dst_t[:, :, 0], N - 1, None, op0=ALU.min))
                    seq.link(dve.tensor_scalar(firsti[:, :], firsti[:, :], 7, 7, op0=ALU.logical_shift_right,
                                               op1=ALU.logical_shift_left))
                    seq.link(dve.tensor_copy(firstf[:, :], firsti[:, :]))
                    seq.mark(dve.tensor_copy(src_f, src_t))
                    seq.link(dve.tensor_tensor(relv[:, :, :], dst_t, firstf[:, :].unsqueeze(2).broadcast_to([P, IC, P]),
                                               ALU.subtract))
                    dve.sem_inc(S("tof"), 1)
                    dve.wait_ge(S("first"), 32)
                    seq.mark(dve.tensor_scalar(blk[:, :], blk[:, :], 7, None, op0=ALU.logical_shift_right))
                    dve.wait_ge(S("consts"), 1)
                    dve.wait_ge(S("weights"), 1)
                    seq.mark(dve.tensor_scalar(att[:, 0:H], hmask[:, :], col["as"][:, :], None, op0=ALU.mult))
                    seq.mark(dve.tensor_scalar(att[:, H:2 * H], hmask[:, :], col["ad"][:, :], None, op0=ALU.mult))
                    seq.link(dve.tensor_scalar(W["gram"][:, :], ones[:, :], col["bg"][:, :], None, op0=ALU.mult))
                    dve.sem_inc(S("att"), 1)
                    for j in range(2 * IC):
                        dve.wait_ge(S("turned"), min(4 * (j // 4) + 4, 2 * IC))
                        seq.mark(dve.tensor_copy((relF if j < IC else srcI)[:, (j % IC) * P:(j % IC + 1) * P],
                                                 bank[j // 4][:, (j % 4) * P:(j % 4 + 1) * P]))
                    dve.wait_ge(S("bl"), 1)
                    seq.link(dve.scalar_tensor_tensor(row["blin"][:, :], bank[7][:, 0:P], ALPHA, row["blin"][:, :],
                                                      op0=ALU.mult, op1=ALU.add))

        def project():
            def S(name):
                return sem("proj", name)

            with nc.Block() as block:
                @block.tensor
                def _(pe):
                    pe.sem_inc(S("turned"), 1)
                    with pe.Fori(0, NCH) as c:
                        pe.wait_ge(S("res"), c + 1)
                        pe.transpose(bank[0][:, 0:P], res[:, 0, :], ident[:, :]).then_inc(S("turned"), 1)
                        for j in range(CB):
                            if j + 1 < CB:
                                t = pe.transpose(bank[(j + 1) % 2][:, 0:P], res[:, j + 1, :], ident[:, :])
                                t.then_inc(S("turned"), 1)
                            pe.wait_ge(S("xT"), c * CB + j + 1)
                            pe.wait_ge(S("out_free"), c * CB + j + (2 if j == 0 else 1))
                            pe.matmul(bank[2 + j % 2][:, 0:D + 2 * H], xT[:, j % 2, :], wA[:, :],
                                      start=True, stop=True).then_inc(S("out"), 1)
                    pe.wait_ge(S("top"), 1)
                    pe.transpose(bank[4][0:H, 0:P], top[:, 0:H], ident[:, :]).then_inc(S("topT"), 1)
                    pe.wait_ge(S("diag"), 1)
                    pe.matmul(bank[5][:, 0:H], ones[0:H, :], top[0:H, 2 * H:3 * H], start=True, stop=True).then_inc(S("gmax"), 1)

                @block.scalar
                def _(act):
                    with act.Fori(0, NCH) as c:
                        act.wait_ge(S("turned"), c * CB + 1)
                        act.activation(res[:, :, :], chunk(X, c), ACT.Copy).then_inc(S("res"), 1)
                        for j in range(CB):
                            act.wait_ge(S("turned"), c * CB + j + 2)
                            act.activation(xT[:, j % 2, :], bank[j % 2][:, 0:P], ACT.Copy).then_inc(S("xT"), 1)
                    act.wait_ge(S("selfz"), 1)
                    act.activation(selfw[:, :, :], own[:, :, :], ACT.Exp).then_inc(S("selfw"), 1)
                    act.wait_ge(S("selfw"), 1)

                @block.vector
                def _(dve):
                    seq = Chain(dve, S("dve"))
                    dve.sem_inc(S("out_free"), 2)
                    with dve.Fori(0, NCH) as c:
                        for j in range(CB):
                            dve.wait_ge(S("out"), c * CB + j + 1)
                            dve.tensor_copy(AB[:, bass.ds(c * CB + j, 1), 0:D + 2 * H],
                                            bank[2 + j % 2][:, 0:D + 2 * H].unsqueeze(1)).then_inc(S("out_free"), 1)
                    dve.wait_ge(S("out_free"), 2 + NB)
                    a_s, a_d = AB[:, 0:NB, D:D + H], AB[:, 0:NB, D + H:D + 2 * H]
                    dve.tensor_reduce(top[:, 0:H], a_s.rearrange("p b h -> p h b"), axis=AX.X, op=ALU.max).then_inc(S("top"), 1)
                    dve.wait_ge(S("topT"), 1)
                    seq.link(dve.tensor_reduce(top[0:H, H:H + 1], bank[4][0:H, 0:P], axis=AX.X, op=ALU.max))
                    dve.tensor_scalar(top[0:H, 2 * H:3 * H], ident[0:H, 0:H], top[0:H, H:H + 1], None,
                                      op0=ALU.mult).then_inc(S("diag"), 1)
                    seq.link(dve.tensor_tensor(own[:, :, :], a_s, a_d, ALU.add))
                    seq.mark(dve.scalar_tensor_tensor(own[:, :, :], own[:, :, :], SLOPE, own[:, :, :],
                                                      op0=ALU.mult, op1=ALU.max))
                    dve.wait_ge(S("gmax"), 1)
                    seq.link(dve.tensor_tensor(bound[:, :, :], a_d, bank[5][:, 0:H].unsqueeze(1).broadcast_to([P, NB, H]), ALU.add))
                    seq.link(dve.scalar_tensor_tensor(bound[:, :, :], bound[:, :, :], SLOPE, bound[:, :, :],
                                                      op0=ALU.mult, op1=ALU.max))
                    seq.link(dve.scalar_tensor_tensor(AB[:, 0:NB, D + 2 * H:D + 3 * H], bound[:, :, :], -RANGE, own[:, :, :],
                                                      op0=ALU.add, op1=ALU.max))
                    seq.link(dve.tensor_tensor(own[:, :, :], own[:, :, :], AB[:, 0:NB, D + 2 * H:D + 3 * H], ALU.subtract))
                    dve.sem_inc(S("selfz"), 1)

                @block.sync
                def _(sp):
                    with sp.Fori(0, NCH) as c:
                        sp.wait_ge(S("out_free"), 2 + (c + 1) * CB)
                        sp.dma_start(table_rows(0, c), chunk(AB, c, slice(0, WS))).then_inc(S("stored"), 16)
                    sp.wait_ge(S("stored"), 16 * NCH)

        def gather_all(pool, l, S, width, taken, extra):
            def gather(q, k, index):
                pool.indirect_dma_start(
                    out=rows[:, q * BT + k, 0:width], out_offset=None, in_=table[l],
                    in_offset=bass.IndirectOffsetOnAxis(ap=index, axis=0)).then_inc(S(f"landed{q}"), 16)

            for q in range(RB):
                for k in range(BT):
                    gather(q, k, srcI[:, q * BT + k:q * BT + k + 1])
            with pool.Fori(1, ITERS) as i:
                for q in range(RB):
                    pool.wait_ge(S("staged"), i * RB + q - (RB - 1))
                    pool.wait_ge(taken, i * RT + q * BT - (RT - BT))
                    pass_gate(pool, S)
                    for k in range(BT):
                        gather(q, k, idx[:, q * BT + k:q * BT + k + 1])
            if extra:
                pool.wait_ge(S("staged"), ITERS * RB - (RB - 1))
                pool.wait_ge(taken, ITERS * RT - (RT - BT))
                for k in range(BT):
                    gather(0, k, idx[:, k:k + 1])

        def stage_indices(act, S, i, q):
            act.activation(idx[:, q * BT:(q + 1) * BT], srcI[:, bass.ds(i * RT + (q + RB) * BT, BT)],
                           ACT.Copy).then_inc(S("staged"), 1)

        def mark_nodes(dve, S, tile, k):
            dve.tensor_scalar(onehot[:, k, :], iota[:, :], relF[:, bass.ds(tile, 1)], None,
                              op0=ALU.is_equal).then_inc(S("hot"), 1)

        def add_sums(dve, S, tile, k, block, width):
            dve.wait_ge(S("summed"), tile + 1)
            dve.wait_ge(S("added"), tile + 2)
            to = sums[:, bass.ds(block, 2), 0:width]
            dve.tensor_tensor(to, to, bank[4 + k % 2][:, 0:2 * width].rearrange("p (b c) -> p b c", b=2),
                              ALU.add).then_inc(S("added"), 1)

        def sum_tile(pe, S, tile, k, value, width):
            pe.wait_ge(S("added"), tile + 1)
            for b in range(2):
                m = pe.matmul(bank[4 + k % 2][:, b * width:(b + 1) * width], onehot[:, k, b * P:(b + 1) * P],
                              value, start=True, stop=True)
            m.then_inc(S("summed"), 1)

        def turn(pe, k):
            pe.transpose(bank[k % 2][:, 0:P], onehot[:, k, 0:P], ident[:, :])
            return pe.transpose(bank[k % 2][:, P:2 * P], onehot[:, k, P:2 * P], ident[:, :])

        def take_turned(act, k):
            return act.activation(onehotT[:, k % BT, :, :],
                                  bank[k % 2][:, 0:2 * P].rearrange("p (b e) -> p b e", b=2), ACT.Copy)

        def edges0():
            def S(name):
                return sem("e0", name)

            with nc.Block() as block:
                @block.gpsimd
                def _(pool):
                    gather_all(pool, 0, S, WS, S("msgs"), False)

                @block.tensor
                def _(pe):
                    def spread(m, k, blks):
                        for b in range(2):
                            t = pe.matmul(bank[2 + m][:, k * 2 * H:(k + 1) * 2 * H], onehotT[:, k, b, :],
                                          AB[:, bass.ds(blks[k] + b, 1), D + H:D + 3 * H].rearrange("p o c -> p (o c)"),
                                          start=(b == 0), stop=(b == 1))
                        t.then_inc(S("spread"), 1)

                    blks = first_blocks(pe, 0, BT)
                    for k in range(BT):
                        pe.wait_ge(S("hot"), k + 1)
                        if k >= 2:
                            pe.wait_ge(S("hotT"), k - 1)
                        turn(pe, k).then_inc(S("turned"), 1)
                    for k in range(BT):
                        pe.wait_ge(S("hotT"), k + 1)
                        spread(0, k, blks)
                    with pe.Fori(0, ITERS) as i:
                        for q in range(RB):
                            t0, m = i * RT + q * BT, (q % 2) * BT
                            blks = first_blocks(pe, t0 + BT, BT)
                            for k in range(BT):
                                pe.wait_ge(S("hot"), t0 + BT + k + 1)
                                pe.wait_ge(S("hotT"), t0 + BT + k - 1)
                                turn(pe, (BT - m) + k).then_inc(S("turned"), 1)
                                if k >= 1:
                                    pe.wait_ge(S("hotT"), t0 + BT + k)
                                    spread(1 - q % 2, k - 1, blks)
                            pe.wait_ge(S("hotT"), t0 + 2 * BT)
                            spread(1 - q % 2, BT - 1, blks)
                            for k in range(BT):
                                pe.wait_ge(S("msgs"), t0 + k + 1)
                                sum_tile(pe, S, t0 + k, m + k, msg[:, m + k, :], WS)

                @block.scalar
                def _(act):
                    for k in range(BT):
                        act.wait_ge(S("turned"), k + 1)
                        take_turned(act, k).then_inc(S("hotT"), 1)
                    with act.Fori(0, ITERS) as i:
                        for q in range(RB):
                            m = (q % 2) * BT
                            act.wait_ge(S("scored"), i * RB + q + 1)
                            act.activation(msg[:, m:m + BT, D:D + H], score[:, q % 2, :, :], ACT.Exp).then_inc(S("weighed"), 1)
                            stage_indices(act, S, i, q)
                            for k in range(BT):
                                tile = i * RT + (q + 1) * BT + k
                                act.wait_ge(S("turned"), tile + 1)
                                act.wait_ge(S("spread"), tile - BT + 1)
                                take_turned(act, k).then_inc(S("hotT"), 1)

                @block.vector
                def _(dve):
                    dve.sem_inc(S("added"), 2)
                    seq = Chain(dve, S("dve"))
                    for k in range(BT):
                        mark_nodes(dve, S, k, k)
                    with dve.Fori(0, ITERS) as i:
                        seq.enter(i, 2 * RB)
                        for q in range(RB):
                            t0, m = i * RT + q * BT, (q % 2) * BT
                            blks = first_blocks(dve, t0, BT)
                            got = rows[:, q * BT:(q + 1) * BT, :]
                            sc = score[:, q % 2, :, :]
                            of_dst = bank[2 + q % 2][:, 0:BT * 2 * H].rearrange("p (k c) -> p k c", k=BT)
                            dve.wait_ge(S("spread"), t0 + BT)
                            dve.wait_ge(S(f"landed{q}"), (i + 1) * 16 * BT)
                            seq.link(dve.tensor_tensor(sc, got[:, :, D:D + H], of_dst[:, :, 0:H], ALU.add))
                            seq.link(dve.scalar_tensor_tensor(sc, sc, SLOPE, sc, op0=ALU.mult, op1=ALU.max))
                            dve.tensor_tensor(sc, sc, of_dst[:, :, H:2 * H], ALU.subtract).then_inc(S("scored"), 1)
                            for k in range(BT):
                                mark_nodes(dve, S, t0 + BT + k, (BT - m) + k)
                            dve.wait_ge(S("weighed"), i * RB + q + 1)
                            for k in range(BT):
                                w = msg[:, m + k, D:D + H].unsqueeze(2).broadcast_to([P, H, HC])
                                dve.tensor_tensor(msg[:, m + k, 0:D].rearrange("p (h c) -> p h c", h=H),
                                                  got[:, k, 0:D].rearrange("p (h c) -> p h c", h=H), w,
                                                  ALU.mult).then_inc(S("msgs"), 1)
                            for k in range(BT):
                                add_sums(dve, S, t0 + k, m + k, blks[k], WS)
                        seq.leave(ITERS)

        def nodes0():
            def S(name):
                return sem("n0", name)

            with nc.Block() as block:
                @block.vector
                def _(dve):
                    seq = Chain(dve, S("dve"))
                    with dve.Fori(0, NCH) as c:
                        seq.enter(c, 7 + NORM)
                        acc, w0 = chunk(sums, c, slice(0, D)), chunk(selfw, c)
                        seq.mark(dve.tensor_tensor(den, chunk(sums, c, slice(D, D + H)), w0, ALU.add))
                        for_heads = tmp[:, :, :].rearrange("p b (h c) -> p b h c", h=H)
                        seq.link(dve.tensor_tensor(for_heads, chunk(AB, c, slice(0, D)).rearrange("p b (h c) -> p b h c", h=H),
                                                   w0.unsqueeze(3).broadcast_to([P, CB, H, HC]), ALU.mult))
                        seq.mark(dve.reciprocal(den, den))
                        seq.link(dve.tensor_tensor(tmp[:, :, :], tmp[:, :, :], acc, ALU.add))
                        dve.sem_inc(S("sums_used"), 1)
                        seq.link(dve.tensor_tensor(for_heads, for_heads, den.unsqueeze(3).broadcast_to([P, CB, H, HC]), ALU.mult))
                        seq.link(dve.tensor_tensor(tmp[:, :, :], tmp[:, :, :], row["bias"][:, :].unsqueeze(1).broadcast_to([P, CB, D]), ALU.add))
                        seq.link(dve.scalar_tensor_tensor(tmp[:, :, :], tmp[:, :, :], 0.0, chunk(X, c), op0=ALU.max, op1=ALU.add))
                        dve.wait_ge(S("turned"), c * CB + 1)
                        dve.wait_ge(S("kept"), c + 1)
                        normalise(dve, seq, CB, S, c + 1, valid[:, bass.ds(c * CB, CB)])
                        dve.sem_inc(S("res"), 1)
                        seq.leave(NCH)

                @block.gpsimd
                def _(pool):
                    pool.sem_inc(S("kept"), 1)
                    pool.memset(msg[:, :, D + 1:D + 2], 1.0).then_inc(S("cleared"), 1)
                    with pool.Fori(0, NCH) as c:
                        pool.wait_ge(S("sums_used"), c + 1)
                        pool.tensor_copy(chunk(sums, c), zeros(CB, WS)).then_inc(S("cleared"), 1)
                        pool.wait_ge(S("res"), c + 1)
                        pool.tensor_copy(chunk(X, c), res[:, :, :]).then_inc(S("kept"), 1)
                    pool.wait_ge(S("kept"), NCH + 1)
                    pool.wait_ge(S("cleared"), NCH + 1)

                @block.tensor
                def _(pe):
                    pe.sem_inc(S("turned"), 1)
                    with pe.Fori(0, NCH) as c:
                        pe.wait_ge(S("res"), c + 1)
                        pe.transpose(bank[0][:, 0:P], res[:, 0, :], ident[:, :]).then_inc(S("turned"), 1)
                        for j in range(CB):
                            if j + 1 < CB:
                                t = pe.transpose(bank[(j + 1) % 2][:, 0:P], res[:, j + 1, :], ident[:, :])
                                t.then_inc(S("turned"), 1)
                            pe.wait_ge(S("xT"), c * CB + j + 1)
                            pe.wait_ge(S("ab"), c * CB + j + (2 if j == 0 else 1))
                            pe.matmul(bank[2 + j % 2][:, 0:2 * D], xT[:, j % 2, :], wB[:, :],
                                      start=True, stop=True).then_inc(S("out"), 1)

                @block.scalar
                def _(act):
                    act.sem_inc(S("ab"), 2)
                    with act.Fori(0, NCH) as c:
                        roots(act, CB, S, c + 1)

                        def to_ab(j):
                            act.wait_ge(S("out"), c * CB + j + 1)
                            act.activation(AB[:, bass.ds(c * CB + j, 1), :], bank[2 + j % 2][:, 0:2 * D].unsqueeze(1),
                                           ACT.Copy).then_inc(S("ab"), 1)

                        for j in range(CB):
                            act.wait_ge(S("turned"), c * CB + j + 2)
                            act.activation(xT[:, j % 2, :], bank[j % 2][:, 0:P], ACT.Copy).then_inc(S("xT"), 1)
                            if j:
                                to_ab(j - 1)
                        to_ab(CB - 1)

                @block.sync
                def _(sp):
                    with sp.Fori(0, NCH) as c:
                        sp.wait_ge(S("kept"), c + 2)
                        sp.dma_start(table_rows(1, c)[:, :, 0:D], chunk(X, c)).then_inc(S("stored"), 16)
                        sp.wait_ge(S("ab"), 2 + (c + 1) * CB)
                        sp.dma_start(table_rows(1, c)[:, :, D:2 * D], chunk(AB, c, slice(0, D))).then_inc(S("stored"), 16)
                    sp.wait_ge(S("stored"), 2 * 16 * NCH)

        def edges1():
            def S(name):
                return sem("e1", name)

            with nc.Block() as block:
                @block.gpsimd
                def _(pool):
                    gather_all(pool, 1, S, 2 * D, S("msgs"), True)

                @block.tensor
                def _(pe):
                    def spread(m, k, block):
                        for b in range(2):
                            t = pe.matmul(bank[2 + m][:, k * D:(k + 1) * D], onehotT[:, k, b, :],
                                          AB[:, bass.ds(block + b, 1), 0:D].rearrange("p o c -> p (o c)"),
                                          start=(b == 0), stop=(b == 1))
                        t.then_inc(S("spread"), 1)

                    blks = first_blocks(pe, 0, BT)
                    for k in range(BT):
                        pe.wait_ge(S("hot"), k + 1)
                        if k >= 2:
                            pe.wait_ge(S("hotT"), k - 1)
                        turn(pe, k).then_inc(S("turned"), 1)
                    pe.wait_ge(S("b1"), 1)
                    for k in range(BT):
                        pe.wait_ge(S("hotT"), k + 1)
                        spread(0, k, blks[k])
                        pe.wait_ge(S("hot"), BT + k + 1)
                        pe.wait_ge(S("hotT"), BT + k - 1)
                        turn(pe, BT + k).then_inc(S("turned"), 1)
                    with pe.Fori(0, ITERS) as i:
                        for q in range(RB):
                            t0, m = i * RT + q * BT, (q % 2) * BT
                            blks = first_blocks(pe, t0 + BT, BT)
                            for k in range(BT):
                                pe.wait_ge(S("hotT"), t0 + BT + k + 1)
                                spread(1 - q % 2, k, blks[k])
                            for k in range(BT):
                                pe.wait_ge(S("msgs"), t0 + k + 1)
                                sum_tile(pe, S, t0 + k, m + k, msg[:, m + k, 0:D + 2], D + 2)
                                pe.wait_ge(S("hot"), t0 + 2 * BT + k + 1)
                                pe.wait_ge(S("hotT"), t0 + 2 * BT + k - 1)
                                turn(pe, m + k).then_inc(S("turned"), 1)

                @block.scalar
                def _(act):
                    for k in range(2 * BT):
                        act.wait_ge(S("turned"), k + 1)
                        if k >= BT:
                            act.wait_ge(S("spread"), k - BT + 1)
                        take_turned(act, k).then_inc(S("hotT"), 1)
                    with act.Fori(0, ITERS) as i:
                        for q in range(RB):
                            m = (q % 2) * BT
                            act.wait_ge(S("scored"), i * RT + (q + 1) * BT)
                            act.activation(msg[:, m:m + BT, D:D + 1], logit[:, q % 2, :].unsqueeze(2), ACT.Sigmoid,
                                           bias=col["b2"][:, :]).then_inc(S("gated"), 1)
                            act.wait_ge(S("gated"), i * RB + q + 1)
                            for k in range(BT):
                                act.activation(msg[:, m + k, 0:D], rows[:, q * BT + k, 0:D], ACT.Copy,
                                               scale=msg[:, m + k, D:D + 1]).then_inc(S("msgs"), 1)
                                tile = i * RT + (q + 2) * BT + k
                                act.wait_ge(S("turned"), tile + 1)
                                act.wait_ge(S("spread"), tile - BT + 1)
                                take_turned(act, k).then_inc(S("hotT"), 1)
                            stage_indices(act, S, i, q)

                @block.vector
                def _(dve):
                    def logits(q, m, tiles, rounds):
                        dve.wait_ge(S("spread"), tiles)
                        dve.wait_ge(S(f"landed{q}"), rounds * 16 * BT)
                        seq.link(dve.tensor_tensor(diff[:, m, :, :], bank[2 + m][:, :].rearrange("p (k c) -> p k c", k=BT),
                                                   rows[:, q * BT:(q + 1) * BT, D:2 * D], ALU.subtract))
                        for k in range(BT):
                            dve.scalar_tensor_tensor(diff[:, m, k, :], diff[:, m, k, :], 0.0, row["w2"][:, :], op0=ALU.max,
                                                     op1=ALU.mult, accum_out=logit[:, m, k:k + 1]).then_inc(S("scored"), 1)

                    dve.sem_inc(S("added"), 2)
                    seq = Chain(dve, S("dve"))
                    for k in range(BT):
                        mark_nodes(dve, S, k, k)
                    dve.tensor_tensor(AB[:, 0:NB, 0:D], AB[:, 0:NB, 0:D], row["b1"][:, :].unsqueeze(1).broadcast_to([P, NB, D]),
                                      ALU.add).then_inc(S("b1"), 1)
                    for k in range(BT):
                        mark_nodes(dve, S, BT + k, BT + k)
                    logits(0, 0, BT, 1)
                    with dve.Fori(0, ITERS) as i:
                        seq.enter(i, RB)
                        for q in range(RB):
                            t0, m = i * RT + q * BT, (q % 2) * BT
                            blks = first_blocks(dve, t0, BT)
                            logits((q + 1) % RB, 1 - q % 2, t0 + 2 * BT, i + (1 if q + 1 < RB else 2))
                            for k in range(BT):
                                add_sums(dve, S, t0 + k, m + k, blks[k], D + 2)
                                mark_nodes(dve, S, t0 + 2 * BT + k, m + k)
                        seq.leave(ITERS)

        def nodes1():
            def S(name):
                return sem("n1", name)

            with nc.Block() as block:
                @block.vector
                def _(dve):
                    seq = Chain(dve, S("dve"))
                    gates, degree = sums[:, 0:NB, D], sums[:, 0:NB, D + 1]
                    dve.tensor_copy(dinv[:, :], degree).then_inc(S("deg"), 1)
                    dve.wait_ge(S("rootdeg"), 1)
                    seq.link(dve.reciprocal(dinv[:, :], dinv[:, :]))
                    with dve.Fori(0, NCH) as c:
                        seq.enter(c, 5 + NORM + 1)

                        def per_node(t):
                            return t.unsqueeze(2).broadcast_to([P, CB, D]) if len(t.shape) == 2 else t.broadcast_to([P, CB, D])
                        r4 = chunk(AB, c, slice(D, 2 * D))
                        seq.link(dve.scalar_tensor_tensor(tmp[:, :, :], chunk(sums, c, slice(D, D + 1)).broadcast_to([P, CB, D]), 1.0, chunk(X, c),
                                                          op0=ALU.add, op1=ALU.mult))
                        seq.mark(dve.tensor_tensor(tmp[:, :, :], tmp[:, :, :], chunk(sums, c, slice(0, D)), ALU.subtract))
                        seq.link(dve.tensor_tensor(r4, r4, row["b4"][:, :].unsqueeze(1).broadcast_to([P, CB, D]), ALU.add))
                        seq.link(dve.tensor_tensor(r4, r4, chunk(sums, c, slice(D + 1, D + 2)).broadcast_to([P, CB, D]), ALU.mult))
                        dve.sem_inc(S("sums_used"), 1)
                        seq.link(dve.tensor_tensor(tmp[:, :, :], tmp[:, :, :], r4, ALU.add))
                        dve.wait_ge(S("gram_free"), c + 1)
                        dve.wait_ge(S("kept"), c + 1)
                        normalise(dve, seq, CB, S, c + 1, valid[:, bass.ds(c * CB, CB)])
                        dve.sem_inc(S("res"), 1)
                        seq.link(dve.tensor_tensor(r4, res[:, :, :], dinv[:, bass.ds(c * CB, CB)].unsqueeze(2).broadcast_to([P, CB, D]), ALU.mult))
                        dve.sem_inc(S("scaled"), 1)
                        seq.leave(NCH)

                @block.gpsimd
                def _(pool):
                    pool.sem_inc(S("kept"), 1)
                    with pool.Fori(0, NCH) as c:
                        pool.wait_ge(S("sums_used"), c + 1)
                        pool.tensor_copy(chunk(sums, c), zeros(CB, WS)).then_inc(S("cleared"), 1)
                        pool.wait_ge(S("res"), c + 1)
                        pool.tensor_copy(chunk(X, c), res[:, :, :]).then_inc(S("kept"), 1)
                    pool.wait_ge(S("kept"), NCH + 1)
                    pool.wait_ge(S("cleared"), NCH)

                @block.tensor
                def _(pe):
                    zero = iota[:, 0:1].broadcast_to([P, P])
                    pe.matmul(bank[6][:, 0:P], ident[:, :], zero, start=True, stop=False, skip_group_check=True)
                    pe.matmul(bank[7][:, 0:1], ident[:, :], iota[:, 0:1], start=True, stop=False, skip_group_check=True)
                    pe.sem_inc(S("gram_free"), 1)
                    with pe.Fori(0, NCH) as c:
                        pe.wait_ge(S("res"), c + 1)
                        for j in range(CB):
                            pe.matmul(bank[6][:, 0:P], res[:, j, :], res[:, j, :], start=False, stop=False, skip_group_check=True)
                            t = pe.matmul(bank[7][:, 0:1], res[:, j, :], ones[:, 0:1], start=False, stop=False, skip_group_check=True)
                        t.then_inc(S("gram_free"), 1)
                    pe.matmul(bank[6][:, 0:P], ident[:, :], zero, start=False, stop=True, skip_group_check=True)
                    pe.matmul(bank[7][:, 0:1], ident[:, :], iota[:, 0:1], start=False, stop=True, skip_group_check=True).then_inc(S("gram"), 1)
                    pe.wait_ge(S("gram"), 1)

                @block.scalar
                def _(act):
                    act.wait_ge(S("deg"), 1)
                    act.activation(dinv[:, :], dinv[:, :], ACT.Sqrt, bias=ones[:, 0:1]).then_inc(S("rootdeg"), 1)
                    with act.Fori(0, NCH) as c:
                        roots(act, CB, S, c + 1)

                @block.sync
                def _(sp):
                    with sp.Fori(0, NCH) as c:
                        sp.wait_ge(S("scaled"), c + 1)
                        sp.dma_start(table_rows(2, c), chunk(AB, c, slice(D, 2 * D))).then_inc(S("stored"), 16)
                    sp.wait_ge(S("stored"), 16 * NCH)

        def plain_edge_loops(S, l, before_pe, before_act, before_dve):
            with nc.Block() as block:
                @block.gpsimd
                def _(pool):
                    gather_all(pool, l, S, D, S("summed"), False)

                @block.tensor
                def _(pe):
                    before_pe(pe)
                    with pe.Fori(0, ITERS) as i:
                        for q in range(RB):
                            t0, m = i * RT + q * BT, (q % 2) * BT
                            pe.wait_ge(S(f"landed{q}"), (i + 1) * 16 * BT)
                            for k in range(BT):
                                pe.wait_ge(S("hot"), t0 + k + 1)
                                sum_tile(pe, S, t0 + k, m + k, rows[:, q * BT + k, 0:D], D)

                @block.scalar
                def _(act):
                    before_act(act)
                    with act.Fori(0, ITERS) as i:
                        for q in range(RB):
                            act.wait_ge(S(f"landed{q}"), (i + 1) * 16 * BT)
                            stage_indices(act, S, i, q)

                @block.vector
                def _(dve):
                    before_dve(dve)
                    dve.sem_inc(S("added"), 2)
                    for k in range(BT):
                        mark_nodes(dve, S, k, k)
                    with dve.Fori(0, ITERS) as i:
                        for q in range(RB):
                            t0, m = i * RT + q * BT, (q % 2) * BT
                            blks = first_blocks(dve, t0, BT)
                            for k in range(BT):
                                mark_nodes(dve, S, t0 + BT + k, (BT - m) + k)
                                add_sums(dve, S, t0 + k, m + k, blks[k], D)

        def edges2():
            def S(name):
                return sem("e2", name)

            def mix_pe(pe):
                pe.wait_ge(S("gram_sb"), 2)
                for b, k in enumerate("qkv"):
                    t = pe.matmul(bank[0][:, b * P:(b + 1) * P], W["gram"][:, :], W[k][:, :], start=True, stop=True)
                t.then_inc(S("gw"), 1)
                pe.matmul(bank[1][:, 0:1], W["KQ"][:, :], sx[:, :], start=True, stop=True).then_inc(S("u"), 1)
                pe.wait_ge(S("squares"), 2)
                pe.matmul(bank[2][:, 0:2], ones[:, :], scal[:, 0:2], start=True, stop=True).then_inc(S("norms"), 1)
                pe.wait_ge(S("gv"), 1)
                pe.matmul(bank[3][:, 0:P], W["KQ"][:, :], W["gv"][:, :], start=True, stop=True).then_inc(S("kv"), 1)
                pe.wait_ge(S("attn"), 1)
                pe.transpose(bank[4][:, 0:P], W["t"][:, :], ident[:, :]).then_inc(S("attnT"), 1)
                pe.wait_ge(S("attnT_sb"), 1)
                pe.matmul(bank[5][:, 0:P], W["gv"][:, :], W["linT"][:, :], start=True, stop=True).then_inc(S("wx"), 1)
                pe.wait_ge(S("wX"), 3)
                pe.sem_inc(S("turned"), 1)
                with pe.Fori(0, NCH) as c:
                    pe.wait_ge(S("res"), c + 1)
                    pe.transpose(bank[0][:, 0:P], res[:, 0, :], ident[:, :]).then_inc(S("turned"), 1)
                    for j in range(CB):
                        if j + 1 < CB:
                            pe.transpose(bank[(j + 1) % 2][:, 0:P], res[:, j + 1, :], ident[:, :]).then_inc(S("turned"), 1)
                        pe.wait_ge(S("xT"), c * CB + j + 1)
                        pe.wait_ge(S("out_free"), c * CB + j + (2 if j == 0 else 1))
                        pe.matmul(bank[2 + j % 2][:, 0:2 * D + 1], xT[:, j % 2, :], wX[:, 0:2 * D + 1],
                                  start=True, stop=True).then_inc(S("out"), 1)

            def mix_act(act):
                act.activation(W["gram"][:, :], bank[6][:, 0:P], ACT.Copy).then_inc(S("gram_sb"), 1)
                act.activation(sx[:, :], bank[7][:, 0:1], ACT.Copy).then_inc(S("gram_sb"), 1)
                act.activation(wX[:, D:2 * D], W["linT"][:, :], ACT.Copy, scale=(1 - BETA) * (1 - ALPHA)).then_inc(S("wX"), 1)
                act.wait_ge(S("squares"), 2)
                act.activation(W["gv"][:, :], bank[0][:, 2 * P:3 * P], ACT.Copy).then_inc(S("gv"), 1)
                act.wait_ge(S("norms"), 1)
                act.activation(scal[:, 2:4], bank[2][:, 0:2], ACT.Sqrt).then_inc(S("roots"), 1)
                act.wait_ge(S("attnT"), 1)
                act.activation(W["gv"][:, :], bank[4][:, 0:P], ACT.Copy).then_inc(S("attnT_sb"), 1)
                act.wait_ge(S("wx"), 1)
                act.activation(wX[:, 0:D], bank[5][:, 0:P], ACT.Copy, scale=BETA * (1 - ALPHA)).then_inc(S("wX"), 1)
                with act.Fori(0, NCH) as c:
                    act.wait_ge(S("turned"), c * CB + 1)
                    act.activation(res[:, :, :], chunk(X, c), ACT.Copy).then_inc(S("res"), 1)

                    def linear_part(j):
                        act.wait_ge(S("out"), c * CB + j + 1)
                        act.activation(AB[:, bass.ds(c * CB + j, 1), 0:D], bank[2 + j % 2][:, D:2 * D].unsqueeze(1),
                                       ACT.Copy).then_inc(S("lin"), 1)

                    for j in range(CB):
                        act.wait_ge(S("turned"), c * CB + j + 2)
                        act.activation(xT[:, j % 2, :], bank[j % 2][:, 0:P], ACT.Copy).then_inc(S("xT"), 1)
                        if j:
                            linear_part(j - 1)
                    linear_part(CB - 1)

            def mix_dve(dve):
                seq = Chain(dve, S("dve"))
                dve.wait_ge(S("gw"), 1)
                for b, k in enumerate("qk"):
                    dve.scalar_tensor_tensor(tmp[:, b, :], bank[0][:, b * P:(b + 1) * P], 1.0, W[k][:, :], op0=ALU.mult,
                                             op1=ALU.mult, accum_out=scal[:, b:b + 1]).then_inc(S("squares"), 1)
                dve.wait_ge(S("roots"), 1)
                seq.link(dve.scalar_tensor_tensor(scal[:, 4:5], scal[:, 2:3], float(D), scal[:, 3:4], op0=ALU.mult, op1=ALU.mult))
                seq.link(dve.reciprocal(scal[:, 5:6], scal[:, 4:5]))
                dve.wait_ge(S("u"), 1)
                seq.mark(dve.tensor_scalar(wX[:, 2 * D:2 * D + 1], bank[1][:, 0:1], scal[:, 5:6], None, op0=ALU.mult))
                dve.wait_ge(S("kv"), 1)
                seq.link(dve.scalar_tensor_tensor(W["t"][:, :], bank[3][:, 0:P], scal[:, 5:6], W["v"][:, :],
                                                  op0=ALU.mult, op1=ALU.add))
                dve.sem_inc(S("attn"), 1)
                dve.sem_inc(S("wX"), 1)
                dve.sem_inc(S("out_free"), 2)
                with dve.Fori(0, NCH) as c:
                    seq.enter(c, 2 * CB)
                    for j in range(CB):
                        dve.wait_ge(S("lin"), c * CB + j + 1)
                        seq.link(dve.tensor_scalar(scal[:, 6:7], bank[2 + j % 2][:, 2 * D:2 * D + 1], 1.0, None, op0=ALU.add))
                        seq.link(dve.reciprocal(scal[:, 7:8], scal[:, 6:7]))
                        to = AB[:, bass.ds(c * CB + j, 1), 0:D]
                        dve.scalar_tensor_tensor(to, bank[2 + j % 2][:, 0:D].unsqueeze(1), scal[:, 7:8], to, op0=ALU.mult,
                                                 op1=ALU.add).then_inc(S("out_free"), 1)
                    seq.leave(NCH)

            plain_edge_loops(S, 2, mix_pe, mix_act, mix_dve)

        def nodes2():
            def S(name):
                return sem("n2", name)

            with nc.Block() as block:
                @block.vector
                def _(dve):
                    seq = Chain(dve, S("dve"))
                    dve.sem_inc(S("out_free"), 2)
                    with dve.Fori(0, NCH) as c:
                        seq.enter(c, 4 + NORM)
                        scale = dinv[:, bass.ds(c * CB, CB)].unsqueeze(2).broadcast_to([P, CB, D])
                        dve.wait_ge(S("kept"), c + 1)
                        seq.link(dve.tensor_tensor(res[:, :, :], chunk(sums, c, slice(0, D)), chunk(AB, c, slice(D, 2 * D)), ALU.add))
                        dve.sem_inc(S("sums_used"), 1)
                        seq.link(dve.tensor_tensor(res[:, :, :], res[:, :, :], scale, ALU.mult))
                        dve.sem_inc(S("gcn_in"), 1)
                        seq.mark(dve.tensor_tensor(tmp[:, :, :], chunk(X, c), chunk(AB, c, slice(0, D)), ALU.add))
                        for j in range(CB):
                            dve.wait_ge(S("out"), c * CB + j + 1)
                            if j == 0:
                                seq.wait()
                            dve.tensor_tensor(tmp[:, j, :], tmp[:, j, :], bank[2 + j % 2][:, 0:D], ALU.add).then_inc(S("out_free"), 1)
                        dve.wait_ge(S("out_free"), 2 + (c + 1) * CB)
                        seq.link(dve.tensor_tensor(tmp[:, :, :], tmp[:, :, :], row["blin"][:, :].unsqueeze(1).broadcast_to([P, CB, D]), ALU.add))
                        normalise(dve, seq, CB, S, c + 1, valid[:, bass.ds(c * CB, CB)])
                        dve.sem_inc(S("res"), 1)
                        seq.leave(NCH)

                @block.gpsimd
                def _(pool):
                    pool.sem_inc(S("kept"), 1)
                    with pool.Fori(0, NCH) as c:
                        pool.wait_ge(S("sums_used"), c + 1)
                        pool.tensor_copy(chunk(sums, c), zeros(CB, WS)).then_inc(S("cleared"), 1)
                        pool.wait_ge(S("res"), c + 1)
                        pool.tensor_copy(chunk(X, c), res[:, :, :]).then_inc(S("kept"), 1)
                    pool.wait_ge(S("kept"), NCH + 1)
                    pool.wait_ge(S("cleared"), NCH)

                @block.tensor
                def _(pe):
                    pe.sem_inc(S("turned"), 1)
                    with pe.Fori(0, NCH) as c:
                        pe.wait_ge(S("gcn_in"), c + 1)
                        pe.transpose(bank[0][:, 0:P], res[:, 0, :], ident[:, :]).then_inc(S("turned"), 1)
                        for j in range(CB):
                            if j + 1 < CB:
                                pe.transpose(bank[(j + 1) % 2][:, 0:P], res[:, j + 1, :], ident[:, :]).then_inc(S("turned"), 1)
                            pe.wait_ge(S("xT"), c * CB + j + 1)
                            pe.wait_ge(S("out_free"), c * CB + j + (2 if j == 0 else 1))
                            pe.matmul(bank[2 + j % 2][:, 0:D], xT[:, j % 2, :], wG[:, :], start=True, stop=True).then_inc(S("out"), 1)

                @block.scalar
                def _(act):
                    with act.Fori(0, NCH) as c:
                        for j in range(CB):
                            act.wait_ge(S("turned"), c * CB + j + 2)
                            act.activation(xT[:, j % 2, :], bank[j % 2][:, 0:P], ACT.Copy).then_inc(S("xT"), 1)
                        roots(act, CB, S, c + 1)

                @block.sync
                def _(sp):
                    with sp.Fori(0, NCH) as c:
                        sp.wait_ge(S("kept"), c + 2)
                        sp.dma_start(table_rows(3, c), chunk(X, c)).then_inc(S("stored"), 16)
                    sp.wait_ge(S("stored"), 16 * NCH)

        def edges3():
            def nothing(eng):
                pass

            plain_edge_loops(lambda name: sem("e3", name), 3, nothing, nothing, nothing)

        def nodes3():
            def S(name):
                return sem("n3", name)

            def products(eng, step):
                with eng.Fori(0, NFM // 2) as g:
                    step(g * 2, FM, 0)
                    step(g * 2 + 1, FM, 1)
                step(NFM, FREST, 0)

            relu = [diff[:, b, :, :] for b in range(2)]

            with nc.Block() as block:
                @block.vector
                def _(dve):
                    seq = Chain(dve, S("dve"))

                    def batch_stats(layer):
                        def step(m, width, b):
                            dve.wait_ge(S("y" + layer), 2 + m + 1)
                            dve.bn_stats(bnst[:, bass.ds(m, 1), :].rearrange("p o c -> p (o c)"),
                                         HT[1][:, bass.ds(m * FM, width)]).then_inc(S("st" + layer), 1)
                        products(dve, step)
                        dve.wait_ge(S("st" + layer), NFM + 1)
                        dve.bn_aggr(bnmv[:, 0:2], bnst[:, :, :]).then_inc(S("bnvar" + layer), 1)
                        dve.wait_ge(S("bnroot" + layer), 1)
                        seq.link(dve.reciprocal(bnmv[:, 3:4], bnmv[:, 2:3]))
                        seq.link(dve.tensor_tensor(bnmv[:, 4:5], bnmv[:, 3:4], col["g" + layer][:, :], ALU.mult))
                        seq.link(dve.tensor_tensor(bnmv[:, 6:7], bnmv[:, 0:1], bnmv[:, 4:5], ALU.mult))
                        dve.tensor_tensor(bnmv[:, 5:6], col["be" + layer][:, :], bnmv[:, 6:7], ALU.subtract).then_inc(S("bn" + layer), 1)

                    seq.link(dve.tensor_scalar(col["eps"][:, :], col["eps"][:, :], 1.0, None, op0=ALU.add))
                    with dve.Fori(0, NCH) as c:
                        dve.wait_ge(S("turned"), c * CB + 1)
                        dve.scalar_tensor_tensor(res[:, :, :], chunk(X, c), col["eps"][:, :], chunk(sums, c, slice(0, D)),
                                                 op0=ALU.mult, op1=ALU.add).then_inc(S("h"), 1)
                    batch_stats("1")
                    batch_stats("2")

                    def last(m, nb, b):
                        to = X[:, bass.ds(m * 4, nb), :]
                        dve.wait_ge(S("back"), m + 3)
                        seq.link(dve.tensor_tensor(tmp[:, 0:nb, :], to, bank[b][:, 0:nb * P].rearrange("p (k f) -> p k f", k=nb), ALU.add))
                        normalise(dve, seq, nb, S, m + 1, valid[:, bass.ds(m * 4, nb)],
                                  lambda j: X[:, bass.ds(m * 4 + j, 1), :].rearrange("p o c -> p (o c)"))
                        dve.sem_inc(S("done"), 1)

                    with dve.Fori(0, NFM // 2) as g:
                        seq.enter(g, 2 * (1 + 3 * 4 + 1))
                        last(g * 2, 4, 0)
                        last(g * 2 + 1, 4, 1)
                        seq.leave(NFM // 2)
                    last(NFM, 1, 0)

                @block.tensor
                def _(pe):
                    pe.sem_inc(S("turned"), 1)
                    with pe.Fori(0, NCH) as c:
                        pe.wait_ge(S("h"), c + 1)
                        for j in range(CB):
                            pe.wait_ge(S("hT"), c * CB + j + 1)
                            pe.transpose(bank[j % 2][:, 0:P], res[:, j, :], ident[:, :]).then_inc(S("turned"), 1)
                            if j == CB - 1:
                                pe.wait_ge(S("hT"), (c + 1) * CB + 2)

                    def product(layer, w):
                        def step(m, width, b):
                            if layer == "2":
                                pe.wait_ge(S("relu1"), m + 1)
                            pe.wait_ge(S("y" + layer), m + 1)
                            pe.matmul(bank[2 + b][:, 0:width], w[:, :], HT[0][:, bass.ds(m * FM, width)],
                                      start=True, stop=True).then_inc(S("p" + layer), 1)
                        products(pe, step)

                    pe.sem_inc(S("back"), 2)
                    pe.wait_ge(S("hT"), 2 + NB)
                    product("1", W["w1T"])
                    product("2", W["w2T"])

                    def back(m, width, b):
                        pe.wait_ge(S("relu2"), m + 1)
                        pe.wait_ge(S("done"), m + 1)
                        for k in range(-(-width // P)):
                            t = pe.transpose(bank[b][:, k * P:(k + 1) * P], relu[b][:, k, :], ident[:, :])
                        t.then_inc(S("back"), 1)
                    products(pe, back)

                @block.gpsimd
                def _(pool):
                    pool.sem_inc(S("done"), 2)

                @block.scalar
                def _(act):
                    act.sem_inc(S("hT"), 2)
                    act.sem_inc(S("y1"), 2)
                    act.sem_inc(S("y2"), 2)
                    with act.Fori(0, NCH) as c:
                        for j in range(CB):
                            act.wait_ge(S("turned"), c * CB + j + 2)
                            act.activation(HT[0][:, bass.ds((c * CB + j) * P, P)], bank[j % 2][:, 0:P], ACT.Copy).then_inc(S("hT"), 1)

                    def product(layer):
                        def step(m, width, b):
                            act.wait_ge(S("p" + layer), m + 1)
                            act.activation(HT[1][:, bass.ds(m * FM, width)], bank[2 + b][:, 0:width], ACT.Identity,
                                           bias=col["lb" + layer][:, :]).then_inc(S("y" + layer), 1)
                        products(act, step)
                        act.wait_ge(S("bnvar" + layer), 1)
                        act.activation(bnmv[:, 2:3], bnmv[:, 1:2], ACT.Sqrt, bias=eps_ln[:, :]).then_inc(S("bnroot" + layer), 1)
                        act.wait_ge(S("bn" + layer), 1)

                    product("1")

                    def relu1(m, width, b):
                        act.activation(HT[0][:, bass.ds(m * FM, width)], HT[1][:, bass.ds(m * FM, width)], ACT.Relu,
                                       bias=bnmv[:, 5:6], scale=bnmv[:, 4:5]).then_inc(S("relu1"), 1)
                    products(act, relu1)
                    act.wait_ge(S("relu1"), NFM + 1)
                    product("2")

                    def relu2(m, width, b):
                        act.wait_ge(S("back"), m + 1)
                        act.activation(relu[b].rearrange("p k f -> p (k f)")[:, 0:width], HT[1][:, bass.ds(m * FM, width)], ACT.Relu,
                                       bias=bnmv[:, 5:6], scale=bnmv[:, 4:5]).then_inc(S("relu2"), 1)
                        roots(act, -(-width // P), S, m + 1)
                    products(act, relu2)

                @block.sync
                def _(sp):
                    with sp.Fori(0, NFM) as m:
                        sp.wait_ge(S("done"), m + 3)
                        sp.dma_start(out[0:NFM * FM].rearrange("(b p) c -> p b c", p=P)[:, bass.ds(m * 4, 4), :],
                                     X[:, bass.ds(m * 4, 4), :]).then_inc(S("wrote"), 16)
                    sp.wait_ge(S("done"), NFM + 3)
                    sp.dma_start(out[NFM * FM:N], X[0:FREST, NB - 1, :]).then_inc(S("wrote"), 16)
                    sp.wait_ge(S("wrote"), 16 * (NFM + 1))

        prepare()
        project()
        edges0()
        nodes0()
        edges1()
        nodes1()
        clear_semaphores()
        edges2()
        nodes2()
        edges3()
        nodes3()


INPUTS = ['x', 'src', 'dst', 'L0_gnn_W', 'L0_gnn_att_src', 'L0_gnn_att_dst', 'L0_gnn_bias', 'L1_gnn_W1', 'L1_gnn_b1',
          'L1_gnn_W2', 'L1_gnn_b2', 'L1_gnn_W4', 'L1_gnn_b4', 'L2_gnn_Wq', 'L2_gnn_Wk', 'L2_gnn_Wv', 'L2_gnn_W_gcn',
          'L2_gnn_b_gcn', 'L2_gnn_W_lin', 'L2_gnn_b_lin', 'L3_gnn_eps', 'L3_gnn_W1', 'L3_gnn_b1', 'L3_gnn_g1',
          'L3_gnn_be1', 'L3_gnn_W2', 'L3_gnn_b2', 'L3_gnn_g2', 'L3_gnn_be2']


def kernel(**inputs):
    import concourse.bacc as bacc
    from concourse.bass_utils import run_bass_kernel_spmd

    nc = bacc.Bacc("TRN2", target_bir_lowering=False, num_devices=1)
    arrays, args = {}, {}
    for name in INPUTS:
        v = np.ascontiguousarray(inputs[name])
        v = v.reshape(v.shape or (1,))
        arrays["in_" + name] = v
        args[name] = nc.dram_tensor("in_" + name, v.shape, mybir.dt.from_np(v.dtype), kind="ExternalInput").ap()
    out = nc.dram_tensor("out_x", (N, D), F32, kind="ExternalOutput").ap()
    tables = [nc.dram_tensor(f"table{l}", (NB * P, w), F32).ap() for l, w in enumerate((WS, 2 * D, D, D))]
    gnn(nc, args, out, tables)
    return run_bass_kernel_spmd(nc, [arrays], core_ids=[0]).results[0]["out_x"]
```

```python
import numpy as np
from contextlib import ExitStack

import concourse.bass as bass
from concourse import mybir

P = 128
N = 6250
E = 106250
D = 128
H = 4
HC = D // H
NB = -(-N // P)
LAST = N - (NB - 1) * P
CB = 7
NCH = NB // CB
TILES = -(-E // P)
BT = 4
RB = 4
RT = RB * BT
ITERS = -(-TILES // RT)
IC = -(-(ITERS + 1) * RT // P)
TPAD = IC * P
FULL = E // P
REST = E - FULL * P
SLOPE = 0.2
ALPHA, BETA = 0.6, 0.4
LN_EPS = 1e-5
BN_EPS = 1e-5
RANGE = 60.0
FAR = 30000
WS = D + H + 1
WAB = 2 * D
FM = 512
NFM = N // FM
FREST = N - NFM * FM
F32 = mybir.dt.float32
BF16 = mybir.dt.bfloat16
I32 = mybir.dt.int32
ALU = mybir.AluOpType
ACT = mybir.ActivationFunctionType
AX = mybir.AxisListType


class Chain:

    def __init__(self, eng, sem):
        self.eng, self.sem, self.n, self.i, self.per = eng, sem, 0, None, 0

    def enter(self, i, per):
        self.i, self.per, self.start = i, per, self.n

    def leave(self, count):
        assert self.n - self.start == self.per, (self.n - self.start, self.per)
        self.n, self.i = self.start + self.per * count, None

    def mark(self, ins):
        ins.then_inc(self.sem, 1)
        self.n += 1

    def wait(self):
        self.eng.wait_ge(self.sem, self.n if self.i is None else self.i * self.per + self.n)

    def link(self, ins):
        self.mark(ins)
        self.wait()


def gnn(nc, a, out, table, rel):
    ctx = ExitStack()
    with ctx:
        def sb(name, shape, dt=F32):
            return ctx.enter_context(nc.sbuf_tensor(name, shape, dt))

        def sem(name):
            return ctx.enter_context(nc.semaphore(name))

        X = sb("X", [P, NB, D])
        AB = sb("AB", [P, NB + 1, WAB])
        sums = sb("sums", [P, NB + 1, WS])
        selfw = sb("selfw", [P, NB, H])
        valid = sb("valid", [P, NB])
        dinv = sb("dinv", [P, NB])
        ABf = AB[:, :, :].rearrange("p b c -> p (b c)")
        HT = [ABf[:, 0:NB * P], ABf[:, NB * P:2 * NB * P]]
        srcI = sb("srcI", [P, TPAD], I32)
        relF = sb("relF", [P, TPAD])
        blk = sb("blk", [1, BT + TPAD], I32)
        relB = sb("relB", [P, RB, BT * P], BF16)
        idx = sb("idx", [P, RT], I32)
        onehot = sb("onehot", [P, 2 * BT, 2 * P])
        onehotT = sb("onehotT", [P, 2, 2, BT * P])
        dist = sb("dist", [P, 2, 2 * P])
        rows = sb("rows", [P, RT, 2 * D + 1])
        msg = sb("msg", [P, 2 * BT, WS])
        diff = sb("diff", [P, 2, BT, D])
        minus = sb("minus", [P, BT])
        score = sb("score", [P, 2, BT, H])
        logit = sb("logit", [P, 2, BT])
        ident = sb("ident", [P, P])
        ones = sb("ones", [P, P])
        iota = sb("iota", [P, 2 * P])
        node = sb("node", [P, 2])
        degree = sb("degree", [P, NB])
        relb = sb("relb", [P, IC, P], BF16)
        hmask = sb("hmask", [P, H])
        eps_ln = sb("eps_ln", [P, 1])
        wA = sb("wA", [P, D + 2 * H])
        wB = sb("wB", [P, 2 * D])
        wX = sb("wX", [P, 2 * D + 2])
        wG = sb("wG", [P, P])
        W = {k: sb(f"w_{k}", [P, P]) for k in
             ("q", "k", "v", "gcn", "lin", "w1", "w2", "qT", "kT", "linT", "KQ", "w1T", "w2T", "gram", "gv", "t")}
        row = {k: sb(f"row_{k}", [P, D]) for k in ("bias", "b1", "w2", "b4", "blin")}
        col = {k: sb(f"col_{k}", [P, 1]) for k in
               ("as", "ad", "b2", "bg", "eps", "lb1", "g1", "be1", "lb2", "g2", "be2")}
        att = sb("att", [P, 2 * H])
        tmp = sb("tmp", [P, CB, D])
        res = sb("res", [P, CB, D])
        relv = sb("relv", [P, IC, P])
        xT = sb("xT", [P, 2, P])
        stats = sb("stats", [P, CB, 6])
        mv = sb("mv", [P, CB, 2])
        rstd = sb("rstd", [P, CB])
        firsti = sb("firsti", [P, IC], I32)
        firstf = sb("firstf", [P, IC])
        den = sb("den", [P, CB, H])[:, :, :]
        top = sb("top", [P, 3 * H])
        bound = sb("bound", [P, NB, H])
        own = sb("own", [P, NB, H])
        scal = sb("scal", [P, 12])
        sx = sb("sx", [P, 1])
        bnst = sb("bnst", [P, NFM + 1, 6])
        bnmv = sb("bnmv", [P, 8])

        bank = [ctx.enter_context(nc.psum_tensor(f"bank{i}", [P, 512], F32)) for i in range(8)]

        semaphores = {}

        def sem(phase, name):
            key = f"{phase}_{name}"
            if key not in semaphores:
                semaphores[key] = nc.alloc_semaphore(key)
            return semaphores[key]

        def clear_semaphores():
            nc.clear_and_free_semaphores(list(semaphores.values()))
            semaphores.clear()
            nc.all_engine_barrier()

        def chunk(t, c, of=slice(None)):
            return t[:, bass.ds(c * CB, CB), of]

        def table_rows(l, c):
            return table[l].rearrange("(b p) c -> p b c", p=P)[:, bass.ds(c * CB, CB), :]

        def first_blocks(eng, tile, count):
            return nc.values_load_multi_w_load_instructions(
                blk[0:1, bass.ds(tile, count)], engines=[eng.engine], min_val=0, max_val=NB - 1,
                skip_runtime_bounds_check_because="every dst is below N")[1]

        def zeros(k, width):
            return iota[:, 0:1].unsqueeze(2).broadcast_to([P, k, width])

        def pass_gate(eng, S):
            eng.sem_inc(S("gate" + str(eng.engine)[-4:]), 1)

        def normalise(dve, seq, nb, S, k, mask, to=lambda j: res[:, j, :]):
            for j in range(nb):
                seq.mark(dve.bn_stats(stats[:, j, :], tmp[:, j, :]))
            seq.wait()
            pass_gate(dve, S)
            for j in range(nb - 1):
                seq.mark(dve.bn_aggr(mv[:, j, :], stats[:, j, :]))
            seq.wait()
            pass_gate(dve, S)
            dve.bn_aggr(mv[:, nb - 1, :], stats[:, nb - 1, :]).then_inc(S("var"), 1)
            dve.wait_ge(S("root"), k)
            seq.link(dve.reciprocal(rstd[:, 0:nb], rstd[:, 0:nb]))
            seq.link(dve.tensor_tensor(rstd[:, 0:nb], rstd[:, 0:nb], mask, ALU.mult))
            for j in range(nb):
                seq.mark(dve.tensor_scalar(to(j), tmp[:, j, :], mv[:, j, 0:1], rstd[:, j:j + 1],
                                           op0=ALU.subtract, op1=ALU.mult))
            seq.wait()

        def roots(act, nb, S, k):
            act.wait_ge(S("var"), k)
            act.activation(rstd[:, 0:nb], mv[:, 0:nb, 1], ACT.Sqrt, bias=eps_ln[:, :]).then_inc(S("root"), 1)

        NORM = 3 * CB + 1

        def prepare():
            def S(name):
                return sem("prep", name)

            dst_t = tmp[:, :, :].bitcast(I32)
            src_t = res[:, :, :].bitcast(I32)
            src_f = AB[:, 0:IC, 0:P]
            to_turn = [relv[:, c, :] for c in range(IC)] + [src_f[:, c, :] for c in range(IC)]
            loads = [(wA[:, 0:D], a["L0_gnn_W"]),
                     (col["as"][:, :], a["L0_gnn_att_src"].rearrange("h (c o) -> (h c) o", o=1)),
                     (col["ad"][:, :], a["L0_gnn_att_dst"].rearrange("h (c o) -> (h c) o", o=1)),
                     (wB[:, 0:D], a["L1_gnn_W1"]), (wB[:, D:2 * D], a["L1_gnn_W4"]),
                     (col["b2"][:, :], a["L1_gnn_b2"].partition_broadcast(P)),
                     (row["w2"][:, :], a["L1_gnn_W2"].rearrange("k o -> (k o)").partition_broadcast(P)),
                     (W["q"][:, :], a["L2_gnn_Wq"]), (W["k"][:, :], a["L2_gnn_Wk"]), (W["v"][:, :], a["L2_gnn_Wv"]),
                     (W["gcn"][:, :], a["L2_gnn_W_gcn"]), (W["lin"][:, :], a["L2_gnn_W_lin"]),
                     (W["w1"][:, :], a["L3_gnn_W1"]), (W["w2"][:, :], a["L3_gnn_W2"]),
                     (col["eps"][:, :], a["L3_gnn_eps"].partition_broadcast(P))]
            loads += [(row[r][:, :], a[name].partition_broadcast(P)) for r, name in
                      (("bias", "L0_gnn_bias"), ("b1", "L1_gnn_b1"), ("b4", "L1_gnn_b4"), ("blin", "L2_gnn_b_lin"))]
            loads += [(col[c][:, :], a[name].rearrange("(p o) -> p o", o=1)) for c, name in
                      (("bg", "L2_gnn_b_gcn"), ("lb1", "L3_gnn_b1"), ("g1", "L3_gnn_g1"), ("be1", "L3_gnn_be1"),
                       ("lb2", "L3_gnn_b2"), ("g2", "L3_gnn_g2"), ("be2", "L3_gnn_be2"))]

            with nc.Block() as block:
                @block.sync
                def _(sp):
                    sp.wait_ge(S("filled"), 1)
                    t0 = (IC - 1) * P
                    for v, name in ((dst_t, "dst"), (src_t, "src")):
                        e = a[name]
                        sp.dma_start(v[:, 0:IC - 1, :], e[0:t0 * P].rearrange("(c p e) -> p c e", p=P, e=P)).then_inc(S("idx"), 16)
                        sp.dma_start(v[0:FULL - t0, IC - 1, :], e[t0 * P:FULL * P].rearrange("(p e) -> p e", e=P)).then_inc(S("idx"), 16)
                        sp.dma_start(v[FULL - t0:FULL - t0 + 1, IC - 1, 0:REST],
                                     e[FULL * P:E].rearrange("(p e) -> p e", p=1)).then_inc(S("idx"), 16)
                    sp.dma_start(blk[0:1, BT:BT + FULL], a["dst"][0:FULL * P].rearrange("(t e) -> e t", e=P)[0:1, :],
                                 allow_slow_non_contiguous=True).then_inc(S("first"), 16)
                    sp.dma_start(blk[0:1, BT + FULL:BT + FULL + 1],
                                 a["dst"][FULL * P:FULL * P + 1].rearrange("(p e) -> p e", p=1)).then_inc(S("first"), 16)
                    sp.dma_start(X[:, 0:NB - 1, :], a["x"][0:(NB - 1) * P].rearrange("(b p) c -> p b c", p=P)).then_inc(S("x"), 16)
                    sp.dma_start(X[0:LAST, NB - 1, :], a["x"][(NB - 1) * P:N]).then_inc(S("x"), 16)
                    sp.wait_ge(S("relb"), 1)
                    sp.dma_start(rel.rearrange("(c p e) -> p c e", p=P, e=P), relb[:, :, :]).then_inc(S("x"), 16)
                    sp.wait_ge(S("x"), 48)

                @block.gpsimd
                def _(pool):
                    seq = Chain(pool, S("pool"))
                    seq.mark(pool.memset(dst_t[:, IC - 1, :], FAR))
                    seq.mark(pool.memset(src_t[:, IC - 1, :], 0))
                    seq.mark(pool.memset(blk[:, :], 0))
                    seq.link(pool.memset(X[:, NB - 1, :], 0.0))
                    pool.sem_inc(S("filled"), 1)
                    seq.mark(pool.memset(ident[:, :], 0.0))
                    seq.mark(pool.memset(hmask[:, :], 1.0))
                    seq.mark(pool.memset(valid[:, :], 1.0))
                    seq.mark(pool.memset(ones[:, :], 1.0))
                    seq.mark(pool.memset(eps_ln[:, :], LN_EPS))
                    seq.mark(pool.iota(node[:, :], pattern=[[P, 2]], base=0, channel_multiplier=1,
                                       allow_small_or_imprecise_dtypes=True))
                    seq.link(pool.iota(iota[:, :], pattern=[[1, 2 * P]], base=0, channel_multiplier=0,
                                       allow_small_or_imprecise_dtypes=True))
                    seq.mark(pool.affine_select(out=ident[:, :], in_=ident[:, :], compare_op=ALU.not_equal, fill=1.0,
                                                base=0, pattern=[[-1, P]], channel_multiplier=1))
                    seq.mark(pool.affine_select(out=valid[:, NB - 1:NB], in_=valid[:, NB - 1:NB], compare_op=ALU.is_ge,
                                                fill=0.0, base=LAST - 1, pattern=[[0, 1]], channel_multiplier=-1))
                    seq.link(pool.affine_select(out=hmask[:, :], in_=hmask[:, :], compare_op=ALU.is_ge, fill=0.0,
                                                base=0, pattern=[[-HC, H]], channel_multiplier=1))
                    seq.link(pool.affine_select(out=hmask[:, :], in_=hmask[:, :], compare_op=ALU.is_ge, fill=0.0,
                                                base=HC - 1, pattern=[[HC, H]], channel_multiplier=-1))
                    pool.sem_inc(S("consts"), 1)
                    seq.mark(pool.memset(sums[:, :, :], 0.0))
                    seq.mark(pool.memset(AB[:, NB, :], 0.0))
                    seq.mark(pool.memset(rows[:, :, 2 * D:2 * D + 1], 1.0))
                    seq.link(pool.memset(msg[:, :, WS - 1:WS], 1.0))

                @block.scalar
                def _(act):
                    for to, of in loads:
                        act.dma_start(to, of).then_inc(S("w"), 16)
                    act.wait_ge(S("w"), 16 * len(loads))
                    act.sem_inc(S("weights"), 1)
                    act.wait_ge(S("wt"), 1)
                    act.activation(W["t"][:, :], bank[4][:, 0:P], ACT.Copy).then_inc(S("wt_sb"), 1)
                    act.activation(W["qT"][:, :], bank[4][:, P:2 * P], ACT.Copy).then_inc(S("wt_sb"), 1)
                    act.activation(W["kT"][:, :], bank[4][:, 2 * P:3 * P], ACT.Copy).then_inc(S("wt_sb"), 1)
                    act.activation(W["linT"][:, :], bank[4][:, 3 * P:4 * P], ACT.Copy).then_inc(S("wt_sb"), 1)
                    act.activation(W["w1T"][:, :], bank[5][:, 0:P], ACT.Copy).then_inc(S("wt_sb"), 1)
                    act.activation(W["w2T"][:, :], bank[5][:, P:2 * P], ACT.Copy).then_inc(S("wt_sb"), 1)
                    act.wait_ge(S("wp"), 1)
                    act.activation(wA[:, D:D + 2 * H], bank[6][:, 0:2 * H], ACT.Copy).then_inc(S("act"), 1)
                    act.activation(W["KQ"][:, :], bank[6][:, P:2 * P], ACT.Copy).then_inc(S("act"), 1)
                    act.activation(wG[:, :], bank[6][:, 2 * P:3 * P], ACT.Copy, scale=ALPHA).then_inc(S("act"), 1)
                    act.wait_ge(S("act"), 3)

                @block.tensor
                def _(pe):
                    pe.wait_ge(S("consts"), 1)
                    pe.wait_ge(S("weights"), 1)
                    for b, w in enumerate((wA[:, 0:D], W["q"][:, :], W["k"][:, :], W["lin"][:, :])):
                        pe.transpose(bank[4][:, b * P:(b + 1) * P], w, ident[:, :])
                    pe.transpose(bank[5][:, 0:P], W["w1"][:, :], ident[:, :])
                    pe.transpose(bank[5][:, P:2 * P], W["w2"][:, :], ident[:, :]).then_inc(S("wt"), 1)
                    pe.wait_ge(S("tof"), 1)
                    for j, v in enumerate(to_turn):
                        pe.transpose(bank[j // 4][:, (j % 4) * P:(j % 4 + 1) * P], v, ident[:, :]).then_inc(S("turned"), 1)
                    pe.wait_ge(S("wt_sb"), 6)
                    pe.wait_ge(S("att"), 1)
                    pe.matmul(bank[6][:, 0:2 * H], W["t"][:, :], att[:, :], start=True, stop=True)
                    pe.matmul(bank[6][:, P:2 * P], W["kT"][:, :], W["qT"][:, :], start=True, stop=True)
                    pe.matmul(bank[6][:, 2 * P:3 * P], W["gcn"][:, :], W["linT"][:, :], start=True, stop=True).then_inc(S("wp"), 1)
                    pe.matmul(bank[7][:, 0:P], W["gram"][:, :], W["linT"][:, :], start=True, stop=True).then_inc(S("bl"), 1)

                @block.vector
                def _(dve):
                    seq = Chain(dve, S("dve"))
                    dve.wait_ge(S("idx"), 16 * 6)
                    seq.link(dve.tensor_scalar(firsti[:, :], dst_t[:, :, 0], N - 1, None, op0=ALU.min))
                    seq.link(dve.tensor_scalar(firsti[:, :], firsti[:, :], 7, 7, op0=ALU.logical_shift_right,
                                               op1=ALU.logical_shift_left))
                    seq.link(dve.tensor_copy(firstf[:, :], firsti[:, :]))
                    seq.mark(dve.tensor_copy(src_f, src_t))
                    seq.link(dve.tensor_tensor(relv[:, :, :], dst_t, firstf[:, :].unsqueeze(2).broadcast_to([P, IC, P]),
                                               ALU.subtract))
                    dve.sem_inc(S("tof"), 1)
                    dve.tensor_copy(relb[:, :, :], relv[:, :, :]).then_inc(S("relb"), 1)
                    dve.wait_ge(S("first"), 32)
                    seq.mark(dve.tensor_scalar(blk[:, :], blk[:, :], 7, None, op0=ALU.logical_shift_right))
                    dve.wait_ge(S("consts"), 1)
                    dve.wait_ge(S("weights"), 1)
                    seq.mark(dve.tensor_scalar(att[:, 0:H], hmask[:, :], col["as"][:, :], None, op0=ALU.mult))
                    seq.mark(dve.tensor_scalar(att[:, H:2 * H], hmask[:, :], col["ad"][:, :], None, op0=ALU.mult))
                    seq.link(dve.tensor_scalar(W["gram"][:, :], ones[:, :], col["bg"][:, :], None, op0=ALU.mult))
                    dve.sem_inc(S("att"), 1)
                    for j in range(2 * IC):
                        dve.wait_ge(S("turned"), min(4 * (j // 4) + 4, 2 * IC))
                        seq.mark(dve.tensor_copy((relF if j < IC else srcI)[:, (j % IC) * P:(j % IC + 1) * P],
                                                 bank[j // 4][:, (j % 4) * P:(j % 4 + 1) * P]))
                    dve.wait_ge(S("bl"), 1)
                    seq.link(dve.scalar_tensor_tensor(row["blin"][:, :], bank[7][:, 0:P], ALPHA, row["blin"][:, :],
                                                      op0=ALU.mult, op1=ALU.add))

        def project():
            def S(name):
                return sem("proj", name)

            with nc.Block() as block:
                @block.tensor
                def _(pe):
                    pe.sem_inc(S("turned"), 1)
                    with pe.Fori(0, NCH) as c:
                        pe.wait_ge(S("res"), c + 1)
                        pe.transpose(bank[0][:, 0:P], res[:, 0, :], ident[:, :]).then_inc(S("turned"), 1)
                        for j in range(CB):
                            if j + 1 < CB:
                                t = pe.transpose(bank[(j + 1) % 2][:, 0:P], res[:, j + 1, :], ident[:, :])
                                t.then_inc(S("turned"), 1)
                            pe.wait_ge(S("xT"), c * CB + j + 1)
                            pe.wait_ge(S("out_free"), c * CB + j + (2 if j == 0 else 1))
                            pe.matmul(bank[2 + j % 2][:, 0:D + 2 * H], xT[:, j % 2, :], wA[:, :],
                                      start=True, stop=True).then_inc(S("out"), 1)
                    pe.wait_ge(S("top"), 1)
                    pe.transpose(bank[4][0:H, 0:P], top[:, 0:H], ident[:, :]).then_inc(S("topT"), 1)
                    pe.wait_ge(S("diag"), 1)
                    pe.matmul(bank[5][:, 0:H], ones[0:H, :], top[0:H, 2 * H:3 * H], start=True, stop=True).then_inc(S("gmax"), 1)

                @block.scalar
                def _(act):
                    with act.Fori(0, NCH) as c:
                        act.wait_ge(S("turned"), c * CB + 1)
                        act.activation(res[:, :, :], chunk(X, c), ACT.Copy).then_inc(S("res"), 1)
                        for j in range(CB):
                            act.wait_ge(S("turned"), c * CB + j + 2)
                            act.activation(xT[:, j % 2, :], bank[j % 2][:, 0:P], ACT.Copy).then_inc(S("xT"), 1)
                    act.wait_ge(S("selfz"), 1)
                    act.activation(selfw[:, :, :], own[:, :, :], ACT.Exp).then_inc(S("selfw"), 1)
                    act.wait_ge(S("selfw"), 1)

                @block.vector
                def _(dve):
                    seq = Chain(dve, S("dve"))
                    dve.sem_inc(S("out_free"), 2)
                    with dve.Fori(0, NCH) as c:
                        for j in range(CB):
                            dve.wait_ge(S("out"), c * CB + j + 1)
                            dve.tensor_copy(AB[:, bass.ds(c * CB + j, 1), 0:D + 2 * H],
                                            bank[2 + j % 2][:, 0:D + 2 * H].unsqueeze(1)).then_inc(S("out_free"), 1)
                    dve.wait_ge(S("out_free"), 2 + NB)
                    a_s, a_d = AB[:, 0:NB, D:D + H], AB[:, 0:NB, D + H:D + 2 * H]
                    dve.tensor_reduce(top[:, 0:H], a_s.rearrange("p b h -> p h b"), axis=AX.X, op=ALU.max).then_inc(S("top"), 1)
                    dve.wait_ge(S("topT"), 1)
                    seq.link(dve.tensor_reduce(top[0:H, H:H + 1], bank[4][0:H, 0:P], axis=AX.X, op=ALU.max))
                    dve.tensor_scalar(top[0:H, 2 * H:3 * H], ident[0:H, 0:H], top[0:H, H:H + 1], None,
                                      op0=ALU.mult).then_inc(S("diag"), 1)
                    seq.link(dve.tensor_tensor(own[:, :, :], a_s, a_d, ALU.add))
                    seq.mark(dve.scalar_tensor_tensor(own[:, :, :], own[:, :, :], SLOPE, own[:, :, :],
                                                      op0=ALU.mult, op1=ALU.max))
                    dve.wait_ge(S("gmax"), 1)
                    seq.link(dve.tensor_tensor(bound[:, :, :], a_d, bank[5][:, 0:H].unsqueeze(1).broadcast_to([P, NB, H]), ALU.add))
                    seq.link(dve.scalar_tensor_tensor(bound[:, :, :], bound[:, :, :], SLOPE, bound[:, :, :],
                                                      op0=ALU.mult, op1=ALU.max))
                    seq.link(dve.scalar_tensor_tensor(AB[:, 0:NB, D + 2 * H:D + 3 * H], bound[:, :, :], -RANGE, own[:, :, :],
                                                      op0=ALU.add, op1=ALU.max))
                    seq.link(dve.tensor_tensor(own[:, :, :], own[:, :, :], AB[:, 0:NB, D + 2 * H:D + 3 * H], ALU.subtract))
                    dve.sem_inc(S("selfz"), 1)

                @block.sync
                def _(sp):
                    with sp.Fori(0, NCH) as c:
                        sp.wait_ge(S("out_free"), 2 + (c + 1) * CB)
                        sp.dma_start(table_rows(0, c), chunk(AB, c, slice(0, D + H))).then_inc(S("stored"), 16)
                    sp.wait_ge(S("stored"), 16 * NCH)

        def gather_all(pool, l, S, width, taken, before, extra):
            def gather(q, k, index):
                pool.indirect_dma_start(
                    out=rows[:, q * BT + k, 0:width], out_offset=None, in_=table[l],
                    in_offset=bass.IndirectOffsetOnAxis(ap=index, axis=0)).then_inc(S(f"landed{q}"), 16)

            for q in range(RB):
                for k in range(BT):
                    gather(q, k, srcI[:, q * BT + k:q * BT + k + 1])
            with pool.Fori(1, ITERS) as i:
                for q in range(RB):
                    pool.wait_ge(S("staged"), i * RB + q - (RB - 1))
                    pool.wait_ge(taken, i * RT + q * BT - (RT - BT) + before)
                    pass_gate(pool, S)
                    for k in range(BT):
                        gather(q, k, idx[:, q * BT + k:q * BT + k + 1])
            if extra:
                pool.wait_ge(S("staged"), ITERS * RB - (RB - 1))
                pool.wait_ge(taken, ITERS * RT - (RT - BT) + before)
                for k in range(BT):
                    gather(0, k, idx[:, k:k + 1])

        def stage_indices(act, S, i, q):
            act.activation(idx[:, q * BT:(q + 1) * BT], srcI[:, bass.ds(i * RT + (q + RB) * BT, BT)],
                           ACT.Copy).then_inc(S("staged"), 1)


        def mark_nodes(dve, S, tile, k):
            dve.tensor_scalar(onehot[:, k, :], iota[:, :], relF[:, bass.ds(tile, 1)], None,
                              op0=ALU.is_equal).then_inc(S("hot"), 1)

        def add_sums(dve, S, tile, k, block, width):
            dve.wait_ge(S("summed"), tile + 1)
            dve.wait_ge(S("added"), tile + 2)
            to = sums[:, bass.ds(block, 2), 0:width]
            dve.tensor_tensor(to, to, bank[4 + k % 2][:, 0:2 * width].rearrange("p (b c) -> p b c", b=2),
                              ALU.add).then_inc(S("added"), 1)

        def sum_tile(pe, S, tile, k, value, width):
            pe.wait_ge(S("added"), tile + 1)
            for b in range(2):
                m = pe.matmul(bank[4 + k % 2][:, b * width:(b + 1) * width], onehot[:, k, b * P:(b + 1) * P],
                              value, start=True, stop=True)
            m.then_inc(S("summed"), 1)


        def load_rel(sp, S):
            def load(s, q):
                sp.dma_start(relB[:, q, :], rel[bass.ds(s * BT * P, BT * P)].partition_broadcast(P)).then_inc(S(f"rel{q}"), 16)

            for q in range(RB):
                load(q, q)
            with sp.Fori(1, ITERS) as i:
                for q in range(RB):
                    sp.wait_ge(S("hotT"), i * RB + q - (RB - 1))
                    load(i * RB + q, q)
            for q in range(2):
                sp.wait_ge(S("hotT"), ITERS * RB + q - (RB - 1))
                load(ITERS * RB + q, q)

        def mark_edges(dve, S, s, q, rounds):
            dve.wait_ge(S(f"rel{q}"), rounds * 16)
            if not isinstance(s, int) or s > 1:
                dve.wait_ge(S("spread"), (s - 1) * BT)
            for b in range(2):
                t = dve.tensor_scalar(onehotT[:, q % 2, b, :], relB[:, q, :], node[:, b:b + 1], None, op0=ALU.is_equal)
            t.then_inc(S("hotT"), 1)

        def spread(pe, S, s, q, blocks, columns, width):
            pe.wait_ge(S("hotT"), s + 1)
            for k in range(BT):
                for b in range(2):
                    t = pe.matmul(bank[q % 2][:, k * width:(k + 1) * width], onehotT[:, q % 2, b, k * P:(k + 1) * P],
                                  AB[:, bass.ds(blocks[k] + b, 1), columns].rearrange("p o c -> p (o c)"),
                                  start=(b == 0), stop=(b == 1))
                t.then_inc(S("spread"), 1)

        def distance(act, S, t0, k):
            act.wait_ge(S("hot"), t0 + k + 1)
            act.activation(dist[:, k % 2, :], iota[:, :], ACT.Abs, scale=-1.0,
                           bias=relF[:, bass.ds(t0 + k, 1)]).then_inc(S("dist"), 1)

        def sum_in_bank(pe, S, k, hot, value, width):
            for b in range(2):
                m = pe.matmul(bank[4 + k][:, b * width:(b + 1) * width], hot[b], value, start=True, stop=True)
            m.then_inc(S("summed"), 1)

        def sum_zeros(pe, S, width):
            for k in range(BT):
                sum_in_bank(pe, S, k, [ident[:, :]] * 2, iota[:, 0:1].broadcast_to([P, width]), width)

        def add_tile(dve, S, after, k, block, width):
            dve.wait_ge(S("summed"), after + 1)
            dve.wait_ge(S("added"), after + 1)
            to = sums[:, bass.ds(block, 2), 0:width]
            dve.tensor_tensor(to, to, bank[4 + k][:, 0:2 * width].rearrange("p (b c) -> p b c", b=2),
                              ALU.add).then_inc(S("added"), 1)

        def edges0():
            def S(name):
                return sem("e0", name)

            spread_columns = slice(D + H, D + 3 * H)

            with nc.Block() as block:
                @block.gpsimd
                def _(pool):
                    gather_all(pool, 0, S, D + H, S("msgs"), 0, True)

                @block.sync
                def _(sp):
                    load_rel(sp, S)

                @block.tensor
                def _(pe):
                    sum_zeros(pe, S, WS)
                    blks = first_blocks(pe, BT, 2 * BT)
                    for q in range(2):
                        spread(pe, S, q, q, blks[q * BT:(q + 1) * BT], spread_columns, 2 * H)
                    with pe.Fori(0, ITERS) as i:
                        first = first_blocks(pe, i * RT + 3 * BT, RT)
                        for q in range(RB):
                            t0, m = i * RT + q * BT, (q % 2) * BT
                            pe.wait_ge(S("scored"), i * RB + q + 1)
                            spread(pe, S, i * RB + q + 2, q, first[q * BT:(q + 1) * BT], spread_columns, 2 * H)
                            for k in range(BT):
                                pe.wait_ge(S("hot"), t0 + k + 3)
                                pe.wait_ge(S("msgs"), t0 + k + 1)
                                pe.wait_ge(S("added"), t0 + k + 2)
                                sum_in_bank(pe, S, k, [onehot[:, m + k, b * P:(b + 1) * P] for b in range(2)], msg[:, m + k, :], WS)

                @block.scalar
                def _(act):
                    def weights_and_onehot(s, q):
                        m = (q % 2) * BT
                        act.wait_ge(S("scored"), s + 1)
                        if not isinstance(s, int):
                            act.wait_ge(S("summed"), s * BT)
                        act.activation(msg[:, m:m + BT, D:D + H], score[:, q % 2, :, :], ACT.Exp).then_inc(S("weighed"), 1)
                        distance(act, S, s * BT, 0)
                        for k in range(BT):
                            if k + 1 < BT:
                                distance(act, S, s * BT, k + 1)
                            act.wait_ge(S("dist"), s * BT + k + 1)
                            act.activation(onehot[:, m + k, :], dist[:, k % 2, :], ACT.Relu, scale=-1.0,
                                           bias=ones[:, 0:1]).then_inc(S("hot"), 1)

                    act.sem_inc(S("hot"), 2)
                    weights_and_onehot(0, 0)
                    with act.Fori(0, ITERS) as i:
                        for q in range(RB):
                            weights_and_onehot(i * RB + q + 1, (q + 1) % RB)
                            stage_indices(act, S, i, q)

                @block.vector
                def _(dve):
                    dve.sem_inc(S("added"), 1)
                    seq = Chain(dve, S("dve"))

                    def scores(s, q, rounds):
                        sc, a_s = score[:, q % 2, :, :], rows[:, q * BT:(q + 1) * BT, D:D + H]
                        of_dst = bank[q % 2][:, 0:BT * 2 * H].rearrange("p (k c) -> p k c", k=BT)
                        dve.wait_ge(S("spread"), s * BT + BT)
                        dve.wait_ge(S(f"landed{q}"), rounds * 16 * BT)
                        seq.link(dve.tensor_tensor(sc, a_s, of_dst[:, :, 0:H], ALU.add))
                        seq.link(dve.scalar_tensor_tensor(sc, sc, SLOPE, sc, op0=ALU.mult, op1=ALU.max))
                        dve.tensor_tensor(sc, sc, of_dst[:, :, H:2 * H], ALU.subtract).then_inc(S("scored"), 1)

                    mark_edges(dve, S, 0, 0, 1)
                    mark_edges(dve, S, 1, 1, 1)
                    scores(0, 0, 1)
                    with dve.Fori(0, ITERS) as i:
                        seq.enter(i, 2 * RB)
                        first = first_blocks(dve, i * RT, RT)
                        for q in range(RB):
                            t0, m = i * RT + q * BT, (q % 2) * BT
                            mark_edges(dve, S, i * RB + q + 2, (q + 2) % RB, i + (1 if q + 2 < RB else 2))
                            scores(i * RB + q + 1, (q + 1) % RB, i + (1 if q + 1 < RB else 2))
                            dve.wait_ge(S("weighed"), i * RB + q + 1)
                            for k in range(BT):
                                w = msg[:, m + k, D:D + H].unsqueeze(2).broadcast_to([P, H, HC])
                                dve.tensor_tensor(msg[:, m + k, 0:D].rearrange("p (h c) -> p h c", h=H),
                                                  rows[:, q * BT + k, 0:D].rearrange("p (h c) -> p h c", h=H), w,
                                                  ALU.mult).then_inc(S("msgs"), 1)
                                add_tile(dve, S, t0 + k, k, first[q * BT + k], WS)
                        seq.leave(ITERS)
                    blks = first_blocks(dve, ITERS * RT, BT)
                    for k in range(BT):
                        add_tile(dve, S, ITERS * RT + k, k, blks[k], WS)

        def nodes0():
            def S(name):
                return sem("n0", name)

            with nc.Block() as block:
                @block.vector
                def _(dve):
                    seq = Chain(dve, S("dve"))
                    with dve.Fori(0, NCH) as c:
                        seq.enter(c, 8 + NORM)
                        acc, w0 = chunk(sums, c, slice(0, D)), chunk(selfw, c)
                        seq.mark(dve.tensor_tensor(den, chunk(sums, c, slice(D, D + H)), w0, ALU.add))
                        for_heads = tmp[:, :, :].rearrange("p b (h c) -> p b h c", h=H)
                        seq.link(dve.tensor_tensor(for_heads, chunk(AB, c, slice(0, D)).rearrange("p b (h c) -> p b h c", h=H),
                                                   w0.unsqueeze(3).broadcast_to([P, CB, H, HC]), ALU.mult))
                        seq.mark(dve.reciprocal(den, den))
                        seq.link(dve.tensor_tensor(tmp[:, :, :], tmp[:, :, :], acc, ALU.add))
                        seq.link(dve.tensor_copy(degree[:, bass.ds(c * CB, CB)].unsqueeze(2), chunk(sums, c, slice(WS - 1, WS))))
                        dve.sem_inc(S("sums_used"), 1)
                        seq.link(dve.tensor_tensor(for_heads, for_heads, den.unsqueeze(3).broadcast_to([P, CB, H, HC]), ALU.mult))
                        seq.link(dve.tensor_tensor(tmp[:, :, :], tmp[:, :, :], row["bias"][:, :].unsqueeze(1).broadcast_to([P, CB, D]), ALU.add))
                        seq.link(dve.scalar_tensor_tensor(tmp[:, :, :], tmp[:, :, :], 0.0, chunk(X, c), op0=ALU.max, op1=ALU.add))
                        dve.wait_ge(S("turned"), c * CB + 1)
                        dve.wait_ge(S("kept"), c + 1)
                        normalise(dve, seq, CB, S, c + 1, valid[:, bass.ds(c * CB, CB)])
                        dve.sem_inc(S("res"), 1)
                        seq.leave(NCH)

                @block.gpsimd
                def _(pool):
                    pool.sem_inc(S("kept"), 1)
                    with pool.Fori(0, NCH) as c:
                        pool.wait_ge(S("sums_used"), c + 1)
                        pool.tensor_copy(chunk(sums, c), zeros(CB, WS)).then_inc(S("cleared"), 1)
                        pool.wait_ge(S("res"), c + 1)
                        pool.tensor_copy(chunk(X, c), res[:, :, :]).then_inc(S("kept"), 1)
                    pool.wait_ge(S("kept"), NCH + 1)
                    pool.wait_ge(S("cleared"), NCH)

                @block.tensor
                def _(pe):
                    pe.sem_inc(S("turned"), 1)
                    with pe.Fori(0, NCH) as c:
                        pe.wait_ge(S("res"), c + 1)
                        pe.transpose(bank[0][:, 0:P], res[:, 0, :], ident[:, :]).then_inc(S("turned"), 1)
                        for j in range(CB):
                            if j + 1 < CB:
                                t = pe.transpose(bank[(j + 1) % 2][:, 0:P], res[:, j + 1, :], ident[:, :])
                                t.then_inc(S("turned"), 1)
                            pe.wait_ge(S("xT"), c * CB + j + 1)
                            pe.wait_ge(S("ab"), c * CB + j + (2 if j == 0 else 1))
                            pe.matmul(bank[2 + j % 2][:, 0:2 * D], xT[:, j % 2, :], wB[:, :],
                                      start=True, stop=True).then_inc(S("out"), 1)

                @block.scalar
                def _(act):
                    act.sem_inc(S("ab"), 2)
                    with act.Fori(0, NCH) as c:
                        roots(act, CB, S, c + 1)

                        def to_ab(j):
                            act.wait_ge(S("out"), c * CB + j + 1)
                            act.activation(AB[:, bass.ds(c * CB + j, 1), :], bank[2 + j % 2][:, 0:2 * D].unsqueeze(1),
                                           ACT.Copy).then_inc(S("ab"), 1)

                        for j in range(CB):
                            act.wait_ge(S("turned"), c * CB + j + 2)
                            act.activation(xT[:, j % 2, :], bank[j % 2][:, 0:P], ACT.Copy).then_inc(S("xT"), 1)
                            if j:
                                to_ab(j - 1)
                        to_ab(CB - 1)

                @block.sync
                def _(sp):
                    with sp.Fori(0, NCH) as c:
                        sp.wait_ge(S("kept"), c + 2)
                        sp.dma_start(table_rows(1, c)[:, :, D:2 * D], chunk(X, c)).then_inc(S("stored"), 16)
                        sp.wait_ge(S("ab"), 2 + (c + 1) * CB)
                        sp.dma_start(table_rows(1, c)[:, :, 0:D], chunk(AB, c, slice(0, D))).then_inc(S("stored"), 16)
                    sp.wait_ge(S("stored"), 2 * 16 * NCH)

        def edges1():
            def S(name):
                return sem("e1", name)

            with nc.Block() as block:
                @block.gpsimd
                def _(pool):
                    gather_all(pool, 1, S, 2 * D, S("summed"), BT, True)

                @block.sync
                def _(sp):
                    load_rel(sp, S)

                @block.tensor
                def _(pe):
                    sum_zeros(pe, S, D + 1)
                    blks = first_blocks(pe, BT, 2 * BT)
                    pe.wait_ge(S("b1"), 1)
                    for q in range(2):
                        spread(pe, S, q, q, blks[q * BT:(q + 1) * BT], slice(0, D), D)
                    with pe.Fori(0, ITERS) as i:
                        first = first_blocks(pe, i * RT + 3 * BT, RT)
                        for q in range(RB):
                            t0, m = i * RT + q * BT, (q % 2) * BT
                            pe.wait_ge(S("scored"), t0 + BT)
                            spread(pe, S, i * RB + q + 2, q, first[q * BT:(q + 1) * BT], slice(0, D), D)
                            for k in range(BT):
                                pe.wait_ge(S("hot"), t0 + k + 3)
                                pe.wait_ge(S("added"), t0 + k + 2)
                                sum_in_bank(pe, S, k, [onehot[:, m + k, b * P:(b + 1) * P] for b in range(2)],
                                            rows[:, q * BT + k, D:2 * D + 1], D + 1)

                @block.scalar
                def _(act):
                    def gates_and_onehot(s, q):
                        m = (q % 2) * BT
                        gate = score[:, q % 2, :, 0]
                        distance(act, S, s * BT, 0)
                        act.wait_ge(S("scored"), s * BT + BT)
                        act.activation(gate, logit[:, q % 2, :], ACT.Sigmoid, bias=col["b2"][:, :]).then_inc(S("gated"), 1)
                        distance(act, S, s * BT, 1)
                        act.wait_ge(S("gated"), 2 * s + 3)
                        act.activation(minus[:, :], gate, ACT.Copy, scale=-1.0).then_inc(S("gated"), 1)
                        act.wait_ge(S("gated"), 2 * s + 4)
                        if not isinstance(s, int):
                            act.wait_ge(S("summed"), s * BT)
                        for k in range(BT):
                            if k >= 1 and k + 1 < BT:
                                distance(act, S, s * BT, k + 1)
                            act.wait_ge(S("dist"), s * BT + k + 1)
                            act.activation(onehot[:, m + k, :], dist[:, k % 2, :], ACT.Relu, scale=minus[:, k:k + 1],
                                           bias=gate[:, k:k + 1]).then_inc(S("hot"), 1)

                    act.sem_inc(S("hot"), 2)
                    act.sem_inc(S("gated"), 2)
                    gates_and_onehot(0, 0)
                    with act.Fori(0, ITERS) as i:
                        for q in range(RB):
                            gates_and_onehot(i * RB + q + 1, (q + 1) % RB)
                            stage_indices(act, S, i, q)

                @block.vector
                def _(dve):
                    dve.sem_inc(S("added"), 1)
                    seq = Chain(dve, S("dve"))

                    def logits(s, q, rounds):
                        m = q % 2
                        dve.wait_ge(S("spread"), s * BT + BT)
                        dve.wait_ge(S(f"landed{q}"), rounds * 16 * BT)
                        seq.link(dve.tensor_tensor(diff[:, m, :, :], bank[m][:, :].rearrange("p (k c) -> p k c", k=BT),
                                                   rows[:, q * BT:(q + 1) * BT, 0:D], ALU.subtract))
                        if not isinstance(s, int):
                            dve.wait_ge(S("gated"), 2 * s - 1)
                        for k in range(BT):
                            dve.scalar_tensor_tensor(diff[:, m, k, :], diff[:, m, k, :], 0.0, row["w2"][:, :], op0=ALU.max,
                                                     op1=ALU.mult, accum_out=logit[:, m, k:k + 1]).then_inc(S("scored"), 1)

                    dve.tensor_tensor(AB[:, 0:NB, 0:D], AB[:, 0:NB, 0:D], row["b1"][:, :].unsqueeze(1).broadcast_to([P, NB, D]),
                                      ALU.add).then_inc(S("b1"), 1)
                    mark_edges(dve, S, 0, 0, 1)
                    mark_edges(dve, S, 1, 1, 1)
                    logits(0, 0, 1)
                    with dve.Fori(0, ITERS) as i:
                        seq.enter(i, RB)
                        first = first_blocks(dve, i * RT, RT)
                        for q in range(RB):
                            t0 = i * RT + q * BT
                            mark_edges(dve, S, i * RB + q + 2, (q + 2) % RB, i + (1 if q + 2 < RB else 2))
                            logits(i * RB + q + 1, (q + 1) % RB, i + (1 if q + 1 < RB else 2))
                            for k in range(BT):
                                add_tile(dve, S, t0 + k, k, first[q * BT + k], D + 1)
                        seq.leave(ITERS)
                    blks = first_blocks(dve, ITERS * RT, BT)
                    for k in range(BT):
                        add_tile(dve, S, ITERS * RT + k, k, blks[k], D + 1)

        def nodes1():
            def S(name):
                return sem("n1", name)

            with nc.Block() as block:
                @block.vector
                def _(dve):
                    seq = Chain(dve, S("dve"))
                    dve.tensor_copy(dinv[:, :], degree[:, :]).then_inc(S("deg"), 1)
                    dve.wait_ge(S("rootdeg"), 1)
                    seq.link(dve.reciprocal(dinv[:, :], dinv[:, :]))
                    with dve.Fori(0, NCH) as c:
                        seq.enter(c, 5 + NORM + 1)

                        def per_node(t):
                            return t.unsqueeze(2).broadcast_to([P, CB, D]) if len(t.shape) == 2 else t.broadcast_to([P, CB, D])
                        r4 = chunk(AB, c, slice(D, 2 * D))
                        seq.link(dve.scalar_tensor_tensor(tmp[:, :, :], chunk(sums, c, slice(D, D + 1)).broadcast_to([P, CB, D]), 1.0, chunk(X, c),
                                                          op0=ALU.add, op1=ALU.mult))
                        seq.mark(dve.tensor_tensor(tmp[:, :, :], tmp[:, :, :], chunk(sums, c, slice(0, D)), ALU.subtract))
                        seq.link(dve.tensor_tensor(r4, r4, row["b4"][:, :].unsqueeze(1).broadcast_to([P, CB, D]), ALU.add))
                        seq.link(dve.tensor_tensor(r4, r4, degree[:, bass.ds(c * CB, CB)].unsqueeze(2).broadcast_to([P, CB, D]), ALU.mult))
                        dve.sem_inc(S("sums_used"), 1)
                        seq.link(dve.tensor_tensor(tmp[:, :, :], tmp[:, :, :], r4, ALU.add))
                        dve.wait_ge(S("gram_free"), c + 1)
                        dve.wait_ge(S("kept"), c + 1)
                        normalise(dve, seq, CB, S, c + 1, valid[:, bass.ds(c * CB, CB)])
                        dve.sem_inc(S("res"), 1)
                        seq.link(dve.tensor_tensor(r4, res[:, :, :], dinv[:, bass.ds(c * CB, CB)].unsqueeze(2).broadcast_to([P, CB, D]), ALU.mult))
                        dve.sem_inc(S("scaled"), 1)
                        seq.leave(NCH)

                @block.gpsimd
                def _(pool):
                    pool.sem_inc(S("kept"), 1)
                    with pool.Fori(0, NCH) as c:
                        pool.wait_ge(S("sums_used"), c + 1)
                        pool.tensor_copy(chunk(sums, c), zeros(CB, WS)).then_inc(S("cleared"), 1)
                        pool.wait_ge(S("res"), c + 1)
                        pool.tensor_copy(chunk(X, c), res[:, :, :]).then_inc(S("kept"), 1)
                    pool.wait_ge(S("kept"), NCH + 1)
                    pool.wait_ge(S("cleared"), NCH)

                @block.tensor
                def _(pe):
                    zero = iota[:, 0:1].broadcast_to([P, P])
                    pe.matmul(bank[6][:, 0:P], ident[:, :], zero, start=True, stop=False, skip_group_check=True)
                    pe.matmul(bank[7][:, 0:1], ident[:, :], iota[:, 0:1], start=True, stop=False, skip_group_check=True)
                    pe.sem_inc(S("gram_free"), 1)
                    with pe.Fori(0, NCH) as c:
                        pe.wait_ge(S("res"), c + 1)
                        for j in range(CB):
                            pe.matmul(bank[6][:, 0:P], res[:, j, :], res[:, j, :], start=False, stop=False, skip_group_check=True)
                            t = pe.matmul(bank[7][:, 0:1], res[:, j, :], ones[:, 0:1], start=False, stop=False, skip_group_check=True)
                        t.then_inc(S("gram_free"), 1)
                    pe.matmul(bank[6][:, 0:P], ident[:, :], zero, start=False, stop=True, skip_group_check=True)
                    pe.matmul(bank[7][:, 0:1], ident[:, :], iota[:, 0:1], start=False, stop=True, skip_group_check=True).then_inc(S("gram"), 1)
                    pe.wait_ge(S("gram"), 1)

                @block.scalar
                def _(act):
                    act.wait_ge(S("deg"), 1)
                    act.activation(dinv[:, :], dinv[:, :], ACT.Sqrt, bias=ones[:, 0:1]).then_inc(S("rootdeg"), 1)
                    with act.Fori(0, NCH) as c:
                        roots(act, CB, S, c + 1)

                @block.sync
                def _(sp):
                    with sp.Fori(0, NCH) as c:
                        sp.wait_ge(S("scaled"), c + 1)
                        sp.dma_start(table_rows(2, c), chunk(AB, c, slice(D, 2 * D))).then_inc(S("stored"), 16)
                    sp.wait_ge(S("stored"), 16 * NCH)

        def plain_edge_loops(S, l, before_pe, before_act, before_dve):
            with nc.Block() as block:
                @block.gpsimd
                def _(pool):
                    gather_all(pool, l, S, D, S("summed"), 0, False)

                @block.tensor
                def _(pe):
                    before_pe(pe)
                    with pe.Fori(0, ITERS) as i:
                        for q in range(RB):
                            t0, m = i * RT + q * BT, (q % 2) * BT
                            pe.wait_ge(S(f"landed{q}"), (i + 1) * 16 * BT)
                            for k in range(BT):
                                pe.wait_ge(S("hot"), t0 + k + 1)
                                sum_tile(pe, S, t0 + k, m + k, rows[:, q * BT + k, 0:D], D)

                @block.scalar
                def _(act):
                    before_act(act)
                    with act.Fori(0, ITERS) as i:
                        for q in range(RB):
                            act.wait_ge(S(f"landed{q}"), (i + 1) * 16 * BT)
                            stage_indices(act, S, i, q)

                @block.vector
                def _(dve):
                    before_dve(dve)
                    dve.sem_inc(S("added"), 2)
                    for k in range(BT):
                        mark_nodes(dve, S, k, k)
                    with dve.Fori(0, ITERS) as i:
                        first = first_blocks(dve, BT + i * RT, RT)
                        for q in range(RB):
                            t0, m = i * RT + q * BT, (q % 2) * BT
                            blks = first[q * BT:(q + 1) * BT]
                            for k in range(BT):
                                mark_nodes(dve, S, t0 + BT + k, (BT - m) + k)
                                add_sums(dve, S, t0 + k, m + k, blks[k], D)

        def edges2():
            def S(name):
                return sem("e2", name)

            def mix_pe(pe):
                pe.wait_ge(S("gram_sb"), 2)
                for b, k in enumerate("qkv"):
                    t = pe.matmul(bank[0][:, b * P:(b + 1) * P], W["gram"][:, :], W[k][:, :], start=True, stop=True)
                t.then_inc(S("gw"), 1)
                pe.matmul(bank[1][:, 0:1], W["KQ"][:, :], sx[:, :], start=True, stop=True).then_inc(S("u"), 1)
                pe.wait_ge(S("squares"), 2)
                pe.matmul(bank[2][:, 0:2], ones[:, :], scal[:, 0:2], start=True, stop=True).then_inc(S("norms"), 1)
                pe.wait_ge(S("gv"), 1)
                pe.matmul(bank[3][:, 0:P], W["KQ"][:, :], W["gv"][:, :], start=True, stop=True).then_inc(S("kv"), 1)
                pe.wait_ge(S("attn"), 1)
                pe.transpose(bank[4][:, 0:P], W["t"][:, :], ident[:, :]).then_inc(S("attnT"), 1)
                pe.wait_ge(S("attnT_sb"), 1)
                pe.matmul(bank[5][:, 0:P], W["gv"][:, :], W["linT"][:, :], start=True, stop=True).then_inc(S("wx"), 1)
                pe.wait_ge(S("wX"), 3)
                pe.sem_inc(S("turned"), 1)
                with pe.Fori(0, NCH) as c:
                    pe.wait_ge(S("res"), c + 1)
                    pe.transpose(bank[0][:, 0:P], res[:, 0, :], ident[:, :]).then_inc(S("turned"), 1)
                    for j in range(CB):
                        if j + 1 < CB:
                            pe.transpose(bank[(j + 1) % 2][:, 0:P], res[:, j + 1, :], ident[:, :]).then_inc(S("turned"), 1)
                        pe.wait_ge(S("xT"), c * CB + j + 1)
                        pe.wait_ge(S("out_free"), c * CB + j + (2 if j == 0 else 1))
                        pe.matmul(bank[2 + j % 2][:, 0:2 * D + 1], xT[:, j % 2, :], wX[:, 0:2 * D + 1],
                                  start=True, stop=True).then_inc(S("out"), 1)

            def mix_act(act):
                act.activation(W["gram"][:, :], bank[6][:, 0:P], ACT.Copy).then_inc(S("gram_sb"), 1)
                act.activation(sx[:, :], bank[7][:, 0:1], ACT.Copy).then_inc(S("gram_sb"), 1)
                act.activation(wX[:, D:2 * D], W["linT"][:, :], ACT.Copy, scale=(1 - BETA) * (1 - ALPHA)).then_inc(S("wX"), 1)
                act.wait_ge(S("squares"), 2)
                act.activation(W["gv"][:, :], bank[0][:, 2 * P:3 * P], ACT.Copy).then_inc(S("gv"), 1)
                act.wait_ge(S("norms"), 1)
                act.activation(scal[:, 2:4], bank[2][:, 0:2], ACT.Sqrt).then_inc(S("roots"), 1)
                act.wait_ge(S("attnT"), 1)
                act.activation(W["gv"][:, :], bank[4][:, 0:P], ACT.Copy).then_inc(S("attnT_sb"), 1)
                act.wait_ge(S("wx"), 1)
                act.activation(wX[:, 0:D], bank[5][:, 0:P], ACT.Copy, scale=BETA * (1 - ALPHA)).then_inc(S("wX"), 1)
                with act.Fori(0, NCH) as c:
                    act.wait_ge(S("turned"), c * CB + 1)
                    act.activation(res[:, :, :], chunk(X, c), ACT.Copy).then_inc(S("res"), 1)

                    def linear_part(j):
                        act.wait_ge(S("out"), c * CB + j + 1)
                        act.activation(AB[:, bass.ds(c * CB + j, 1), 0:D], bank[2 + j % 2][:, D:2 * D].unsqueeze(1),
                                       ACT.Copy).then_inc(S("lin"), 1)

                    for j in range(CB):
                        act.wait_ge(S("turned"), c * CB + j + 2)
                        act.activation(xT[:, j % 2, :], bank[j % 2][:, 0:P], ACT.Copy).then_inc(S("xT"), 1)
                        if j:
                            linear_part(j - 1)
                    linear_part(CB - 1)

            def mix_dve(dve):
                seq = Chain(dve, S("dve"))
                dve.wait_ge(S("gw"), 1)
                for b, k in enumerate("qk"):
                    dve.scalar_tensor_tensor(tmp[:, b, :], bank[0][:, b * P:(b + 1) * P], 1.0, W[k][:, :], op0=ALU.mult,
                                             op1=ALU.mult, accum_out=scal[:, b:b + 1]).then_inc(S("squares"), 1)
                dve.wait_ge(S("roots"), 1)
                seq.link(dve.scalar_tensor_tensor(scal[:, 4:5], scal[:, 2:3], float(D), scal[:, 3:4], op0=ALU.mult, op1=ALU.mult))
                seq.link(dve.reciprocal(scal[:, 5:6], scal[:, 4:5]))
                dve.wait_ge(S("u"), 1)
                seq.mark(dve.tensor_scalar(wX[:, 2 * D:2 * D + 1], bank[1][:, 0:1], scal[:, 5:6], None, op0=ALU.mult))
                dve.wait_ge(S("kv"), 1)
                seq.link(dve.scalar_tensor_tensor(W["t"][:, :], bank[3][:, 0:P], scal[:, 5:6], W["v"][:, :],
                                                  op0=ALU.mult, op1=ALU.add))
                dve.sem_inc(S("attn"), 1)
                dve.sem_inc(S("wX"), 1)
                dve.sem_inc(S("out_free"), 2)
                with dve.Fori(0, NCH) as c:
                    seq.enter(c, 2 * CB)
                    for j in range(CB):
                        dve.wait_ge(S("lin"), c * CB + j + 1)
                        seq.link(dve.tensor_scalar(scal[:, 6:7], bank[2 + j % 2][:, 2 * D:2 * D + 1], 1.0, None, op0=ALU.add))
                        seq.link(dve.reciprocal(scal[:, 7:8], scal[:, 6:7]))
                        to = AB[:, bass.ds(c * CB + j, 1), 0:D]
                        dve.scalar_tensor_tensor(to, bank[2 + j % 2][:, 0:D].unsqueeze(1), scal[:, 7:8], to, op0=ALU.mult,
                                                 op1=ALU.add).then_inc(S("out_free"), 1)
                    seq.leave(NCH)

            plain_edge_loops(S, 2, mix_pe, mix_act, mix_dve)

        def nodes2():
            def S(name):
                return sem("n2", name)

            with nc.Block() as block:
                @block.vector
                def _(dve):
                    seq = Chain(dve, S("dve"))
                    dve.sem_inc(S("out_free"), 2)
                    with dve.Fori(0, NCH) as c:
                        seq.enter(c, 4 + NORM)
                        scale = dinv[:, bass.ds(c * CB, CB)].unsqueeze(2).broadcast_to([P, CB, D])
                        dve.wait_ge(S("kept"), c + 1)
                        seq.link(dve.tensor_tensor(res[:, :, :], chunk(sums, c, slice(0, D)), chunk(AB, c, slice(D, 2 * D)), ALU.add))
                        dve.sem_inc(S("sums_used"), 1)
                        seq.link(dve.tensor_tensor(res[:, :, :], res[:, :, :], scale, ALU.mult))
                        dve.sem_inc(S("gcn_in"), 1)
                        seq.mark(dve.tensor_tensor(tmp[:, :, :], chunk(X, c), chunk(AB, c, slice(0, D)), ALU.add))
                        for j in range(CB):
                            dve.wait_ge(S("out"), c * CB + j + 1)
                            if j == 0:
                                seq.wait()
                            dve.tensor_tensor(tmp[:, j, :], tmp[:, j, :], bank[2 + j % 2][:, 0:D], ALU.add).then_inc(S("out_free"), 1)
                        dve.wait_ge(S("out_free"), 2 + (c + 1) * CB)
                        seq.link(dve.tensor_tensor(tmp[:, :, :], tmp[:, :, :], row["blin"][:, :].unsqueeze(1).broadcast_to([P, CB, D]), ALU.add))
                        normalise(dve, seq, CB, S, c + 1, valid[:, bass.ds(c * CB, CB)])
                        dve.sem_inc(S("res"), 1)
                        seq.leave(NCH)

                @block.gpsimd
                def _(pool):
                    pool.sem_inc(S("kept"), 1)
                    with pool.Fori(0, NCH) as c:
                        pool.wait_ge(S("sums_used"), c + 1)
                        pool.tensor_copy(chunk(sums, c), zeros(CB, WS)).then_inc(S("cleared"), 1)
                        pool.wait_ge(S("res"), c + 1)
                        pool.tensor_copy(chunk(X, c), res[:, :, :]).then_inc(S("kept"), 1)
                    pool.wait_ge(S("kept"), NCH + 1)
                    pool.wait_ge(S("cleared"), NCH)

                @block.tensor
                def _(pe):
                    pe.sem_inc(S("turned"), 1)
                    with pe.Fori(0, NCH) as c:
                        pe.wait_ge(S("gcn_in"), c + 1)
                        pe.transpose(bank[0][:, 0:P], res[:, 0, :], ident[:, :]).then_inc(S("turned"), 1)
                        for j in range(CB):
                            if j + 1 < CB:
                                pe.transpose(bank[(j + 1) % 2][:, 0:P], res[:, j + 1, :], ident[:, :]).then_inc(S("turned"), 1)
                            pe.wait_ge(S("xT"), c * CB + j + 1)
                            pe.wait_ge(S("out_free"), c * CB + j + (2 if j == 0 else 1))
                            pe.matmul(bank[2 + j % 2][:, 0:D], xT[:, j % 2, :], wG[:, :], start=True, stop=True).then_inc(S("out"), 1)

                @block.scalar
                def _(act):
                    with act.Fori(0, NCH) as c:
                        for j in range(CB):
                            act.wait_ge(S("turned"), c * CB + j + 2)
                            act.activation(xT[:, j % 2, :], bank[j % 2][:, 0:P], ACT.Copy).then_inc(S("xT"), 1)
                        roots(act, CB, S, c + 1)

                @block.sync
                def _(sp):
                    with sp.Fori(0, NCH) as c:
                        sp.wait_ge(S("kept"), c + 2)
                        sp.dma_start(table_rows(3, c), chunk(X, c)).then_inc(S("stored"), 16)
                    sp.wait_ge(S("stored"), 16 * NCH)

        def edges3():
            def nothing(eng):
                pass

            plain_edge_loops(lambda name: sem("e3", name), 3, nothing, nothing, nothing)

        def nodes3():
            def S(name):
                return sem("n3", name)

            def products(eng, step):
                with eng.Fori(0, NFM // 2) as g:
                    step(g * 2, FM, 0)
                    step(g * 2 + 1, FM, 1)
                step(NFM, FREST, 0)

            relu = [diff[:, b, :, :] for b in range(2)]

            with nc.Block() as block:
                @block.vector
                def _(dve):
                    seq = Chain(dve, S("dve"))

                    def batch_stats(layer):
                        def step(m, width, b):
                            dve.wait_ge(S("y" + layer), 2 + m + 1)
                            dve.bn_stats(bnst[:, bass.ds(m, 1), :].rearrange("p o c -> p (o c)"),
                                         HT[1][:, bass.ds(m * FM, width)]).then_inc(S("st" + layer), 1)
                        products(dve, step)
                        dve.wait_ge(S("st" + layer), NFM + 1)
                        dve.bn_aggr(bnmv[:, 0:2], bnst[:, :, :]).then_inc(S("bnvar" + layer), 1)
                        dve.wait_ge(S("bnroot" + layer), 1)
                        seq.link(dve.reciprocal(bnmv[:, 3:4], bnmv[:, 2:3]))
                        seq.link(dve.tensor_tensor(bnmv[:, 4:5], bnmv[:, 3:4], col["g" + layer][:, :], ALU.mult))
                        seq.link(dve.tensor_tensor(bnmv[:, 6:7], bnmv[:, 0:1], bnmv[:, 4:5], ALU.mult))
                        dve.tensor_tensor(bnmv[:, 5:6], col["be" + layer][:, :], bnmv[:, 6:7], ALU.subtract).then_inc(S("bn" + layer), 1)

                    seq.link(dve.tensor_scalar(col["eps"][:, :], col["eps"][:, :], 1.0, None, op0=ALU.add))
                    with dve.Fori(0, NCH) as c:
                        dve.wait_ge(S("turned"), c * CB + 1)
                        dve.scalar_tensor_tensor(res[:, :, :], chunk(X, c), col["eps"][:, :], chunk(sums, c, slice(0, D)),
                                                 op0=ALU.mult, op1=ALU.add).then_inc(S("h"), 1)
                    batch_stats("1")
                    batch_stats("2")

                    def last(m, nb, b):
                        to = X[:, bass.ds(m * 4, nb), :]
                        dve.wait_ge(S("back"), m + 3)
                        seq.link(dve.tensor_tensor(tmp[:, 0:nb, :], to, bank[b][:, 0:nb * P].rearrange("p (k f) -> p k f", k=nb), ALU.add))
                        normalise(dve, seq, nb, S, m + 1, valid[:, bass.ds(m * 4, nb)],
                                  lambda j: X[:, bass.ds(m * 4 + j, 1), :].rearrange("p o c -> p (o c)"))
                        dve.sem_inc(S("done"), 1)

                    with dve.Fori(0, NFM // 2) as g:
                        seq.enter(g, 2 * (1 + 3 * 4 + 1))
                        last(g * 2, 4, 0)
                        last(g * 2 + 1, 4, 1)
                        seq.leave(NFM // 2)
                    last(NFM, 1, 0)

                @block.tensor
                def _(pe):
                    pe.sem_inc(S("turned"), 1)
                    with pe.Fori(0, NCH) as c:
                        pe.wait_ge(S("h"), c + 1)
                        for j in range(CB):
                            pe.wait_ge(S("hT"), c * CB + j + 1)
                            pe.transpose(bank[j % 2][:, 0:P], res[:, j, :], ident[:, :]).then_inc(S("turned"), 1)
                            if j == CB - 1:
                                pe.wait_ge(S("hT"), (c + 1) * CB + 2)

                    def product(layer, w):
                        def step(m, width, b):
                            if layer == "2":
                                pe.wait_ge(S("relu1"), m + 1)
                            pe.wait_ge(S("y" + layer), m + 1)
                            pe.matmul(bank[2 + b][:, 0:width], w[:, :], HT[0][:, bass.ds(m * FM, width)],
                                      start=True, stop=True).then_inc(S("p" + layer), 1)
                        products(pe, step)

                    pe.sem_inc(S("back"), 2)
                    pe.wait_ge(S("hT"), 2 + NB)
                    product("1", W["w1T"])
                    product("2", W["w2T"])

                    def back(m, width, b):
                        pe.wait_ge(S("relu2"), m + 1)
                        pe.wait_ge(S("done"), m + 1)
                        for k in range(-(-width // P)):
                            t = pe.transpose(bank[b][:, k * P:(k + 1) * P], relu[b][:, k, :], ident[:, :])
                        t.then_inc(S("back"), 1)
                    products(pe, back)

                @block.gpsimd
                def _(pool):
                    pool.sem_inc(S("done"), 2)

                @block.scalar
                def _(act):
                    act.sem_inc(S("hT"), 2)
                    act.sem_inc(S("y1"), 2)
                    act.sem_inc(S("y2"), 2)
                    with act.Fori(0, NCH) as c:
                        for j in range(CB):
                            act.wait_ge(S("turned"), c * CB + j + 2)
                            act.activation(HT[0][:, bass.ds((c * CB + j) * P, P)], bank[j % 2][:, 0:P], ACT.Copy).then_inc(S("hT"), 1)

                    def product(layer):
                        def step(m, width, b):
                            act.wait_ge(S("p" + layer), m + 1)
                            act.activation(HT[1][:, bass.ds(m * FM, width)], bank[2 + b][:, 0:width], ACT.Identity,
                                           bias=col["lb" + layer][:, :]).then_inc(S("y" + layer), 1)
                        products(act, step)
                        act.wait_ge(S("bnvar" + layer), 1)
                        act.activation(bnmv[:, 2:3], bnmv[:, 1:2], ACT.Sqrt, bias=eps_ln[:, :]).then_inc(S("bnroot" + layer), 1)
                        act.wait_ge(S("bn" + layer), 1)

                    product("1")

                    def relu1(m, width, b):
                        act.activation(HT[0][:, bass.ds(m * FM, width)], HT[1][:, bass.ds(m * FM, width)], ACT.Relu,
                                       bias=bnmv[:, 5:6], scale=bnmv[:, 4:5]).then_inc(S("relu1"), 1)
                    products(act, relu1)
                    act.wait_ge(S("relu1"), NFM + 1)
                    product("2")

                    def relu2(m, width, b):
                        act.wait_ge(S("back"), m + 1)
                        act.activation(relu[b].rearrange("p k f -> p (k f)")[:, 0:width], HT[1][:, bass.ds(m * FM, width)], ACT.Relu,
                                       bias=bnmv[:, 5:6], scale=bnmv[:, 4:5]).then_inc(S("relu2"), 1)
                        roots(act, -(-width // P), S, m + 1)
                    products(act, relu2)

                @block.sync
                def _(sp):
                    with sp.Fori(0, NFM) as m:
                        sp.wait_ge(S("done"), m + 3)
                        sp.dma_start(out[0:NFM * FM].rearrange("(b p) c -> p b c", p=P)[:, bass.ds(m * 4, 4), :],
                                     X[:, bass.ds(m * 4, 4), :]).then_inc(S("wrote"), 16)
                    sp.wait_ge(S("done"), NFM + 3)
                    sp.dma_start(out[NFM * FM:N], X[0:FREST, NB - 1, :]).then_inc(S("wrote"), 16)
                    sp.wait_ge(S("wrote"), 16 * (NFM + 1))

        prepare()
        project()
        edges0()
        nodes0()
        edges1()
        nodes1()
        clear_semaphores()
        edges2()
        nodes2()
        edges3()
        nodes3()


INPUTS = ['x', 'src', 'dst', 'L0_gnn_W', 'L0_gnn_att_src', 'L0_gnn_att_dst', 'L0_gnn_bias', 'L1_gnn_W1', 'L1_gnn_b1',
          'L1_gnn_W2', 'L1_gnn_b2', 'L1_gnn_W4', 'L1_gnn_b4', 'L2_gnn_Wq', 'L2_gnn_Wk', 'L2_gnn_Wv', 'L2_gnn_W_gcn',
          'L2_gnn_b_gcn', 'L2_gnn_W_lin', 'L2_gnn_b_lin', 'L3_gnn_eps', 'L3_gnn_W1', 'L3_gnn_b1', 'L3_gnn_g1',
          'L3_gnn_be1', 'L3_gnn_W2', 'L3_gnn_b2', 'L3_gnn_g2', 'L3_gnn_be2']


def kernel(**inputs):
    import concourse.bacc as bacc
    from concourse.bass_utils import run_bass_kernel_spmd

    nc = bacc.Bacc("TRN2", target_bir_lowering=False, num_devices=1)
    arrays, args = {}, {}
    for name in INPUTS:
        v = np.ascontiguousarray(inputs[name])
        v = v.reshape(v.shape or (1,))
        arrays["in_" + name] = v
        args[name] = nc.dram_tensor("in_" + name, v.shape, mybir.dt.from_np(v.dtype), kind="ExternalInput").ap()
    out = nc.dram_tensor("out_x", (N, D), F32, kind="ExternalOutput").ap()
    tables = [nc.dram_tensor(f"table{l}", (NB * P, w), F32).ap() for l, w in enumerate((D + H, 2 * D, D, D))]
    rel = nc.dram_tensor("rel", (TPAD * P,), BF16).ap()
    gnn(nc, args, out, tables, rel)
    return run_bass_kernel_spmd(nc, [arrays], core_ids=[0]).results[0]["out_x"]
```

```python
import numpy as np
from contextlib import ExitStack

import concourse.bass as bass
from concourse import mybir

P = 128
N = 6250
E = 106250
D = 128
H = 4
HC = D // H
NB = -(-N // P)
LAST = N - (NB - 1) * P
CB = 7
NCH = NB // CB
TILES = -(-E // P)
BT = 4
RB = 4
RT = RB * BT
ITERS = -(-TILES // RT)
IC = -(-(ITERS + 1) * RT // P)
TPAD = IC * P
FULL = E // P
REST = E - FULL * P
SLOPE = 0.2
ALPHA, BETA = 0.6, 0.4
LN_EPS = 1e-5
BN_EPS = 1e-5
RANGE = 60.0
FAR = 30000
WS = D + H + 1
WAB = 2 * D
FM = 512
NFM = N // FM
FREST = N - NFM * FM
F32 = mybir.dt.float32
BF16 = mybir.dt.bfloat16
I32 = mybir.dt.int32
ALU = mybir.AluOpType
ACT = mybir.ActivationFunctionType
AX = mybir.AxisListType


class Chain:

    def __init__(self, eng, sem):
        self.eng, self.sem, self.n, self.i, self.per = eng, sem, 0, None, 0

    def enter(self, i, per):
        self.i, self.per, self.start = i, per, self.n

    def leave(self, count):
        assert self.n - self.start == self.per, (self.n - self.start, self.per)
        self.n, self.i = self.start + self.per * count, None

    def mark(self, ins):
        ins.then_inc(self.sem, 1)
        self.n += 1

    def wait(self):
        self.eng.wait_ge(self.sem, self.n if self.i is None else self.i * self.per + self.n)

    def link(self, ins):
        self.mark(ins)
        self.wait()


def gnn(nc, a, out, table, rel):
    ctx = ExitStack()
    with ctx:
        def sb(name, shape, dt=F32):
            return ctx.enter_context(nc.sbuf_tensor(name, shape, dt))

        X = sb("X", [P, NB, D])
        AB = sb("AB", [P, NB + 1, WAB])
        sums = sb("sums", [P, NB + 1, WS])
        parts = sb("parts", [P, NB + 1, 3, 2 * H], BF16)
        selfw = sb("selfw", [P, NB, H])
        valid = sb("valid", [P, NB])
        degree = sb("degree", [P, NB])
        dinv = sb("dinv", [P, NB])
        ABf = AB[:, :, :].rearrange("p b c -> p (b c)")
        HT = [ABf[:, 0:NB * P], ABf[:, NB * P:2 * NB * P]]
        srcI = sb("srcI", [P, TPAD], I32)
        relF = sb("relF", [P, TPAD])
        blk = sb("blk", [1, BT + TPAD], I32)
        relb = sb("relb", [P, IC, P], BF16)
        relB = sb("relB", [P, RB, BT * P], BF16)
        idx = sb("idx", [P, RT], I32)
        onehot = sb("onehot", [P, 2 * BT, 2 * P])
        onehotT = sb("onehotT", [P, 2, 2, BT * P])
        onehotTb = onehotT[:, :, :, :].bitcast(BF16)[:, :, :, 0:BT * P]
        ofdst = sb("ofdst", [P, BT, 2 * H])
        dist = sb("dist", [P, BT, 2 * P])
        rows = sb("rows", [P, RT, 2 * D + 1])
        msg = sb("msg", [P, 2 * BT, WS])
        diff = sb("diff", [P, 2, BT, D])
        minus = sb("minus", [P, BT])
        score = sb("score", [P, 2, BT, H])
        logit = sb("logit", [P, 2, BT])
        ident = sb("ident", [P, P])
        ones = sb("ones", [P, P])
        iota = sb("iota", [P, 2 * P])
        node = sb("node", [P, 2])
        hmask = sb("hmask", [P, H])
        eps_ln = sb("eps_ln", [P, 1])
        wA = sb("wA", [P, D + 2 * H])
        wB = sb("wB", [P, 2 * D])
        wX = sb("wX", [P, 2 * D + 2])
        wG = sb("wG", [P, P])
        W = {k: sb(f"w_{k}", [P, P]) for k in
             ("q", "k", "v", "gcn", "lin", "w1", "w2", "qT", "kT", "linT", "KQ", "w1T", "w2T", "gram", "gv", "t")}
        row = {k: sb(f"row_{k}", [P, D]) for k in ("bias", "b1", "w2", "b4", "blin")}
        col = {k: sb(f"col_{k}", [P, 1]) for k in
               ("as", "ad", "b2", "bg", "eps", "lb1", "g1", "be1", "lb2", "g2", "be2")}
        att = sb("att", [P, 2 * H])
        tmp = sb("tmp", [P, CB, D])
        res = sb("res", [P, CB, D])
        relv = sb("relv", [P, IC, P])
        xT = sb("xT", [P, 2, P])
        stats = sb("stats", [P, 2, CB, 6])
        mv = sb("mv", [P, 2, CB, 2])
        rstd = sb("rstd", [P, 2, CB])
        shift = sb("shift", [P, 2, CB])
        tmps = [tmp[:, :, :], dist[:, :, :].rearrange("p k c -> p (k c)")[:, 0:CB * D].rearrange("p (b c) -> p b c", b=CB)]
        ress = [res[:, :, :], relv[:, :, :]]
        xTs = onehot[:, :, :].rearrange("p k c -> p (k c)")[:, 0:CB * P].rearrange("p (b c) -> p b c", b=CB)
        firsti = sb("firsti", [P, IC], I32)
        firstf = sb("firstf", [P, IC])
        den = sb("den", [P, CB, H])[:, :, :]
        top = sb("top", [P, 3 * H])
        bound = sb("bound", [P, NB, H])
        own = sb("own", [P, NB, H])
        scal = sb("scal", [P, 12])
        sx = sb("sx", [P, 1])
        bnst = sb("bnst", [P, NFM + 1, 6])
        bnmv = sb("bnmv", [P, 8])

        bank = [ctx.enter_context(nc.psum_tensor(f"bank{i}", [P, 512], F32)) for i in range(8)]

        semaphores = {}

        def sem(phase, name):
            key = f"{phase}_{name}"
            if key not in semaphores:
                semaphores[key] = nc.alloc_semaphore(key)
            return semaphores[key]

        def clear_semaphores():
            nc.clear_and_free_semaphores(list(semaphores.values()))
            semaphores.clear()
            nc.all_engine_barrier()

        def chunk(t, c, of=slice(None)):
            return t[:, bass.ds(c * CB, CB), of]

        def table_rows(l, c):
            return table[l].rearrange("(b p) c -> p b c", p=P)[:, bass.ds(c * CB, CB), :]

        def first_blocks(eng, tile, count):
            return nc.values_load_multi_w_load_instructions(
                blk[0:1, bass.ds(tile, count)], engines=[eng.engine], min_val=0, max_val=NB - 1,
                skip_runtime_bounds_check_because="every dst is below N")[1]

        def zeros(k, width):
            return iota[:, 0:1].unsqueeze(2).broadcast_to([P, k, width])

        def pass_gate(eng, S):
            name = {nc.vector.engine: "dve_gate", nc.gpsimd.engine: "pool_gate", nc.scalar.engine: "act_gate",
                    nc.tensor.engine: "pe_gate"}[eng.engine]
            eng.sem_inc(S(name), 1)


        def moments(dve, seq, S, h, nb):
            for j in range(nb):
                seq.mark(dve.bn_stats(stats[:, h, j, :], tmps[h][:, j, :]))
            seq.wait()
            pass_gate(dve, S)
            for j in range(nb - 1):
                seq.mark(dve.bn_aggr(mv[:, h, j, :], stats[:, h, j, :]))
            seq.wait()
            pass_gate(dve, S)
            dve.bn_aggr(mv[:, h, nb - 1, :], stats[:, h, nb - 1, :]).then_inc(S("var"), 1)

        def root(act, S, m, h, nb):
            act.wait_ge(S("var"), m + 1)
            act.activation(rstd[:, h, 0:nb], mv[:, h, 0:nb, 1], ACT.Sqrt, bias=eps_ln[:, :]).then_inc(S("root"), 1)

        def scale_and_shift(dve, seq, S, m, h, nb, mask):
            r = rstd[:, h, 0:nb]
            dve.wait_ge(S("root"), m + 1)
            seq.link(dve.reciprocal(r, r))
            seq.link(dve.tensor_tensor(r, r, mask, ALU.mult))
            dve.scalar_tensor_tensor(shift[:, h, 0:nb], mv[:, h, 0:nb, 0], -1.0, r, op0=ALU.mult,
                                     op1=ALU.mult).then_inc(S("norm"), 1)

        def apply(act, S, m, h, nb, to, done):
            act.wait_ge(S("norm"), m + 1)
            for j in range(nb):
                act.activation(to(j), tmps[h][:, j:j + 1, :], ACT.Identity, scale=rstd[:, h, j:j + 1],
                               bias=shift[:, h, j:j + 1]).then_inc(S(done), 1)

        def in_turn(eng, step):
            with eng.Fori(0, NCH // 2) as g:
                step(g * 2, 0)
                step(g * 2 + 1, 1)
            step(NCH - 1, 0)

        def in_turn_counted(eng, seq, marks, step):
            with eng.Fori(0, NCH // 2) as g:
                seq.enter(g, 2 * marks)
                step(g * 2, 0)
                step(g * 2 + 1, 1)
                seq.leave(NCH // 2)
            step(NCH - 1, 0)

        def turn_chunk(pe, S, c, h, of, ready, more=0):
            for b, (lo, hi) in enumerate(((0, 4), (4, CB))):
                pe.wait_ge(S("xT"), c * 2 + b + 1)
                if ready:
                    pe.wait_ge(S(ready), c * CB + hi + more)
                for j in range(lo, hi):
                    t = pe.transpose(bank[b][:, (j - lo) * P:(j - lo + 1) * P], of[h][:, j, :], ident[:, :])
                t.then_inc(S("turned"), 1)

        def take_chunk(act, S, c, outs):
            act.wait_ge(S("out"), c * outs + 1)
            for b, (lo, hi) in enumerate(((0, 4), (4, CB))):
                act.wait_ge(S("turned"), c * 2 + b + 5)
                act.activation(xTs[:, lo:hi, :], bank[b][:, 0:(hi - lo) * P].rearrange("p (b c) -> p b c", c=P),
                               ACT.Copy).then_inc(S("xT"), 1)

        def prepare():
            def S(name):
                return sem("prep", name)

            dst_t = tmp[:, :, :].bitcast(I32)
            src_t = res[:, :, :].bitcast(I32)
            src_f = AB[:, 0:IC, 0:P]
            to_turn = [relv[:, c, :] for c in range(IC)] + [src_f[:, c, :] for c in range(IC)]
            loads = [(wA[:, 0:D], a["L0_gnn_W"]),
                     (col["as"][:, :], a["L0_gnn_att_src"].rearrange("h (c o) -> (h c) o", o=1)),
                     (col["ad"][:, :], a["L0_gnn_att_dst"].rearrange("h (c o) -> (h c) o", o=1)),
                     (wB[:, 0:D], a["L1_gnn_W1"]), (wB[:, D:2 * D], a["L1_gnn_W4"]),
                     (col["b2"][:, :], a["L1_gnn_b2"].partition_broadcast(P)),
                     (row["w2"][:, :], a["L1_gnn_W2"].rearrange("k o -> (k o)").partition_broadcast(P)),
                     (W["q"][:, :], a["L2_gnn_Wq"]), (W["k"][:, :], a["L2_gnn_Wk"]), (W["v"][:, :], a["L2_gnn_Wv"]),
                     (W["gcn"][:, :], a["L2_gnn_W_gcn"]), (W["lin"][:, :], a["L2_gnn_W_lin"]),
                     (W["w1"][:, :], a["L3_gnn_W1"]), (W["w2"][:, :], a["L3_gnn_W2"]),
                     (col["eps"][:, :], a["L3_gnn_eps"].partition_broadcast(P))]
            loads += [(row[r][:, :], a[name].partition_broadcast(P)) for r, name in
                      (("bias", "L0_gnn_bias"), ("b1", "L1_gnn_b1"), ("b4", "L1_gnn_b4"), ("blin", "L2_gnn_b_lin"))]
            loads += [(col[c][:, :], a[name].rearrange("(p o) -> p o", o=1)) for c, name in
                      (("bg", "L2_gnn_b_gcn"), ("lb1", "L3_gnn_b1"), ("g1", "L3_gnn_g1"), ("be1", "L3_gnn_be1"),
                       ("lb2", "L3_gnn_b2"), ("g2", "L3_gnn_g2"), ("be2", "L3_gnn_be2"))]

            with nc.Block() as block:
                @block.sync
                def _(sp):
                    sp.wait_ge(S("filled"), 1)
                    t0 = (IC - 1) * P
                    for v, name in ((dst_t, "dst"), (src_t, "src")):
                        e = a[name]
                        sp.dma_start(v[:, 0:IC - 1, :], e[0:t0 * P].rearrange("(c p e) -> p c e", p=P, e=P)).then_inc(S("idx"), 16)
                        sp.dma_start(v[0:FULL - t0, IC - 1, :], e[t0 * P:FULL * P].rearrange("(p e) -> p e", e=P)).then_inc(S("idx"), 16)
                        sp.dma_start(v[FULL - t0:FULL - t0 + 1, IC - 1, 0:REST],
                                     e[FULL * P:E].rearrange("(p e) -> p e", p=1)).then_inc(S("idx"), 16)
                    sp.dma_start(blk[0:1, BT:BT + FULL], a["dst"][0:FULL * P].rearrange("(t e) -> e t", e=P)[0:1, :],
                                 allow_slow_non_contiguous=True).then_inc(S("first"), 16)
                    sp.dma_start(blk[0:1, BT + FULL:BT + FULL + 1],
                                 a["dst"][FULL * P:FULL * P + 1].rearrange("(p e) -> p e", p=1)).then_inc(S("first"), 16)
                    sp.dma_start(X[:, 0:NB - 1, :], a["x"][0:(NB - 1) * P].rearrange("(b p) c -> p b c", p=P)).then_inc(S("x"), 16)
                    sp.dma_start(X[0:LAST, NB - 1, :], a["x"][(NB - 1) * P:N]).then_inc(S("x"), 16)
                    for to, of in loads[1::2]:
                        sp.dma_start(to, of).then_inc(S("w"), 16)
                    sp.wait_ge(S("relb"), 1)
                    sp.dma_start(rel.rearrange("(c p e) -> p c e", p=P, e=P), relb[:, :, :]).then_inc(S("x"), 16)
                    sp.wait_ge(S("x"), 48)

                @block.gpsimd
                def _(pool):
                    seq = Chain(pool, S("pool"))
                    seq.mark(pool.memset(dst_t[:, IC - 1, :], FAR))
                    seq.mark(pool.memset(src_t[:, IC - 1, :], 0))
                    seq.mark(pool.memset(blk[:, :], 0))
                    seq.link(pool.memset(X[:, NB - 1, :], 0.0))
                    pool.sem_inc(S("filled"), 1)
                    seq.mark(pool.memset(ident[:, :], 0.0))
                    seq.mark(pool.memset(hmask[:, :], 1.0))
                    seq.mark(pool.memset(valid[:, :], 1.0))
                    seq.mark(pool.memset(ones[:, :], 1.0))
                    seq.mark(pool.memset(eps_ln[:, :], LN_EPS))
                    seq.mark(pool.iota(node[:, :], pattern=[[P, 2]], base=0, channel_multiplier=1,
                                       allow_small_or_imprecise_dtypes=True))
                    seq.link(pool.iota(iota[:, :], pattern=[[1, 2 * P]], base=0, channel_multiplier=0,
                                       allow_small_or_imprecise_dtypes=True))
                    seq.mark(pool.affine_select(out=ident[:, :], in_=ident[:, :], compare_op=ALU.not_equal, fill=1.0,
                                                base=0, pattern=[[-1, P]], channel_multiplier=1))
                    seq.mark(pool.affine_select(out=valid[:, NB - 1:NB], in_=valid[:, NB - 1:NB], compare_op=ALU.is_ge,
                                                fill=0.0, base=LAST - 1, pattern=[[0, 1]], channel_multiplier=-1))
                    seq.link(pool.affine_select(out=hmask[:, :], in_=hmask[:, :], compare_op=ALU.is_ge, fill=0.0,
                                                base=0, pattern=[[-HC, H]], channel_multiplier=1))
                    seq.link(pool.affine_select(out=hmask[:, :], in_=hmask[:, :], compare_op=ALU.is_ge, fill=0.0,
                                                base=HC - 1, pattern=[[HC, H]], channel_multiplier=-1))
                    pool.sem_inc(S("consts"), 1)
                    seq.mark(pool.memset(sums[:, :, :], 0.0))
                    seq.mark(pool.memset(AB[:, NB, :], 0.0))
                    seq.mark(pool.memset(rows[:, :, 2 * D:2 * D + 1], 1.0))
                    seq.mark(pool.memset(parts[:, NB, :, :], 0.0))
                    seq.link(pool.memset(msg[:, :, WS - 1:WS], 1.0))

                @block.scalar
                def _(act):
                    for to, of in loads[0::2]:
                        act.dma_start(to, of).then_inc(S("w"), 16)
                    act.wait_ge(S("w"), 16 * len(loads))
                    act.sem_inc(S("weights"), 1)
                    act.wait_ge(S("wt"), 1)
                    act.activation(W["t"][:, :], bank[4][:, 0:P], ACT.Copy).then_inc(S("wt_sb"), 1)
                    act.activation(W["qT"][:, :], bank[4][:, P:2 * P], ACT.Copy).then_inc(S("wt_sb"), 1)
                    act.activation(W["kT"][:, :], bank[4][:, 2 * P:3 * P], ACT.Copy).then_inc(S("wt_sb"), 1)
                    act.activation(W["linT"][:, :], bank[4][:, 3 * P:4 * P], ACT.Copy).then_inc(S("wt_sb"), 1)
                    act.activation(W["w1T"][:, :], bank[5][:, 0:P], ACT.Copy).then_inc(S("wt_sb"), 1)
                    act.activation(W["w2T"][:, :], bank[5][:, P:2 * P], ACT.Copy).then_inc(S("wt_sb"), 1)
                    act.wait_ge(S("wp"), 1)
                    act.activation(wA[:, D:D + 2 * H], bank[6][:, 0:2 * H], ACT.Copy).then_inc(S("act"), 1)
                    act.activation(W["KQ"][:, :], bank[6][:, P:2 * P], ACT.Copy).then_inc(S("act"), 1)
                    act.activation(wG[:, :], bank[6][:, 2 * P:3 * P], ACT.Copy, scale=ALPHA).then_inc(S("act"), 1)
                    act.wait_ge(S("act"), 3)

                @block.tensor
                def _(pe):
                    pe.wait_ge(S("consts"), 1)
                    pe.wait_ge(S("weights"), 1)
                    for b, w in enumerate((wA[:, 0:D], W["q"][:, :], W["k"][:, :], W["lin"][:, :])):
                        pe.transpose(bank[4][:, b * P:(b + 1) * P], w, ident[:, :])
                    pe.transpose(bank[5][:, 0:P], W["w1"][:, :], ident[:, :])
                    pe.transpose(bank[5][:, P:2 * P], W["w2"][:, :], ident[:, :]).then_inc(S("wt"), 1)
                    pe.wait_ge(S("tof"), 1)
                    for j, v in enumerate(to_turn):
                        pe.transpose(bank[j // 4][:, (j % 4) * P:(j % 4 + 1) * P], v, ident[:, :]).then_inc(S("turned"), 1)
                    pe.wait_ge(S("wt_sb"), 6)
                    pe.wait_ge(S("att"), 1)
                    pe.matmul(bank[6][:, 0:2 * H], W["t"][:, :], att[:, :], start=True, stop=True)
                    pe.matmul(bank[6][:, P:2 * P], W["kT"][:, :], W["qT"][:, :], start=True, stop=True)
                    pe.matmul(bank[6][:, 2 * P:3 * P], W["gcn"][:, :], W["linT"][:, :], start=True, stop=True).then_inc(S("wp"), 1)
                    pe.matmul(bank[7][:, 0:P], W["gram"][:, :], W["linT"][:, :], start=True, stop=True).then_inc(S("bl"), 1)

                @block.vector
                def _(dve):
                    seq = Chain(dve, S("dve"))
                    dve.wait_ge(S("idx"), 16 * 6)
                    seq.link(dve.tensor_scalar(firsti[:, :], dst_t[:, :, 0], N - 1, None, op0=ALU.min))
                    seq.link(dve.tensor_scalar(firsti[:, :], firsti[:, :], 7, 7, op0=ALU.logical_shift_right,
                                               op1=ALU.logical_shift_left))
                    seq.link(dve.tensor_copy(firstf[:, :], firsti[:, :]))
                    seq.mark(dve.tensor_copy(src_f, src_t))
                    seq.link(dve.tensor_tensor(relv[:, :, :], dst_t, firstf[:, :].unsqueeze(2).broadcast_to([P, IC, P]),
                                               ALU.subtract))
                    dve.sem_inc(S("tof"), 1)
                    dve.tensor_copy(relb[:, :, :], relv[:, :, :]).then_inc(S("relb"), 1)
                    dve.wait_ge(S("first"), 32)
                    seq.mark(dve.tensor_scalar(blk[:, :], blk[:, :], 7, None, op0=ALU.logical_shift_right))
                    dve.wait_ge(S("consts"), 1)
                    dve.wait_ge(S("weights"), 1)
                    seq.mark(dve.tensor_scalar(att[:, 0:H], hmask[:, :], col["as"][:, :], None, op0=ALU.mult))
                    seq.mark(dve.tensor_scalar(att[:, H:2 * H], hmask[:, :], col["ad"][:, :], None, op0=ALU.mult))
                    seq.link(dve.tensor_scalar(W["gram"][:, :], ones[:, :], col["bg"][:, :], None, op0=ALU.mult))
                    dve.sem_inc(S("att"), 1)
                    for j in range(2 * IC):
                        dve.wait_ge(S("turned"), min(4 * (j // 4) + 4, 2 * IC))
                        seq.mark(dve.tensor_copy((relF if j < IC else srcI)[:, (j % IC) * P:(j % IC + 1) * P],
                                                 bank[j // 4][:, (j % 4) * P:(j % 4 + 1) * P]))
                    dve.wait_ge(S("bl"), 1)
                    seq.link(dve.scalar_tensor_tensor(row["blin"][:, :], bank[7][:, 0:P], ALPHA, row["blin"][:, :],
                                                      op0=ALU.mult, op1=ALU.add))

        def project():
            def S(name):
                return sem("proj", name)

            with nc.Block() as block:
                @block.tensor
                def _(pe):
                    pe.sem_inc(S("turned"), 1)
                    with pe.Fori(0, NCH) as c:
                        pe.wait_ge(S("res"), c + 1)
                        pe.transpose(bank[0][:, 0:P], res[:, 0, :], ident[:, :]).then_inc(S("turned"), 1)
                        for j in range(CB):
                            if j + 1 < CB:
                                t = pe.transpose(bank[(j + 1) % 2][:, 0:P], res[:, j + 1, :], ident[:, :])
                                t.then_inc(S("turned"), 1)
                            pe.wait_ge(S("xT"), c * CB + j + 1)
                            pe.wait_ge(S("out_free"), c * CB + j + (2 if j == 0 else 1))
                            pe.matmul(bank[2 + j % 2][:, 0:D + 2 * H], xT[:, j % 2, :], wA[:, :],
                                      start=True, stop=True).then_inc(S("out"), 1)
                    pe.wait_ge(S("top"), 1)
                    pe.transpose(bank[4][0:H, 0:P], top[:, 0:H], ident[:, :]).then_inc(S("topT"), 1)
                    pe.wait_ge(S("diag"), 1)
                    pe.matmul(bank[5][:, 0:H], ones[0:H, :], top[0:H, 2 * H:3 * H], start=True, stop=True).then_inc(S("gmax"), 1)

                @block.scalar
                def _(act):
                    with act.Fori(0, NCH) as c:
                        act.wait_ge(S("turned"), c * CB + 1)
                        act.activation(res[:, :, :], chunk(X, c), ACT.Copy).then_inc(S("res"), 1)
                        for j in range(CB):
                            act.wait_ge(S("turned"), c * CB + j + 2)
                            act.activation(xT[:, j % 2, :], bank[j % 2][:, 0:P], ACT.Copy).then_inc(S("xT"), 1)
                    act.wait_ge(S("selfz"), 1)
                    act.activation(selfw[:, :, :], own[:, :, :], ACT.Exp).then_inc(S("selfw"), 1)
                    act.wait_ge(S("selfw"), 1)

                @block.vector
                def _(dve):
                    seq = Chain(dve, S("dve"))
                    dve.sem_inc(S("out_free"), 2)
                    with dve.Fori(0, NCH) as c:
                        for j in range(CB):
                            dve.wait_ge(S("out"), c * CB + j + 1)
                            dve.tensor_copy(AB[:, bass.ds(c * CB + j, 1), 0:D + 2 * H],
                                            bank[2 + j % 2][:, 0:D + 2 * H].unsqueeze(1)).then_inc(S("out_free"), 1)
                    dve.wait_ge(S("out_free"), 2 + NB)
                    a_s, a_d = AB[:, 0:NB, D:D + H], AB[:, 0:NB, D + H:D + 2 * H]
                    dve.tensor_reduce(top[:, 0:H], a_s.rearrange("p b h -> p h b"), axis=AX.X, op=ALU.max).then_inc(S("top"), 1)
                    dve.wait_ge(S("topT"), 1)
                    seq.link(dve.tensor_reduce(top[0:H, H:H + 1], bank[4][0:H, 0:P], axis=AX.X, op=ALU.max))
                    dve.tensor_scalar(top[0:H, 2 * H:3 * H], ident[0:H, 0:H], top[0:H, H:H + 1], None,
                                      op0=ALU.mult).then_inc(S("diag"), 1)
                    seq.link(dve.tensor_tensor(own[:, :, :], a_s, a_d, ALU.add))
                    seq.mark(dve.scalar_tensor_tensor(own[:, :, :], own[:, :, :], SLOPE, own[:, :, :],
                                                      op0=ALU.mult, op1=ALU.max))
                    dve.wait_ge(S("gmax"), 1)
                    seq.link(dve.tensor_tensor(bound[:, :, :], a_d, bank[5][:, 0:H].unsqueeze(1).broadcast_to([P, NB, H]), ALU.add))
                    seq.link(dve.scalar_tensor_tensor(bound[:, :, :], bound[:, :, :], SLOPE, bound[:, :, :],
                                                      op0=ALU.mult, op1=ALU.max))
                    seq.link(dve.scalar_tensor_tensor(AB[:, 0:NB, D + 2 * H:D + 3 * H], bound[:, :, :], -RANGE, own[:, :, :],
                                                      op0=ALU.add, op1=ALU.max))
                    seq.link(dve.tensor_tensor(own[:, :, :], own[:, :, :], AB[:, 0:NB, D + 2 * H:D + 3 * H], ALU.subtract))
                    dve.sem_inc(S("selfz"), 1)
                    rest = AB[:, 0:NB, D + H:D + 3 * H]
                    left = tmp[:, :, :].rearrange("p c d -> p (c d)")[:, 0:NB * 2 * H].rearrange("p (b c) -> p b c", b=NB)
                    for part in range(3):
                        seq.link(dve.tensor_copy(parts[:, 0:NB, part, :], rest))
                        if part < 2:
                            seq.link(dve.tensor_tensor(left, rest, parts[:, 0:NB, part, :], ALU.subtract))
                            rest = left

                @block.sync
                def _(sp):
                    with sp.Fori(0, NCH) as c:
                        sp.wait_ge(S("out_free"), 2 + (c + 1) * CB)
                        sp.dma_start(table_rows(0, c), chunk(AB, c, slice(0, D + H))).then_inc(S("stored"), 16)
                    sp.wait_ge(S("stored"), 16 * NCH)

        def gather_all(pool, l, S, width, taken, before, extra):
            def gather(q, k, index):
                pool.indirect_dma_start(
                    out=rows[:, q * BT + k, 0:width], out_offset=None, in_=table[l],
                    in_offset=bass.IndirectOffsetOnAxis(ap=index, axis=0)).then_inc(S(f"landed{q}"), 16)

            for q in range(RB):
                for k in range(BT):
                    gather(q, k, srcI[:, q * BT + k:q * BT + k + 1])
            with pool.Fori(1, ITERS) as i:
                for q in range(RB):
                    pool.wait_ge(S("staged"), i * RB + q - (RB - 1))
                    pool.wait_ge(taken, i * RT + q * BT - (RT - BT) + before)
                    pass_gate(pool, S)
                    for k in range(BT):
                        gather(q, k, idx[:, q * BT + k:q * BT + k + 1])
            if extra:
                pool.wait_ge(S("staged"), ITERS * RB - (RB - 1))
                pool.wait_ge(taken, ITERS * RT - (RT - BT) + before)
                for k in range(BT):
                    gather(0, k, idx[:, k:k + 1])

        def stage_indices(act, S, i, q):
            act.activation(idx[:, q * BT:(q + 1) * BT], srcI[:, bass.ds(i * RT + (q + RB) * BT, BT)],
                           ACT.Copy).then_inc(S("staged"), 1)


        def mark_nodes(dve, S, tile, k):
            dve.tensor_scalar(onehot[:, k, :], iota[:, :], relF[:, bass.ds(tile, 1)], None,
                              op0=ALU.is_equal).then_inc(S("hot"), 1)

        def add_sums(dve, S, tile, k, block, width):
            dve.wait_ge(S("summed"), tile + 1)
            dve.wait_ge(S("added"), tile + 2)
            to = sums[:, bass.ds(block, 2), 0:width]
            dve.tensor_tensor(to, to, bank[4 + k % 2][:, 0:2 * width].rearrange("p (b c) -> p b c", b=2),
                              ALU.add).then_inc(S("added"), 1)

        def sum_tile(pe, S, tile, k, value, width):
            pe.wait_ge(S("added"), tile + 1)
            for b in range(2):
                m = pe.matmul(bank[4 + k % 2][:, b * width:(b + 1) * width], onehot[:, k, b * P:(b + 1) * P],
                              value, start=True, stop=True)
            m.then_inc(S("summed"), 1)


        def load_rel(sp, S):
            def load(s, q):
                sp.dma_start(relB[:, q, :], rel[bass.ds(s * BT * P, BT * P)].partition_broadcast(P)).then_inc(S(f"rel{q}"), 16)

            for q in range(RB):
                load(q, q)
            with sp.Fori(1, ITERS) as i:
                for q in range(RB):
                    sp.wait_ge(S("hotT"), (i * RB + q - (RB - 1)) * 2)
                    load(i * RB + q, q)
            for q in range(2):
                sp.wait_ge(S("hotT"), (ITERS * RB + q - (RB - 1)) * 2)
                load(ITERS * RB + q, q)

        def mark_edges(dve, S, to, s, q, rounds, b):
            if b == 0:
                dve.wait_ge(S(f"rel{q}"), rounds * 16)
                if not isinstance(s, int) or s > 1:
                    dve.wait_ge(S("spread"), (s - 1) * BT)
            dve.tensor_scalar(to[:, q % 2, b, :], relB[:, q, :], node[:, b:b + 1], None,
                              op0=ALU.is_equal).then_inc(S("hotT"), 1)

        def spread(pe, S, s, q, blocks, marks, values, width):
            pe.wait_ge(S("hotT"), 2 * s + 2)
            for k in range(BT):
                for b in range(2):
                    t = pe.matmul(bank[q % 2][:, k * width:(k + 1) * width], marks[:, q % 2, b, k * P:(k + 1) * P],
                                  values[:, bass.ds(blocks[k] + b, 1), :].rearrange("p o c -> p (o c)"),
                                  start=(b == 0), stop=(b == 1))
                t.then_inc(S("spread"), 1)

        def distance(act, S, t0, k, of, width):
            act.wait_ge(S("hot"), t0 + k + 1)
            act.activation(dist[:, k, 0:width], iota[:, 0:width], ACT.Abs, scale=-1.0,
                           bias=of[:, bass.ds(t0 + k, 1)]).then_inc(S("dist"), 1)

        def sum_in_bank(pe, S, k, hot, value, width):
            for b in range(2):
                m = pe.matmul(bank[4 + k][:, b * width:(b + 1) * width], hot[b], value, start=True, stop=True)
            m.then_inc(S("summed"), 1)

        def sum_zeros(pe, S, width):
            for k in range(BT):
                sum_in_bank(pe, S, k, [ident[:, :]] * 2, iota[:, 0:1].broadcast_to([P, width]), width)

        def add_tile(dve, S, after, k, block, width):
            dve.wait_ge(S("summed"), after + 1)
            dve.wait_ge(S("added"), after + 1)
            to = sums[:, bass.ds(block, 2), 0:width]
            dve.tensor_tensor(to, to, bank[4 + k][:, 0:2 * width].rearrange("p (b c) -> p b c", b=2),
                              ALU.add).then_inc(S("added"), 1)

        def edges0():
            def S(name):
                return sem("e0", name)

            split = parts[:, :, :, :].rearrange("p b s c -> p b (s c)")

            with nc.Block() as block:
                @block.gpsimd
                def _(pool):
                    gather_all(pool, 0, S, D + H, S("msgs"), 0, True)

                @block.sync
                def _(sp):
                    load_rel(sp, S)

                @block.tensor
                def _(pe):
                    sum_zeros(pe, S, WS)
                    blks = first_blocks(pe, BT, 2 * BT)
                    for q in range(2):
                        spread(pe, S, q, q, blks[q * BT:(q + 1) * BT], onehotTb, split, 6 * H)
                    with pe.Fori(0, ITERS) as i:
                        first = first_blocks(pe, i * RT + 3 * BT, RT)
                        for q in range(RB):
                            t0, m = i * RT + q * BT, (q % 2) * BT
                            pe.wait_ge(S("scored"), i * RB + q + 1)
                            spread(pe, S, i * RB + q + 2, q, first[q * BT:(q + 1) * BT], onehotTb, split, 6 * H)
                            for k in range(BT):
                                pe.wait_ge(S("hot"), t0 + k + 1 + BT)
                                pe.wait_ge(S("msgs"), t0 + k + 1)
                                pe.wait_ge(S("added"), t0 + k + 2)
                                sum_in_bank(pe, S, k, [onehot[:, m + k, b * P:(b + 1) * P] for b in range(2)], msg[:, m + k, :], WS)

                @block.scalar
                def _(act):
                    def weights_and_onehot(s, q):
                        m = (q % 2) * BT
                        act.wait_ge(S("scored"), s + 1)
                        if not isinstance(s, int):
                            act.wait_ge(S("summed"), s * BT)
                        act.activation(msg[:, m:m + BT, D:D + H], score[:, q % 2, :, :], ACT.Exp).then_inc(S("weighed"), 1)
                        for k in range(2):
                            distance(act, S, s * BT, k, relF, 2 * P)
                        for k in range(BT):
                            if k + 2 < BT:
                                distance(act, S, s * BT, k + 2, relF, 2 * P)
                            act.wait_ge(S("dist"), s * BT + k + 1)
                            act.activation(onehot[:, m + k, :], dist[:, k, :], ACT.Relu, scale=-1.0,
                                           bias=ones[:, 0:1]).then_inc(S("hot"), 1)

                    act.sem_inc(S("hot"), BT)
                    weights_and_onehot(0, 0)
                    with act.Fori(0, ITERS) as i:
                        for q in range(RB):
                            weights_and_onehot(i * RB + q + 1, (q + 1) % RB)
                            stage_indices(act, S, i, q)

                @block.vector
                def _(dve):
                    dve.sem_inc(S("added"), 1)
                    seq = Chain(dve, S("dve"))

                    def scores(s, q, rounds, step):
                        sc, a_s = score[:, q % 2, :, :], rows[:, q * BT:(q + 1) * BT, D:D + H]
                        of_dst = ofdst[:, :, :]
                        if step == 0:
                            dve.wait_ge(S("spread"), s * BT + BT)
                            if not isinstance(s, int):
                                dve.wait_ge(S("scored"), s)
                            seq.mark(dve.tensor_reduce(of_dst, bank[q % 2][:, 0:BT * 6 * H].rearrange("p (k s c) -> p k c s", k=BT, s=3),
                                                       axis=AX.X, op=ALU.add))
                        if step == 1:
                            seq.wait()
                            dve.wait_ge(S(f"landed{q}"), rounds * 16 * BT)
                            seq.mark(dve.tensor_tensor(sc, a_s, of_dst[:, :, 0:H], ALU.add))
                        if step == 2:
                            seq.wait()
                            seq.mark(dve.scalar_tensor_tensor(sc, sc, SLOPE, sc, op0=ALU.mult, op1=ALU.max))
                        if step == 3:
                            seq.wait()
                            dve.tensor_tensor(sc, sc, of_dst[:, :, H:2 * H], ALU.subtract).then_inc(S("scored"), 1)

                    for q in range(2):
                        for b in range(2):
                            mark_edges(dve, S, onehotTb, q, q, 1, b)
                    for step in range(4):
                        scores(0, 0, 1, step)
                    with dve.Fori(0, ITERS) as i:
                        seq.enter(i, 3 * RB)
                        first = first_blocks(dve, i * RT, RT)
                        for q in range(RB):
                            t0, m = i * RT + q * BT, (q % 2) * BT
                            scored = i * RB + q + 1, (q + 1) % RB, i + (1 if q + 1 < RB else 2)
                            marked = i * RB + q + 2, (q + 2) % RB, i + (1 if q + 2 < RB else 2)

                            def message(k):
                                if k == 0:
                                    dve.wait_ge(S("weighed"), i * RB + q + 1)
                                w = msg[:, m + k, D:D + H].unsqueeze(2).broadcast_to([P, H, HC])
                                dve.tensor_tensor(msg[:, m + k, 0:D].rearrange("p (h c) -> p h c", h=H),
                                                  rows[:, q * BT + k, 0:D].rearrange("p (h c) -> p h c", h=H), w,
                                                  ALU.mult).then_inc(S("msgs"), 1)

                            scores(*scored, 0)
                            mark_edges(dve, S, onehotTb, *marked, 0)
                            scores(*scored, 1)
                            mark_edges(dve, S, onehotTb, *marked, 1)
                            scores(*scored, 2)
                            for k in range(BT):
                                if k == 1:
                                    scores(*scored, 3)
                                add_tile(dve, S, t0 + k, k, first[q * BT + k], WS)
                                message(k)
                        seq.leave(ITERS)
                    blks = first_blocks(dve, ITERS * RT, BT)
                    for k in range(BT):
                        add_tile(dve, S, ITERS * RT + k, k, blks[k], WS)

        def nodes0():
            def S(name):
                return sem("n0", name)

            PAIRS = -(-CB // 2)

            with nc.Block() as block:
                @block.vector
                def _(dve):
                    seq = Chain(dve, S("dve"))

                    def sums_to_x(c, h):
                        t = tmps[h]
                        acc, w0 = chunk(sums, c, slice(0, D)), chunk(selfw, c)
                        dve.wait_ge(S("res"), (c + 1) * CB)
                        seq.mark(dve.tensor_tensor(den, chunk(sums, c, slice(D, D + H)), w0, ALU.add))
                        for_heads = t.rearrange("p b (h c) -> p b h c", h=H)
                        dve.wait_ge(S("own_part"), c + 1)
                        seq.link(dve.tensor_tensor(t, chunk(AB, c, slice(0, D)), acc, ALU.add))
                        seq.mark(dve.reciprocal(den, den))
                        dve.tensor_copy(degree[:, bass.ds(c * CB, CB)].unsqueeze(2), chunk(sums, c, slice(WS - 1, WS))).then_inc(S("sums_used"), 1)
                        seq.wait()
                        seq.link(dve.tensor_tensor(for_heads, for_heads, den.unsqueeze(3).broadcast_to([P, CB, H, HC]), ALU.mult))
                        seq.link(dve.tensor_tensor(t, t, row["bias"][:, :].unsqueeze(1).broadcast_to([P, CB, D]), ALU.add))
                        seq.link(dve.scalar_tensor_tensor(t, t, 0.0, chunk(X, c), op0=ALU.max, op1=ALU.add))
                        moments(dve, seq, S, h, CB)
                        scale_and_shift(dve, seq, S, c, h, CB, valid[:, bass.ds(c * CB, CB)])

                    in_turn_counted(dve, seq, 6 + 2 * CB - 1 + 2, sums_to_x)

                @block.gpsimd
                def _(pool):
                    pool.sem_inc(S("kept"), 2)

                    def own_part(c):
                        xw = chunk(AB, c, slice(0, D)).rearrange("p b (h c) -> p b h c", h=H)
                        pool.tensor_tensor(xw, xw, chunk(selfw, c).unsqueeze(3).broadcast_to([P, CB, H, HC]),
                                           ALU.mult).then_inc(S("own_part"), 1)

                    def keep(c, h):
                        pool.wait_ge(S("res"), (c + 3) * CB)
                        pool.tensor_copy(chunk(X, c), ress[h]).then_inc(S("kept"), 1)

                    own_part(0)
                    with pool.Fori(0, NCH // 2) as g:
                        for h in range(2):
                            own_part(g * 2 + h + 1)
                            keep(g * 2 + h, h)
                    keep(NCH - 1, 0)
                    pool.wait_ge(S("kept"), NCH + 2)

                @block.tensor
                def _(pe):
                    pe.sem_inc(S("turned"), 4)
                    pe.sem_inc(S("out"), 1)

                    def step(c, h):
                        turn_chunk(pe, S, c, h, ress, "res", 2 * CB)
                        for p in range(PAIRS):
                            pe.wait_ge(S("xT"), c * 2 + p // 2 + 3)
                            pe.wait_ge(S("ab"), c * PAIRS + p + 1)
                            for j in range(2 * p, min(2 * p + 2, CB)):
                                to = bank[2 + p][:, (j % 2) * 2 * D:(j % 2 + 1) * 2 * D]
                                t = pe.matmul(to, xTs[:, j, :], wB[:, :], start=True, stop=True)
                            t.then_inc(S("out"), 1)
                    in_turn(pe, step)

                @block.scalar
                def _(act):
                    act.sem_inc(S("ab"), PAIRS)
                    act.sem_inc(S("xT"), 2)
                    act.sem_inc(S("res"), 2 * CB)

                    def step(c, h):
                        root(act, S, c, h, CB)
                        act.wait_ge(S("turned"), c * 2 + 2)
                        act.wait_ge(S("kept"), c + 1)
                        pass_gate(act, S)
                        apply(act, S, c, h, CB, lambda j: ress[h][:, j:j + 1, :], "res")
                        take_chunk(act, S, c, PAIRS)
                        act.wait_ge(S("sums_used"), c + 1)
                        act.activation(chunk(sums, c), zeros(CB, WS), ACT.Copy).then_inc(S("cleared"), 1)

                    def to_AB(c):
                        for p in range(PAIRS):
                            n = min(2, CB - 2 * p)
                            act.wait_ge(S("out"), c * PAIRS + p + 2)
                            act.activation(AB[:, bass.ds(c * CB + 2 * p, n), :], bank[2 + p][:, 0:n * 2 * D].rearrange("p (b c) -> p b c", b=n),
                                           ACT.Copy).then_inc(S("ab"), 1)

                    step(0, 0)
                    with act.Fori(0, NCH // 2) as g:
                        for h in (1, 0):
                            step(g * 2 + 2 - h, h)
                            to_AB(g * 2 + 1 - h)
                    to_AB(NCH - 1)

                @block.sync
                def _(sp):
                    with sp.Fori(0, NCH) as c:
                        sp.wait_ge(S("kept"), c + 3)
                        sp.dma_start(table_rows(1, c)[:, :, D:2 * D], chunk(X, c)).then_inc(S("stored"), 16)
                        sp.wait_ge(S("ab"), (c + 2) * PAIRS)
                        sp.dma_start(table_rows(1, c)[:, :, 0:D], chunk(AB, c, slice(0, D))).then_inc(S("stored"), 16)
                    sp.wait_ge(S("stored"), 2 * 16 * NCH)

        def edges1():
            def S(name):
                return sem("e1", name)

            with nc.Block() as block:
                @block.gpsimd
                def _(pool):
                    gather_all(pool, 1, S, 2 * D, S("summed"), BT, True)

                @block.sync
                def _(sp):
                    load_rel(sp, S)

                @block.tensor
                def _(pe):
                    sum_zeros(pe, S, D + 1)
                    blks = first_blocks(pe, BT, 2 * BT)
                    pe.wait_ge(S("b1"), 1)
                    for q in range(2):
                        spread(pe, S, q, q, blks[q * BT:(q + 1) * BT], onehotT, AB[:, :, 0:D], D)
                    with pe.Fori(0, ITERS) as i:
                        first = first_blocks(pe, i * RT + 3 * BT, RT)
                        for q in range(RB):
                            t0, m = i * RT + q * BT, (q % 2) * BT
                            pe.wait_ge(S("scored"), t0 + BT)
                            spread(pe, S, i * RB + q + 2, q, first[q * BT:(q + 1) * BT], onehotT, AB[:, :, 0:D], D)
                            for k in range(BT):
                                pe.wait_ge(S("hot"), t0 + k + 1 + BT)
                                pe.wait_ge(S("added"), t0 + k + 2)
                                sum_in_bank(pe, S, k, [onehot[:, m + k, b * P:(b + 1) * P] for b in range(2)],
                                            rows[:, q * BT + k, D:2 * D + 1], D + 1)

                @block.scalar
                def _(act):
                    def gates_and_onehot(s, q):
                        m = (q % 2) * BT
                        gate = score[:, q % 2, :, 0]
                        distance(act, S, s * BT, 0, relF, 2 * P)
                        distance(act, S, s * BT, 1, relF, 2 * P)
                        act.wait_ge(S("scored"), s * BT + BT)
                        act.activation(gate, logit[:, q % 2, :], ACT.Sigmoid, bias=col["b2"][:, :]).then_inc(S("gated"), 1)
                        distance(act, S, s * BT, 2, relF, 2 * P)
                        act.wait_ge(S("gated"), 2 * s + 3)
                        act.activation(minus[:, :], gate, ACT.Copy, scale=-1.0).then_inc(S("gated"), 1)
                        distance(act, S, s * BT, 3, relF, 2 * P)
                        act.wait_ge(S("gated"), 2 * s + 4)
                        if not isinstance(s, int):
                            act.wait_ge(S("summed"), s * BT)
                        for k in range(BT):
                            act.wait_ge(S("dist"), s * BT + k + 1)
                            act.activation(onehot[:, m + k, :], dist[:, k, :], ACT.Relu, scale=minus[:, k:k + 1],
                                           bias=gate[:, k:k + 1]).then_inc(S("hot"), 1)

                    act.sem_inc(S("hot"), BT)
                    act.sem_inc(S("gated"), 2)
                    gates_and_onehot(0, 0)
                    with act.Fori(0, ITERS) as i:
                        for q in range(RB):
                            gates_and_onehot(i * RB + q + 1, (q + 1) % RB)
                            stage_indices(act, S, i, q)

                @block.vector
                def _(dve):
                    dve.sem_inc(S("added"), 1)
                    seq = Chain(dve, S("dve"))

                    def difference(s, q, rounds):
                        dve.wait_ge(S("spread"), s * BT + BT)
                        dve.wait_ge(S(f"landed{q}"), rounds * 16 * BT)
                        seq.mark(dve.tensor_tensor(diff[:, q % 2, :, :], bank[q % 2][:, :].rearrange("p (k c) -> p k c", k=BT),
                                                   rows[:, q * BT:(q + 1) * BT, 0:D], ALU.subtract))

                    def logit_of(s, q, k):
                        if k == 0:
                            seq.wait()
                            if not isinstance(s, int):
                                dve.wait_ge(S("gated"), 2 * s - 1)
                        d = diff[:, q % 2, k, :]
                        dve.scalar_tensor_tensor(d, d, 0.0, row["w2"][:, :], op0=ALU.max, op1=ALU.mult,
                                                 accum_out=logit[:, q % 2, k:k + 1]).then_inc(S("scored"), 1)

                    dve.tensor_tensor(AB[:, 0:NB, 0:D], AB[:, 0:NB, 0:D], row["b1"][:, :].unsqueeze(1).broadcast_to([P, NB, D]),
                                      ALU.add).then_inc(S("b1"), 1)
                    for q in range(2):
                        for b in range(2):
                            mark_edges(dve, S, onehotT, q, q, 1, b)
                    difference(0, 0, 1)
                    for k in range(BT):
                        logit_of(0, 0, k)
                    with dve.Fori(0, ITERS) as i:
                        seq.enter(i, RB)
                        first = first_blocks(dve, i * RT, RT)
                        for q in range(RB):
                            t0, s, qn = i * RT + q * BT, i * RB + q + 1, (q + 1) % RB
                            marked = s + 1, (q + 2) % RB, i + (1 if q + 2 < RB else 2)

                            def add(k):
                                add_tile(dve, S, t0 + k, k, first[q * BT + k], D + 1)

                            add(0)
                            mark_edges(dve, S, onehotT, *marked, 0)
                            add(1)
                            mark_edges(dve, S, onehotT, *marked, 1)
                            difference(s, qn, i + (1 if q + 1 < RB else 2))
                            add(2)
                            logit_of(s, qn, 0)
                            logit_of(s, qn, 1)
                            add(3)
                            logit_of(s, qn, 2)
                            logit_of(s, qn, 3)
                        seq.leave(ITERS)
                    blks = first_blocks(dve, ITERS * RT, BT)
                    for k in range(BT):
                        add_tile(dve, S, ITERS * RT + k, k, blks[k], D + 1)

        def nodes1():
            def S(name):
                return sem("n1", name)

            with nc.Block() as block:
                @block.vector
                def _(dve):
                    seq = Chain(dve, S("dve"))
                    dve.tensor_copy(dinv[:, :], degree[:, :]).then_inc(S("deg"), 1)
                    dve.wait_ge(S("rootdeg"), 1)
                    seq.link(dve.reciprocal(dinv[:, :], dinv[:, :]))

                    def sums_to_x(c, h):
                        t = tmps[h]
                        dve.wait_ge(S("res"), (c + 1) * CB)
                        seq.link(dve.scalar_tensor_tensor(t, chunk(sums, c, slice(D, D + 1)).broadcast_to([P, CB, D]), 1.0, chunk(X, c),
                                                          op0=ALU.add, op1=ALU.mult))
                        dve.tensor_tensor(t, t, chunk(sums, c, slice(0, D)), ALU.subtract).then_inc(S("sums_used"), 1)
                        dve.wait_ge(S("sums_used"), c + 1)
                        dve.wait_ge(S("times_degree"), c + 1)
                        seq.link(dve.tensor_tensor(t, t, chunk(AB, c, slice(D, 2 * D)), ALU.add))
                        moments(dve, seq, S, h, CB)
                        scale_and_shift(dve, seq, S, c, h, CB, valid[:, bass.ds(c * CB, CB)])

                    in_turn_counted(dve, seq, 2 + 2 * CB - 1 + 2, sums_to_x)

                @block.gpsimd
                def _(pool):
                    pool.sem_inc(S("kept"), 2)

                    def times_degree(c):
                        r4 = chunk(AB, c, slice(D, 2 * D))
                        pool.tensor_tensor(r4, r4, row["b4"][:, :].unsqueeze(1).broadcast_to([P, CB, D]), ALU.add).then_inc(S("b4"), 1)
                        pool.wait_ge(S("b4"), c + 1)
                        pool.tensor_tensor(r4, r4, degree[:, bass.ds(c * CB, CB)].unsqueeze(2).broadcast_to([P, CB, D]),
                                           ALU.mult).then_inc(S("times_degree"), 1)

                    def keep(c, h):
                        pool.wait_ge(S("res"), (c + 3) * CB)
                        pool.tensor_copy(chunk(X, c), ress[h]).then_inc(S("kept"), 1)

                    times_degree(0)
                    with pool.Fori(0, NCH // 2) as g:
                        for h in range(2):
                            times_degree(g * 2 + h + 1)
                            keep(g * 2 + h, h)
                    keep(NCH - 1, 0)
                    pool.wait_ge(S("kept"), NCH + 2)

                @block.tensor
                def _(pe):
                    zero = iota[:, 0:1].broadcast_to([P, P])
                    pe.matmul(bank[6][:, 0:P], ident[:, :], zero, start=True, stop=False, skip_group_check=True)
                    pe.matmul(bank[7][:, 0:1], ident[:, :], iota[:, 0:1], start=True, stop=False, skip_group_check=True)
                    pe.sem_inc(S("gram_used"), 2)

                    def step(c, h):
                        for j in range(CB):
                            pe.wait_ge(S("res"), (c + 2) * CB + j + 1)
                            pe.matmul(bank[6][:, 0:P], ress[h][:, j, :], ress[h][:, j, :], start=False, stop=False, skip_group_check=True)
                            t = pe.matmul(bank[7][:, 0:1], ress[h][:, j, :], ones[:, 0:1], start=False, stop=False, skip_group_check=True)
                        t.then_inc(S("gram_used"), 1)
                    in_turn(pe, step)
                    pe.matmul(bank[6][:, 0:P], ident[:, :], zero, start=False, stop=True, skip_group_check=True)
                    pe.matmul(bank[7][:, 0:1], ident[:, :], iota[:, 0:1], start=False, stop=True, skip_group_check=True).then_inc(S("gram"), 1)
                    pe.wait_ge(S("gram"), 1)

                @block.scalar
                def _(act):
                    act.sem_inc(S("res"), 2 * CB)
                    act.wait_ge(S("deg"), 1)
                    act.activation(dinv[:, :], dinv[:, :], ACT.Sqrt, bias=ones[:, 0:1]).then_inc(S("rootdeg"), 1)

                    def step(c, h):
                        root(act, S, c, h, CB)
                        act.wait_ge(S("gram_used"), c + 1)
                        act.wait_ge(S("kept"), c + 1)
                        pass_gate(act, S)
                        apply(act, S, c, h, CB, lambda j: ress[h][:, j:j + 1, :], "res")
                        act.wait_ge(S("sums_used"), c + 1)
                        act.activation(chunk(sums, c), zeros(CB, WS), ACT.Copy).then_inc(S("cleared"), 1)
                        for j in range(CB):
                            act.wait_ge(S("res"), (c + 2) * CB + j + 1)
                            act.activation(AB[:, bass.ds(c * CB + j, 1), D:2 * D], ress[h][:, j:j + 1, :], ACT.Copy,
                                           scale=dinv[:, bass.ds(c * CB + j, 1)]).then_inc(S("scaled"), 1)
                    in_turn(act, step)

                @block.sync
                def _(sp):
                    with sp.Fori(0, NCH) as c:
                        sp.wait_ge(S("scaled"), (c + 1) * CB)
                        sp.dma_start(table_rows(2, c), chunk(AB, c, slice(D, 2 * D))).then_inc(S("stored"), 16)
                    sp.wait_ge(S("stored"), 16 * NCH)

        def plain_edge_loops(S, l, before, beside):
            def loop(name, eng, body):
                before(name, eng)
                if name == "dve":
                    eng.sem_inc(S("added"), 2)
                    for k in range(BT):
                        mark_nodes(eng, S, k, k)
                if beside:
                    with eng.Fori(0, NB) as i:
                        body(i, lambda q: beside(name, eng, i, q))
                with eng.Fori(NB if beside else 0, ITERS) as i:
                    body(i, lambda q: None)

            with nc.Block() as block:
                @block.gpsimd
                def _(pool):
                    gather_all(pool, l, S, D, S("summed"), 0, False)

                @block.tensor
                def _(pe):
                    def body(i, also):
                        for q in range(RB):
                            t0, m = i * RT + q * BT, (q % 2) * BT
                            also(q)
                            pe.wait_ge(S(f"landed{q}"), (i + 1) * 16 * BT)
                            for k in range(BT):
                                pe.wait_ge(S("hot"), t0 + k + 1)
                                sum_tile(pe, S, t0 + k, m + k, rows[:, q * BT + k, 0:D], D)
                    loop("pe", pe, body)

                @block.scalar
                def _(act):
                    def body(i, also):
                        for q in range(RB):
                            act.wait_ge(S(f"landed{q}"), (i + 1) * 16 * BT)
                            stage_indices(act, S, i, q)
                            also(q)
                    loop("act", act, body)

                @block.vector
                def _(dve):
                    def body(i, also):
                        first = first_blocks(dve, BT + i * RT, RT)
                        for q in range(RB):
                            t0, m = i * RT + q * BT, (q % 2) * BT
                            also(q)
                            for k in range(BT):
                                mark_nodes(dve, S, t0 + BT + k, (BT - m) + k)
                                add_sums(dve, S, t0 + k, m + k, first[q * BT + k], D)
                    loop("dve", dve, body)

        def edges2():
            def S(name):
                return sem("e2", name)

            def mix_pe(pe):
                pe.wait_ge(S("gram_sb"), 2)
                for b, k in enumerate("qkv"):
                    t = pe.matmul(bank[0][:, b * P:(b + 1) * P], W["gram"][:, :], W[k][:, :], start=True, stop=True)
                t.then_inc(S("gw"), 1)
                pe.matmul(bank[1][:, 0:1], W["KQ"][:, :], sx[:, :], start=True, stop=True).then_inc(S("u"), 1)
                pe.wait_ge(S("squares"), 2)
                pe.matmul(bank[2][:, 0:2], ones[:, :], scal[:, 0:2], start=True, stop=True).then_inc(S("norms"), 1)
                pe.wait_ge(S("gv"), 1)
                pe.matmul(bank[3][:, 0:P], W["KQ"][:, :], W["gv"][:, :], start=True, stop=True).then_inc(S("kv"), 1)
                pe.wait_ge(S("attn"), 1)
                pe.transpose(bank[4][:, 0:P], W["t"][:, :], ident[:, :]).then_inc(S("attnT"), 1)
                pe.wait_ge(S("attnT_sb"), 1)
                pe.matmul(bank[5][:, 0:P], W["gv"][:, :], W["linT"][:, :], start=True, stop=True).then_inc(S("wx"), 1)
                pe.wait_ge(S("wX"), 2)
                pe.sem_inc(S("turned"), 1)

            def mix_act(act):
                act.activation(W["gram"][:, :], bank[6][:, 0:P], ACT.Copy).then_inc(S("gram_sb"), 1)
                act.activation(sx[:, :], bank[7][:, 0:1], ACT.Copy).then_inc(S("gram_sb"), 1)
                act.wait_ge(S("squares"), 2)
                act.activation(W["gv"][:, :], bank[0][:, 2 * P:3 * P], ACT.Copy).then_inc(S("gv"), 1)
                act.wait_ge(S("norms"), 1)
                act.activation(scal[:, 2:4], bank[2][:, 0:2], ACT.Sqrt).then_inc(S("roots"), 1)
                act.wait_ge(S("attnT"), 1)
                act.activation(W["gv"][:, :], bank[4][:, 0:P], ACT.Copy).then_inc(S("attnT_sb"), 1)
                act.wait_ge(S("wx"), 1)
                act.activation(wX[:, 0:D], bank[5][:, 0:P], ACT.Copy, scale=BETA * (1 - ALPHA)).then_inc(S("wX"), 1)

            def mix_dve(dve):
                seq = Chain(dve, S("dve"))
                seq.mark(dve.scalar_tensor_tensor(wX[:, D:2 * D], W["linT"][:, :], (1 - BETA) * (1 - ALPHA), ident[:, :],
                                                  op0=ALU.mult, op1=ALU.add))
                dve.wait_ge(S("gw"), 1)
                for b, k in enumerate("qk"):
                    dve.scalar_tensor_tensor(tmp[:, b, :], bank[0][:, b * P:(b + 1) * P], 1.0, W[k][:, :], op0=ALU.mult,
                                             op1=ALU.mult, accum_out=scal[:, b:b + 1]).then_inc(S("squares"), 1)
                dve.wait_ge(S("roots"), 1)
                seq.link(dve.scalar_tensor_tensor(scal[:, 4:5], scal[:, 2:3], float(D), scal[:, 3:4], op0=ALU.mult, op1=ALU.mult))
                seq.link(dve.reciprocal(scal[:, 5:6], scal[:, 4:5]))
                dve.wait_ge(S("u"), 1)
                seq.mark(dve.tensor_scalar(wX[:, 2 * D:2 * D + 1], bank[1][:, 0:1], scal[:, 5:6], None, op0=ALU.mult))
                dve.wait_ge(S("kv"), 1)
                seq.link(dve.scalar_tensor_tensor(W["t"][:, :], bank[3][:, 0:P], scal[:, 5:6], W["v"][:, :],
                                                  op0=ALU.mult, op1=ALU.add))
                dve.sem_inc(S("attn"), 1)
                dve.sem_inc(S("wX"), 1)
                dve.sem_inc(S("combined"), 1)

            def before(name, eng):
                {"pe": mix_pe, "act": mix_act, "dve": mix_dve}[name](eng)

            def terms_in_x(name, eng, b, q):
                if name == "act":
                    if q == 0:
                        eng.wait_ge(S("turned"), b + 1)
                        eng.activation(res[:, 0:1, :], X[:, bass.ds(b, 1), :], ACT.Copy).then_inc(S("res"), 1)
                    if q == 1:
                        eng.wait_ge(S("turned"), b + 2)
                        eng.activation(xT[:, 0, :], bank[0][:, 0:P], ACT.Copy).then_inc(S("xT"), 1)
                    if q == 2:
                        eng.wait_ge(S("out"), b + 1)
                        eng.activation(AB[:, bass.ds(b, 1), 0:D], bank[1][:, D:2 * D].unsqueeze(1), ACT.Copy).then_inc(S("lin"), 1)
                if name == "pe":
                    if q == 1:
                        eng.wait_ge(S("res"), b + 1)
                        eng.transpose(bank[0][:, 0:P], res[:, 0, :], ident[:, :]).then_inc(S("turned"), 1)
                    if q == 2:
                        eng.wait_ge(S("xT"), b + 1)
                        eng.wait_ge(S("combined"), b + 1)
                        eng.matmul(bank[1][:, 0:2 * D + 1], xT[:, 0, :], wX[:, 0:2 * D + 1], start=True, stop=False,
                                   skip_group_check=True)
                        eng.matmul(bank[1][:, D:2 * D], ones[0:1, :], row["blin"][0:1, :], start=False, stop=True,
                                   skip_group_check=True).then_inc(S("out"), 1)
                if name == "dve" and q == 3:
                    eng.wait_ge(S("lin"), b + 1)
                    eng.tensor_scalar(scal[:, 6:7], bank[1][:, 2 * D:2 * D + 1], 1.0, None, op0=ALU.add).then_inc(S("scale"), 1)
                    eng.wait_ge(S("scale"), 2 * b + 1)
                    eng.reciprocal(scal[:, 7:8], scal[:, 6:7]).then_inc(S("scale"), 1)
                    eng.wait_ge(S("scale"), 2 * b + 2)
                    to = AB[:, bass.ds(b, 1), 0:D]
                    eng.scalar_tensor_tensor(to, bank[1][:, 0:D].unsqueeze(1), scal[:, 7:8], to, op0=ALU.mult,
                                             op1=ALU.add).then_inc(S("combined"), 1)

            plain_edge_loops(S, 2, before, terms_in_x)

        def nodes2():
            def S(name):
                return sem("n2", name)

            HALVES = ((0, 4), (4, CB))

            with nc.Block() as block:
                @block.vector
                def _(dve):
                    seq = Chain(dve, S("dve"))

                    def gcn_input(c, h):
                        dve.wait_ge(S("turned"), c * 2 + 2)
                        dve.tensor_tensor(ress[h], chunk(sums, c, slice(0, D)), chunk(AB, c, slice(D, 2 * D)),
                                          ALU.add).then_inc(S("gcn_in"), 1)

                    def add_gcn(c, h):
                        dve.wait_ge(S("res"), (c + 1) * CB)
                        for b, (lo, hi) in enumerate(HALVES):
                            dve.wait_ge(S("out"), c * 2 + b + 2)
                            if b == 0:
                                pass_gate(dve, S)
                            for j in range(lo, hi):
                                seq.mark(dve.scalar_tensor_tensor(
                                    tmps[h][:, j:j + 1, :], bank[2 + 2 * h + b][:, (j - lo) * D:(j - lo + 1) * D].unsqueeze(1),
                                    dinv[:, bass.ds(c * CB + j, 1)], AB[:, bass.ds(c * CB + j, 1), 0:D], op0=ALU.mult, op1=ALU.add))
                        seq.wait()
                        dve.sem_inc(S("out_used"), 1)
                        moments(dve, seq, S, h, CB)

                    def step(c, h, more):
                        add_gcn(c, h)
                        if more:
                            gcn_input(c + 2, h)
                        scale_and_shift(dve, seq, S, c, h, CB, valid[:, bass.ds(c * CB, CB)])

                    gcn_input(0, 0)
                    gcn_input(1, 1)
                    with dve.Fori(0, (NCH - 3) // 2) as g:
                        seq.enter(g, 2 * (3 * CB - 1 + 2))
                        step(g * 2, 0, True)
                        step(g * 2 + 1, 1, True)
                        seq.leave((NCH - 3) // 2)
                    step(NCH - 3, 0, True)
                    step(NCH - 2, 1, False)
                    step(NCH - 1, 0, False)

                @block.gpsimd
                def _(pool):
                    with pool.Fori(0, NCH) as c:
                        pool.wait_ge(S("gcn_in"), c + 1)
                        pool.tensor_copy(chunk(sums, c), zeros(CB, WS)).then_inc(S("cleared"), 1)
                    pool.wait_ge(S("cleared"), NCH)

                @block.tensor
                def _(pe):
                    pe.sem_inc(S("turned"), 4)
                    pe.sem_inc(S("out"), 1)

                    def step(c, h):
                        pe.wait_ge(S("gcn_in"), c + 1)
                        pass_gate(pe, S)
                        turn_chunk(pe, S, c, h, ress, None)
                        pe.wait_ge(S("out_used"), c + 1)
                        pass_gate(pe, S)
                        for b, (lo, hi) in enumerate(HALVES):
                            pe.wait_ge(S("xT"), c * 2 + b + 3)
                            for j in range(lo, hi):
                                t = pe.matmul(bank[2 + 2 * h + b][:, (j - lo) * D:(j - lo + 1) * D], xTs[:, j, :], wG[:, :],
                                              start=True, stop=True)
                            t.then_inc(S("out"), 1)
                    in_turn(pe, step)

                @block.scalar
                def _(act):
                    act.sem_inc(S("xT"), 2)
                    act.sem_inc(S("res"), 2 * CB)
                    act.sem_inc(S("out_used"), 2)

                    def normal(c, h):
                        root(act, S, c, h, CB)
                        apply(act, S, c, h, CB, lambda j: X[:, bass.ds(c * CB + j, 1), :], "res")

                    take_chunk(act, S, 0, 2)
                    take_chunk(act, S, 1, 2)
                    with act.Fori(0, (NCH - 3) // 2) as g:
                        for h in range(2):
                            normal(g * 2 + h, h)
                            take_chunk(act, S, g * 2 + h + 2, 2)
                    normal(NCH - 3, 0)
                    take_chunk(act, S, NCH - 1, 2)
                    normal(NCH - 2, 1)
                    normal(NCH - 1, 0)

                @block.sync
                def _(sp):
                    with sp.Fori(0, NCH) as c:
                        sp.wait_ge(S("res"), (c + 3) * CB)
                        sp.dma_start(table_rows(3, c), chunk(X, c)).then_inc(S("stored"), 16)
                    sp.wait_ge(S("stored"), 16 * NCH)

        def edges3():
            plain_edge_loops(lambda name: sem("e3", name), 3, lambda name, eng: None, None)

        def nodes3():
            def S(name):
                return sem("n3", name)

            def products(eng, step):
                with eng.Fori(0, NFM // 2) as g:
                    step(g * 2, FM, 0)
                    step(g * 2 + 1, FM, 1)
                step(NFM, FREST, 0)

            HALVES = ((0, 4), (4, CB))
            relu = [msg[:, :, :].rearrange("p k c -> p (k c)")[:, 0:CB * P].rearrange("p (b c) -> p b c", b=CB), xTs]

            with nc.Block() as block:
                @block.vector
                def _(dve):
                    seq = Chain(dve, S("dve"))

                    def batch_stats(layer):
                        def step(m, width, b):
                            dve.wait_ge(S("y" + layer), 2 + m + 1)
                            dve.bn_stats(bnst[:, bass.ds(m, 1), :].rearrange("p o c -> p (o c)"),
                                         HT[1][:, bass.ds(m * FM, width)]).then_inc(S("st" + layer), 1)
                        products(dve, step)
                        dve.wait_ge(S("st" + layer), NFM + 1)
                        dve.bn_aggr(bnmv[:, 0:2], bnst[:, :, :]).then_inc(S("bnvar" + layer), 1)
                        dve.wait_ge(S("bnroot" + layer), 1)
                        seq.link(dve.reciprocal(bnmv[:, 3:4], bnmv[:, 2:3]))
                        seq.link(dve.tensor_tensor(bnmv[:, 4:5], bnmv[:, 3:4], col["g" + layer][:, :], ALU.mult))
                        seq.link(dve.tensor_tensor(bnmv[:, 6:7], bnmv[:, 0:1], bnmv[:, 4:5], ALU.mult))
                        dve.tensor_tensor(bnmv[:, 5:6], col["be" + layer][:, :], bnmv[:, 6:7], ALU.subtract).then_inc(S("bn" + layer), 1)

                    seq.link(dve.tensor_scalar(col["eps"][:, :], col["eps"][:, :], 1.0, None, op0=ALU.add))

                    def own_and_sums(c, h):
                        dve.wait_ge(S("turned"), c * 2 + 2)
                        dve.scalar_tensor_tensor(ress[h], chunk(X, c), col["eps"][:, :], chunk(sums, c, slice(0, D)),
                                                 op0=ALU.mult, op1=ALU.add).then_inc(S("h"), 1)
                    in_turn(dve, own_and_sums)
                    batch_stats("1")
                    batch_stats("2")

                    def to_x(c, h):
                        dve.wait_ge(S("done"), (c + 1) * CB)
                        for b, (lo, hi) in enumerate(HALVES):
                            dve.wait_ge(S("back"), c * 2 + b + 5)
                            if b == 0:
                                pass_gate(dve, S)
                            seq.mark(dve.tensor_tensor(tmps[h][:, lo:hi, :], X[:, bass.ds(c * CB + lo, hi - lo), :],
                                                       bank[4 * h + b][:, 0:(hi - lo) * P].rearrange("p (k f) -> p k f", f=P), ALU.add))
                        seq.wait()
                        dve.sem_inc(S("back_used"), 1)
                        moments(dve, seq, S, h, CB)
                        scale_and_shift(dve, seq, S, c, h, CB, valid[:, bass.ds(c * CB, CB)])

                    in_turn_counted(dve, seq, 2 + 2 * CB - 1 + 2, to_x)

                @block.tensor
                def _(pe):
                    pe.sem_inc(S("turned"), 4)

                    def turn_input(c, h):
                        pe.wait_ge(S("h"), c + 1)
                        pass_gate(pe, S)
                        turn_chunk(pe, S, c, h, ress, None)
                    in_turn(pe, turn_input)

                    def product(layer, w):
                        def step(m, width, b):
                            if layer == "2":
                                pe.wait_ge(S("relu1"), m + 1)
                            pe.wait_ge(S("y" + layer), m + 1)
                            pe.matmul(bank[2 + b][:, 0:width], w[:, :], HT[0][:, bass.ds(m * FM, width)],
                                      start=True, stop=True).then_inc(S("p" + layer), 1)
                        products(pe, step)

                    pe.sem_inc(S("back"), 4)
                    pe.wait_ge(S("xT"), 2 + 2 * NCH)
                    product("1", W["w1T"])
                    product("2", W["w2T"])

                    def turn_back(c, h):
                        pe.wait_ge(S("relu2"), c + 1)
                        pe.wait_ge(S("back_used"), c + 1)
                        for b, (lo, hi) in enumerate(HALVES):
                            for j in range(lo, hi):
                                t = pe.transpose(bank[4 * h + b][:, (j - lo) * P:(j - lo + 1) * P], relu[h][:, j, :], ident[:, :])
                            t.then_inc(S("back"), 1)
                    in_turn(pe, turn_back)

                @block.scalar
                def _(act):
                    act.sem_inc(S("back_used"), 2)
                    act.sem_inc(S("done"), 2 * CB)
                    act.sem_inc(S("xT"), 2)
                    act.sem_inc(S("y1"), 2)
                    act.sem_inc(S("y2"), 2)

                    def take_input(c, h):
                        for b, (lo, hi) in enumerate(HALVES):
                            act.wait_ge(S("turned"), c * 2 + b + 5)
                            act.activation(HT[0][:, bass.ds((c * CB + lo) * P, (hi - lo) * P)], bank[b][:, 0:(hi - lo) * P],
                                           ACT.Copy).then_inc(S("xT"), 1)
                    in_turn(act, take_input)

                    def product(layer):
                        def step(m, width, b):
                            act.wait_ge(S("p" + layer), m + 1)
                            act.activation(HT[1][:, bass.ds(m * FM, width)], bank[2 + b][:, 0:width], ACT.Identity,
                                           bias=col["lb" + layer][:, :]).then_inc(S("y" + layer), 1)
                        products(act, step)
                        act.wait_ge(S("bnvar" + layer), 1)
                        act.activation(bnmv[:, 2:3], bnmv[:, 1:2], ACT.Sqrt, bias=eps_ln[:, :]).then_inc(S("bnroot" + layer), 1)
                        act.wait_ge(S("bn" + layer), 1)

                    product("1")

                    def relu1(m, width, b):
                        act.activation(HT[0][:, bass.ds(m * FM, width)], HT[1][:, bass.ds(m * FM, width)], ACT.Relu,
                                       bias=bnmv[:, 5:6], scale=bnmv[:, 4:5]).then_inc(S("relu1"), 1)
                    products(act, relu1)
                    act.wait_ge(S("relu1"), NFM + 1)
                    product("2")

                    def relu2(c, h):
                        width = CB * P if not isinstance(c, int) or c < NCH - 1 else N - (NCH - 1) * CB * P
                        act.wait_ge(S("back"), c * 2 + 2)
                        act.activation(relu[h].rearrange("p k f -> p (k f)")[:, 0:width], HT[1][:, bass.ds(c * CB * P, width)], ACT.Relu,
                                       bias=bnmv[:, 5:6], scale=bnmv[:, 4:5]).then_inc(S("relu2"), 1)

                    def normal(c, h):
                        root(act, S, c, h, CB)
                        apply(act, S, c, h, CB, lambda j: X[:, bass.ds(c * CB + j, 1), :], "done")

                    relu2(0, 0)
                    relu2(1, 1)
                    with act.Fori(0, (NCH - 3) // 2) as g:
                        for h in range(2):
                            normal(g * 2 + h, h)
                            relu2(g * 2 + h + 2, h)
                    normal(NCH - 3, 0)
                    relu2(NCH - 1, 0)
                    normal(NCH - 2, 1)
                    normal(NCH - 1, 0)

                @block.sync
                def _(sp):
                    whole = out[0:(NB - 1) * P].rearrange("(b p) c -> p b c", p=P)
                    with sp.Fori(0, NCH - 1) as c:
                        sp.wait_ge(S("done"), (c + 3) * CB)
                        sp.dma_start(whole[:, bass.ds(c * CB, CB), :], chunk(X, c)).then_inc(S("wrote"), 16)
                    sp.wait_ge(S("done"), (NCH + 2) * CB)
                    sp.dma_start(whole[:, NB - CB:NB - 1, :], X[:, NB - CB:NB - 1, :]).then_inc(S("wrote"), 16)
                    sp.dma_start(out[(NB - 1) * P:N], X[0:LAST, NB - 1, :]).then_inc(S("wrote"), 16)
                    sp.wait_ge(S("wrote"), 16 * (NCH + 1))

        prepare()
        project()
        edges0()
        nodes0()
        edges1()
        nodes1()
        clear_semaphores()
        edges2()
        nodes2()
        edges3()
        nodes3()


INPUTS = ['x', 'src', 'dst', 'L0_gnn_W', 'L0_gnn_att_src', 'L0_gnn_att_dst', 'L0_gnn_bias', 'L1_gnn_W1', 'L1_gnn_b1',
          'L1_gnn_W2', 'L1_gnn_b2', 'L1_gnn_W4', 'L1_gnn_b4', 'L2_gnn_Wq', 'L2_gnn_Wk', 'L2_gnn_Wv', 'L2_gnn_W_gcn',
          'L2_gnn_b_gcn', 'L2_gnn_W_lin', 'L2_gnn_b_lin', 'L3_gnn_eps', 'L3_gnn_W1', 'L3_gnn_b1', 'L3_gnn_g1',
          'L3_gnn_be1', 'L3_gnn_W2', 'L3_gnn_b2', 'L3_gnn_g2', 'L3_gnn_be2']


def kernel(**inputs):
    import concourse.bacc as bacc
    from concourse.bass_utils import run_bass_kernel_spmd

    nc = bacc.Bacc("TRN2", target_bir_lowering=False, num_devices=1)
    arrays, args = {}, {}
    for name in INPUTS:
        v = np.ascontiguousarray(inputs[name])
        v = v.reshape(v.shape or (1,))
        arrays["in_" + name] = v
        args[name] = nc.dram_tensor("in_" + name, v.shape, mybir.dt.from_np(v.dtype), kind="ExternalInput").ap()
    out = nc.dram_tensor("out_x", (N, D), F32, kind="ExternalOutput").ap()
    tables = [nc.dram_tensor(f"table{l}", (NB * P, w), F32).ap() for l, w in enumerate((D + H, 2 * D, D, D))]
    rel = nc.dram_tensor("rel", (TPAD * P,), BF16).ap()
    gnn(nc, args, out, tables, rel)
    return run_bass_kernel_spmd(nc, [arrays], core_ids=[0]).results[0]["out_x"]
```
